# Optimizing a Trainium2 kernel written in Bass

```python
import numpy as np
import jax
import jax.numpy as jnp

def _softmax(x, axis=-1):
    return jax.nn.softmax(x, axis=axis)

def _gelu(x):
    return jax.nn.gelu(x, approximate=True)

def _silu(x):
    return jax.nn.silu(x)

def _sigmoid(x):
    return jax.nn.sigmoid(x)

def _layernorm(x, axis=-1, eps=1e-05):
    m = jnp.mean(x, axis=axis, keepdims=True)
    v = jnp.var(x, axis=axis, keepdims=True)
    return (x - m) / jnp.sqrt(v + eps)

def _scatter_add(tgt, idx, src, axis=0):
    return tgt.at[idx].add(src)

def _segment_sum(src, seg, n):
    return jax.ops.segment_sum(src, seg, n)
kernel_name = 'mk_early_fusion_d2_tok_img256_r4_d71518'

def setup_inputs(seed: int=0):
    np.random.seed(seed)
    _w = jnp.asarray

    def _rec_inputs():
        import jax
        import jax.numpy as jnp
        _rk = jax.random.key(seed)
        x = -0.000222058 + 0.999998 * jax.random.normal(jax.random.fold_in(_rk, 1), (16, 3, 128, 128), jnp.float32)
        txt = 0.000118618 + 0.999142 * jax.random.normal(jax.random.fold_in(_rk, 2), (16, 128, 64), jnp.float32)
        return (x, txt)
    x, txt = _rec_inputs()

    def _L0_tok_setup():
        import jax, jax.numpy as jnp
        import numpy as np
        IMAGE_SIZE = 64
        PATCH = 16
        EMBED_DIM = 64
        IN_CH = 3
        BATCH = 128
        IN_DIM = IN_CH * PATCH * PATCH

        def _patchify(x, p):
            B, C, H, Wd = x.shape
            x = x.reshape(B, C, H // p, p, Wd // p, p)
            x = x.transpose(0, 2, 4, 1, 3, 5)
            return x.reshape(B, H // p * (Wd // p), C * p * p)
        key = jax.random.key(seed)
        kx, kw, kb = jax.random.split(key, 3)
        x = jax.random.normal(kx, (BATCH, IN_CH, IMAGE_SIZE, IMAGE_SIZE), dtype=jnp.float32)
        W = jax.random.normal(kw, (EMBED_DIM, IN_DIM), dtype=jnp.float32) * (1.0 / np.sqrt(IN_DIM))
        b = jax.random.normal(kb, (EMBED_DIM,), dtype=jnp.float32) * 0.01
        return {'x': x, 'W': W, 'b': b}
    _L0_tok_all = _L0_tok_setup()
    _L0_tok_in = {k: v for k, v in _L0_tok_all.items() if k in ('W', 'b')}
    del _L0_tok_all

    def _L0_attn_setup():
        import jax, jax.numpy as jnp
        import numpy as np
        B, S, C = (8, 256, 64)
        H, KD = (8, 64)
        HEAD_DIM = KD // H
        key = jax.random.key(seed)
        ks = jax.random.split(key, 5)
        sc = 0.02
        return {'x': jax.random.normal(ks[0], (B, S, C), dtype=jnp.float32), 'Wq': jax.random.normal(ks[1], (H * KD, C), dtype=jnp.float32) * sc, 'Wk': jax.random.normal(ks[2], (KD, C), dtype=jnp.float32) * sc, 'Wv': jax.random.normal(ks[3], (KD, C), dtype=jnp.float32) * sc, 'Wo': jax.random.normal(ks[4], (C, H * KD), dtype=jnp.float32) * sc}
    _L0_attn_all = _L0_attn_setup()
    _L0_attn_in = {k: v for k, v in _L0_attn_all.items() if k in ('Wq', 'Wk', 'Wv', 'Wo')}
    del _L0_attn_all

    def _L0_ffn_setup():
        import jax, jax.numpy as jnp
        import numpy as np
        B, S, D, E, H, K = (4, 1024, 64, 8, 128, 2)
        key = jax.random.key(seed)
        ks = jax.random.split(key, 6)
        x = jax.random.normal(ks[0], (B, S, D), jnp.float32)
        Wg = jax.random.normal(ks[1], (D, E), jnp.float32) * 0.02
        bg = jnp.zeros((E,), jnp.float32)
        W1 = jax.random.normal(ks[2], (E, D, H), jnp.float32) * 0.02
        b1 = jnp.zeros((E, H), jnp.float32)
        W2 = jax.random.normal(ks[3], (E, H, D), jnp.float32) * 0.02
        b2 = jnp.zeros((E, D), jnp.float32)
        return {'x': x, 'Wg': Wg, 'bg': bg, 'W1': W1, 'b1': b1, 'W2': W2, 'b2': b2}
    _L0_ffn_all = _L0_ffn_setup()
    _L0_ffn_in = {k: v for k, v in _L0_ffn_all.items() if k in ('Wg', 'bg', 'W1', 'b1', 'W2', 'b2')}
    del _L0_ffn_all

    def _L1_attn_setup():
        import jax, jax.numpy as jnp
        import numpy as np
        S, B, D, H, DH = (128, 32, 64, 8, 32)
        LN_EPS = 1e-05

        def elu_p1(x):
            return jax.nn.elu(x) + 1.0

        def sum_norm(x):
            return x / jnp.sum(x, axis=-1, keepdims=True)

        def layer_norm(x, g, b):
            mu = jnp.mean(x, axis=-1, keepdims=True)
            var = jnp.mean(jnp.square(x - mu), axis=-1, keepdims=True)
            return (x - mu) * jax.lax.rsqrt(var + LN_EPS) * g + b

        def _fast_rnn_forward(x, slow_W, out_W, ln_g, ln_b):
            slen, bsz, _ = x.shape
            o = layer_norm(x, ln_g, ln_b)
            qkv = jnp.einsum('sbd,ed->sbe', o, slow_W)
            qkv = qkv.reshape(slen, bsz, H, 5 * DH + 2)
            q, k, v, rk, rv, beta, rbeta = jnp.split(qkv, [DH, 2 * DH, 3 * DH, 4 * DH, 5 * DH, 5 * DH + 1], axis=-1)
            beta = jax.nn.sigmoid(beta)
            rbeta = jax.nn.sigmoid(rbeta)
            q = sum_norm(elu_p1(q))
            k = sum_norm(elu_p1(k))
            rk = jax.nn.softmax(rk, axis=-1)

            def ff_step(W, inp):
                qt, kt, vt, bt = inp
                v_old = jnp.einsum('bhij,bhj->bhi', W, kt)
                W = W + (bt * (vt - v_old))[..., :, None] * kt[..., None, :]
                z = jnp.einsum('bhij,bhj->bhi', W, qt)
                return (W, z)
            W0 = jnp.zeros((bsz, H, DH, DH), x.dtype)
            _, z = jax.lax.scan(ff_step, W0, (q, k, v, beta))

            def rec_step(carry, inp):
                R, h = carry
                zt, kt, vt, bt = inp
                q_rec = jax.nn.softmax(h, axis=-1)
                v_old = jnp.einsum('bhij,bhj->bhi', R, kt)
                R = R + (bt * (vt - v_old))[..., :, None] * kt[..., None, :]
                h = zt + jnp.einsum('bhij,bhj->bhi', R, q_rec)
                return ((R, h), h)
            R0 = jnp.zeros((bsz, H, DH, DH), x.dtype)
            h0 = jnp.zeros((bsz, H, DH), x.dtype)
            _, hs = jax.lax.scan(rec_step, (R0, h0), (z, rk, rv, rbeta))
            out = hs.reshape(slen, bsz, H * DH)
            out = jnp.einsum('sbe,de->sbd', out, out_W)
            return x + out
        key = jax.random.key(seed)
        k1, k2, k3 = jax.random.split(key, 3)
        x = jax.random.normal(k1, (S, B, D), jnp.float32)
        slow_W = jax.random.normal(k2, (H * (5 * DH + 2), D), jnp.float32) * 0.02
        out_W = jax.random.normal(k3, (D, H * DH), jnp.float32) * 0.02
        ln_g = jnp.ones((D,), jnp.float32)
        ln_b = jnp.zeros((D,), jnp.float32)
        return {'x': x, 'slow_W': slow_W, 'out_W': out_W, 'ln_g': ln_g, 'ln_b': ln_b}
    _L1_attn_all = _L1_attn_setup()
    _L1_attn_in = {k: v for k, v in _L1_attn_all.items() if k in ('slow_W', 'out_W', 'ln_g', 'ln_b')}
    del _L1_attn_all

    def _L1_ffn_setup():
        import jax, jax.numpy as jnp
        import numpy as np
        B, S, D = (8, 1024, 64)
        H = 4 * D
        CAPACITY = 0.5
        key = jax.random.key(seed)
        ks = jax.random.split(key, 6)
        x = jax.random.normal(ks[0], (B, S, D), dtype=jnp.float32)
        attention_mask = jnp.zeros((B, 1, 1, S), dtype=jnp.float32)
        wr = jax.random.normal(ks[1], (D, 1), dtype=jnp.float32) * 0.02
        br = jnp.zeros((1,), dtype=jnp.float32)
        w1 = jax.random.normal(ks[2], (D, H), dtype=jnp.float32) * 0.02
        b1 = jnp.zeros((H,), dtype=jnp.float32)
        w2 = jax.random.normal(ks[3], (H, D), dtype=jnp.float32) * 0.02
        b2 = jnp.zeros((D,), dtype=jnp.float32)
        return {'x': x, 'attention_mask': attention_mask, 'wr': wr, 'br': br, 'w1': w1, 'b1': b1, 'w2': w2, 'b2': b2}
    _L1_ffn_all = _L1_ffn_setup()
    _L1_ffn_in = {k: v for k, v in _L1_ffn_all.items() if k in ('attention_mask', 'wr', 'br', 'w1', 'b1', 'w2', 'b2')}
    del _L1_ffn_all
    return {'x': x, 'txt': txt, 'L0_tok_W': _L0_tok_in['W'], 'L0_tok_b': _L0_tok_in['b'], 'L0_attn_Wq': _L0_attn_in['Wq'], 'L0_attn_Wk': _L0_attn_in['Wk'], 'L0_attn_Wv': _L0_attn_in['Wv'], 'L0_attn_Wo': _L0_attn_in['Wo'], 'L0_ffn_Wg': _L0_ffn_in['Wg'], 'L0_ffn_bg': _L0_ffn_in['bg'], 'L0_ffn_W1': _L0_ffn_in['W1'], 'L0_ffn_b1': _L0_ffn_in['b1'], 'L0_ffn_W2': _L0_ffn_in['W2'], 'L0_ffn_b2': _L0_ffn_in['b2'], 'L1_attn_slow_W': _L1_attn_in['slow_W'], 'L1_attn_out_W': _L1_attn_in['out_W'], 'L1_attn_ln_g': _L1_attn_in['ln_g'], 'L1_attn_ln_b': _L1_attn_in['ln_b'], 'L1_ffn_attention_mask': _L1_ffn_in['attention_mask'], 'L1_ffn_wr': _L1_ffn_in['wr'], 'L1_ffn_br': _L1_ffn_in['br'], 'L1_ffn_w1': _L1_ffn_in['w1'], 'L1_ffn_b1': _L1_ffn_in['b1'], 'L1_ffn_w2': _L1_ffn_in['w2'], 'L1_ffn_b2': _L1_ffn_in['b2']}

def reference(x, txt, L0_tok_W, L0_tok_b, L0_attn_Wq, L0_attn_Wk, L0_attn_Wv, L0_attn_Wo, L0_ffn_Wg, L0_ffn_bg, L0_ffn_W1, L0_ffn_b1, L0_ffn_W2, L0_ffn_b2, L1_attn_slow_W, L1_attn_out_W, L1_attn_ln_g, L1_attn_ln_b, L1_ffn_attention_mask, L1_ffn_wr, L1_ffn_br, L1_ffn_w1, L1_ffn_b1, L1_ffn_w2, L1_ffn_b2):
    import jax
    import jax.numpy as jnp

    def _L0_tok_ref(x, W, b):
        import jax, jax.numpy as jnp
        import numpy as np
        IMAGE_SIZE = 64
        PATCH = 16
        EMBED_DIM = 64
        IN_CH = 3
        BATCH = 128
        IN_DIM = IN_CH * PATCH * PATCH

        def _patchify(x, p):
            B, C, H, Wd = x.shape
            x = x.reshape(B, C, H // p, p, Wd // p, p)
            x = x.transpose(0, 2, 4, 1, 3, 5)
            return x.reshape(B, H // p * (Wd // p), C * p * p)
        patches = _patchify(x, PATCH)
        return jnp.einsum('bnk,ek->bne', patches, W) + b

    def _L0_attn_ref(x, Wq, Wk, Wv, Wo):
        import jax, jax.numpy as jnp
        import numpy as np
        B, S, C = (8, 256, 64)
        H, KD = (8, 64)
        HEAD_DIM = KD // H
        b, s, c = x.shape
        q = jnp.einsum('bsc,oc->bso', x, Wq).reshape(b, s, H, KD).transpose(0, 2, 1, 3)
        k = jnp.einsum('bsc,oc->bos', x, Wk)
        v_conv = jnp.einsum('bsc,oc->bos', x, Wv)
        v = v_conv.reshape(b, s, KD)
        scale = 1.0 / np.sqrt(HEAD_DIM).astype(np.float32)
        scores = jnp.einsum('bhsd,bdt->bhst', q, k) * scale
        attn = jax.nn.softmax(scores, axis=-1)
        ctx = jnp.einsum('bhst,btd->bhsd', attn, v)
        ctx = ctx.transpose(0, 2, 1, 3).reshape(b, H * KD, s)
        out = jnp.einsum('bcp,oc->bop', ctx, Wo)
        return out.transpose(0, 2, 1)

    def _L0_ffn_ref(x, Wg, bg, W1, b1, W2, b2):
        import jax, jax.numpy as jnp
        import numpy as np
        B, S, D, E, H, K = (4, 1024, 64, 8, 128, 2)
        Bv, Sv, Dv = x.shape
        gate_scores = x @ Wg + bg
        _, idx = jax.lax.top_k(gate_scores, K)
        mask = jax.nn.one_hot(idx, E, dtype=x.dtype).sum(axis=-2)
        xf = x.reshape(-1, Dv)
        mf = mask.reshape(-1, E)
        h = jax.nn.gelu(jnp.einsum('td,edh->teh', xf, W1) + b1[None], approximate=False)
        y = jnp.einsum('teh,ehd->ted', h, W2) + b2[None]
        out = jnp.einsum('ted,te->td', y, mf)
        return out.reshape(Bv, Sv, Dv)

    def _L1_attn_ref(x, slow_W, out_W, ln_g, ln_b):
        import jax, jax.numpy as jnp
        import numpy as np
        S, B, D, H, DH = (128, 32, 64, 8, 32)
        LN_EPS = 1e-05

        def elu_p1(x):
            return jax.nn.elu(x) + 1.0

        def sum_norm(x):
            return x / jnp.sum(x, axis=-1, keepdims=True)

        def layer_norm(x, g, b):
            mu = jnp.mean(x, axis=-1, keepdims=True)
            var = jnp.mean(jnp.square(x - mu), axis=-1, keepdims=True)
            return (x - mu) * jax.lax.rsqrt(var + LN_EPS) * g + b

        def _fast_rnn_forward(x, slow_W, out_W, ln_g, ln_b):
            slen, bsz, _ = x.shape
            o = layer_norm(x, ln_g, ln_b)
            qkv = jnp.einsum('sbd,ed->sbe', o, slow_W)
            qkv = qkv.reshape(slen, bsz, H, 5 * DH + 2)
            q, k, v, rk, rv, beta, rbeta = jnp.split(qkv, [DH, 2 * DH, 3 * DH, 4 * DH, 5 * DH, 5 * DH + 1], axis=-1)
            beta = jax.nn.sigmoid(beta)
            rbeta = jax.nn.sigmoid(rbeta)
            q = sum_norm(elu_p1(q))
            k = sum_norm(elu_p1(k))
            rk = jax.nn.softmax(rk, axis=-1)

            def ff_step(W, inp):
                qt, kt, vt, bt = inp
                v_old = jnp.einsum('bhij,bhj->bhi', W, kt)
                W = W + (bt * (vt - v_old))[..., :, None] * kt[..., None, :]
                z = jnp.einsum('bhij,bhj->bhi', W, qt)
                return (W, z)
            W0 = jnp.zeros((bsz, H, DH, DH), x.dtype)
            _, z = jax.lax.scan(ff_step, W0, (q, k, v, beta))

            def rec_step(carry, inp):
                R, h = carry
                zt, kt, vt, bt = inp
                q_rec = jax.nn.softmax(h, axis=-1)
                v_old = jnp.einsum('bhij,bhj->bhi', R, kt)
                R = R + (bt * (vt - v_old))[..., :, None] * kt[..., None, :]
                h = zt + jnp.einsum('bhij,bhj->bhi', R, q_rec)
                return ((R, h), h)
            R0 = jnp.zeros((bsz, H, DH, DH), x.dtype)
            h0 = jnp.zeros((bsz, H, DH), x.dtype)
            _, hs = jax.lax.scan(rec_step, (R0, h0), (z, rk, rv, rbeta))
            out = hs.reshape(slen, bsz, H * DH)
            out = jnp.einsum('sbe,de->sbd', out, out_W)
            return x + out
        return _fast_rnn_forward(x, slow_W, out_W, ln_g, ln_b)

    def _L1_ffn_ref(x, attention_mask, wr, br, w1, b1, w2, b2):
        import jax, jax.numpy as jnp
        import numpy as np
        B, S, D = (8, 1024, 64)
        H = 4 * D
        CAPACITY = 0.5
        b, s, d = x.shape
        weights = (jnp.einsum('bsd,do->bso', x, wr) + br)[..., 0]
        k = max(1, int(CAPACITY * s))
        kk = k - 1 if k > 1 else 1
        _, idx = jax.lax.top_k(weights, k)
        sel_idx = idx[:, :kk]
        sel = jnp.take_along_axis(x, sel_idx[:, :, None], axis=1)
        h = jax.nn.gelu(jnp.einsum('bkd,dh->bkh', sel, w1) + b1)
        y = jnp.einsum('bkh,hd->bkd', h, w2) + b2
        w_sel = jnp.take_along_axis(weights, sel_idx, axis=1)
        y = y * w_sel[..., None]
        batch_idx = jnp.arange(b)[:, None]
        processed = jnp.zeros_like(x).at[batch_idx, sel_idx].set(y)
        return processed + x
    h = _L0_tok_ref(x, L0_tok_W, L0_tok_b)
    h = jnp.concatenate([h, txt], axis=1)
    h = h + _L0_attn_ref(_layernorm(h, axis=-1), L0_attn_Wq, L0_attn_Wk, L0_attn_Wv, L0_attn_Wo)
    h = h + _L0_ffn_ref(_layernorm(h, axis=-1), L0_ffn_Wg, L0_ffn_bg, L0_ffn_W1, L0_ffn_b1, L0_ffn_W2, L0_ffn_b2)
    h = h + _L1_attn_ref(_layernorm(h, axis=-1), L1_attn_slow_W, L1_attn_out_W, L1_attn_ln_g, L1_attn_ln_b)
    h = h + _L1_ffn_ref(_layernorm(h, axis=-1), L1_ffn_attention_mask, L1_ffn_wr, L1_ffn_br, L1_ffn_w1, L1_ffn_b1, L1_ffn_w2, L1_ffn_b2)
    return h

_drawn_inputs = setup_inputs


def setup_inputs(seed=0):
    import zlib

    import numpy as np

    out = dict(_drawn_inputs(seed))
    spreads = {'L0_ffn_bg': (0.0, 0.1),
     'L0_ffn_b1': (0.0, 0.519),
     'L0_ffn_b2': (0.0, 0.1),
     'L1_attn_ln_g': (1.0, 0.6),
     'L1_attn_ln_b': (0.0, 0.8),
     'L1_ffn_b1': (0.0, 0.8),
     'L1_ffn_b2': (0.0, 0.8)}
    factors = {'L0_tok_b': 5.976,
     'L0_attn_Wq': 8.0,
     'L0_attn_Wk': 8.0,
     'L0_attn_Wv': 7.377,
     'L0_attn_Wo': 5.183,
     'L1_attn_slow_W': 8.0,
     'L1_attn_out_W': 8.0,
     'L1_ffn_wr': 8.0,
     'L1_ffn_w1': 8.0,
     'L1_ffn_w2': 8.0,
     'L0_ffn_W1': 3.292}
    for name, (base, spread) in spreads.items():
        noise = np.random.default_rng([zlib.crc32(name.encode()), seed]).standard_normal(out[name].shape)
        drawn = base * np.exp(spread * noise) if base else spread * noise
        out[name] = jnp.asarray(drawn.astype(out[name].dtype))
    for name, factor in factors.items():
        out[name] = (out[name] * factor).astype(out[name].dtype)
    return out
```

```python
import concourse.bass as bass
from concourse import mybir
from contextlib import ExitStack

F32 = mybir.dt.float32
ALU = mybir.AluOpType
ACT = mybir.ActivationFunctionType
AXL = mybir.AxisListType

IMAGES, CHANNELS, SIDE, PATCH = 16, 3, 128, 16
GRID = SIDE // PATCH
D = 64
SEQ = GRID * GRID + 128
P = 128
TILES = IMAGES * SEQ // P
HEADS = 8
PAIRS = HEADS // 2
EXPERTS, HIDDEN = 8, 128
DH = 32
UNITS = 12
BOTH = 2 * UNITS
ROW = BOTH * DH
FFN_HIDDEN = 256
KEPT = SEQ // 2 - 1
EPS = 1e-5


def token_mixer_kernel(nc, x, txt, tok_W, tok_b, Wq, Wk, Wv, Wo, Wg, bg, W1, b1, W2, b2, slow_W, out_W,
                       ln_g, ln_b, wr, br, w1, fb1, w2, fb2, out):
    ctx = ExitStack()
    with ctx:
        def sb(name, shape):
            return ctx.enter_context(nc.sbuf_tensor(name, shape, F32))

        def sem(name):
            return ctx.enter_context(nc.semaphore(name))

        ps = ctx.enter_context(nc.psum_tensor("ps", [P, 8, 512], F32))
        arena_a = sb("arena_a", [P, 12288])
        arena_b = sb("arena_b", [P, 12288])
        arena_c = sb("arena_c", [P, 12288])
        h = sb("h", [P, TILES, D])
        xn = sb("xn", [P, TILES, D])
        xT = sb("xT", [D, TILES * P])
        ident = sb("ident", [P, P])
        stat = sb("stat", [P, 2, TILES])
        Nh = sb("Nh", [D, HEADS, D])
        WoT = arena_c[:, 4608:5376].rearrange("p (n d) -> p n d", d=D)
        WvT = sb("WvT", [D, 2, D])
        slowT = sb("slowT", [D, HEADS, 162])
        WoutT = sb("WoutT", [P, 2, D])
        b1T = sb("b1T", [P, EXPERTS])
        fb1T = sb("fb1T", [P, 2])
        W1_sb = arena_c[0:D, 6656:7680].rearrange("p (e k) -> p e k", e=EXPERTS)
        W2_sb = arena_c[:, 7680:8192].rearrange("p (e d) -> p e d", e=EXPERTS)
        Wg_sb = sb("Wg_sb", [D, EXPERTS])
        bg_sb = sb("bg_sb", [P, EXPERTS])
        b2rep = sb("b2rep", [D, D])
        b2blk = arena_c[0:D, 8192:8704].rearrange("p (t d) -> p t d", d=D)
        tokb_sb = sb("tokb_sb", [P, D])
        g_sb = sb("g_sb", [P, D])
        b_sb = sb("b_sb", [P, D])
        wr_sb = sb("wr_sb", [D, 1])
        wrB = sb("wrB", [D, P])
        br_sb = sb("br_sb", [P, 1])
        w1_sb = sb("w1_sb", [D, FFN_HIDDEN])
        w2_sb = sb("w2_sb", [P, 2, D])
        fb2_sb = sb("fb2_sb", [P, D])
        par = sb("par", [P, 2])
        earlier = sb("earlier", [P, 3, SEQ])

        rows = arena_a[:, 0:6144].rearrange("p (n c w) -> p n c w", n=IMAGES, c=CHANNELS)
        Wblk = arena_a[:, 6144:12288].rearrange("p (n s e) -> p n s e", n=CHANNELS * PATCH, s=2)
        KK = arena_a[:, :].rearrange("p (t r) -> p t r", r=ROW)
        cen = arena_b[:, 0:1536].rearrange("p (t d) -> p t d", d=D)
        sq = arena_b[:, 1536:3072].rearrange("p (t d) -> p t d", d=D)
        UU = arena_b[:, :].rearrange("p (t r) -> p t r", r=ROW)
        o_tok = arena_b[:, 3072:4608].rearrange("p (t d) -> p t d", d=D)
        Qs = [arena_b[0:D, 3072 + 1536 * i:3072 + 1536 * (i + 1)].rearrange("p (n s) -> p n s", n=12) for i in range(2)]
        probs = [arena_b[:, 6144 + 2304 * i:6144 + 2304 * (i + 1)].rearrange("p (n t) -> p n t", n=12) for i in range(2)]
        tokW_rep = arena_b[0:D, 0:6144].rearrange("e (n k) -> e n k", k=P)

        def repeat_tokW(c):
            src = tokW_raw[:, 256 * c:256 * c + 256].rearrange("e (y x) -> e x y", x=PATCH)
            return (tokW_rep[:, PATCH * c:PATCH * c + PATCH, :].rearrange("e x (i y) -> e x i y", y=PATCH),
                    src.unsqueeze(2).to_broadcast([D, PATCH, GRID, PATCH]))

        raw = arena_c
        tokW_raw = raw[0:D, 0:768]
        Wq_raw = raw[0:D, 768:1280].rearrange("p (h c) -> p h c", h=HEADS)
        Wk_raw = raw[0:D, 1280:1344]
        Wv_raw = raw[0:D, 1344:1408]
        Wo_raw = raw[0:D, 1408:1920]
        slowA = raw[0:96, 1920:2432].rearrange("p (h c) -> p h c", h=HEADS)
        slowB = raw[0:66, 2432:2944].rearrange("p (h c) -> p h c", h=HEADS)
        outW_raw = raw[0:D, 2944:3200]
        b1_raw = raw[0:EXPERTS, 3200:3328]
        fb1_raw = raw[0:2, 3328:3456]
        hT = raw[0:D, 3456:4480]
        WoS = [arena_b[:, 10752 + 768 * i:11520 + 768 * i].rearrange("p (n d) -> p n d", d=D) for i in range(2)]
        negmax = [sb(f"negmax{i}", [P, 12]) for i in range(2)]
        rowsum = [sb(f"rowsum{i}", [P, 12]) for i in range(2)]
        rinv = sb("rinv", [P, 12])
        xb = [sb(f"xb{i}", [D, SEQ]) for i in range(2)]
        Glo = [arena_c[:, 5376 + 192 * i:5568 + 192 * i].rearrange("p (j d) -> p j d", j=3) for i in range(2)]
        Ghi = [arena_c[0:D, 5760 + 192 * i:5952 + 192 * i].rearrange("p (j d) -> p j d", j=3) for i in range(2)]
        Vlo = [arena_c[:, 6144 + 128 * i:6272 + 128 * i].rearrange("p (j d) -> p j d", j=2) for i in range(2)]
        Vhi = [arena_c[0:D, 6400 + 128 * i:6528 + 128 * i].rearrange("p (j d) -> p j d", j=2) for i in range(2)]
        gate = sb("gate", [P, TILES, EXPERTS])
        mask = sb("mask", [P, TILES, EXPERTS])
        maskT = arena_c[0:D, 8704:9088].rearrange("p (c n) -> p c n", c=3)
        beats = arena_b[:, 0:1536].rearrange("p (t a b) -> p t a b", a=EXPERTS, b=EXPERTS)
        hid = [arena_c[:, 512 * i:512 * (i + 1)] for i in range(4)]
        ysel = [arena_c[:, 2048 + 512 * i:2048 + 512 * (i + 1)].rearrange("p (e d) -> p e d", e=EXPERTS) for i in range(2)]
        ysum = arena_c[:, 3072:3136]
        prod = arena_c[:, :].rearrange("p (t r) -> p t r", r=ROW)
        gram = sb("gram", [P, IMAGES, BOTH])
        coef = sb("coef", [P, IMAGES, BOTH])
        QE = sb("QE", [P, UNITS, 2, DH])
        relu_qk = sb("relu_qk", [P, UNITS, 2 * DH])
        exp_qk = sb("exp_qk", [P, UNITS, 2 * DH])
        beta = [sb(f"beta{i}", [P, UNITS, 2]) for i in range(2)]
        top = sb("top", [P, UNITS])
        rk_top = sb("rk_top", [P, UNITS])
        ksum = sb("ksum", [P, BOTH])
        qsum = sb("qsum", [P, BOTH])
        hs = [sb(f"hs{i}", [P, UNITS, DH]) for i in range(2)]
        hsT = sb("hsT", [P, 2, SEQ])
        wcols = arena_a[:, 0:3072]
        wdiag = arena_a[:, 3072:6144].rearrange("p (t j) -> p t j", j=P)
        tie = arena_a[:, 6144:6336]
        over = arena_a[:, 6336:6528]
        fhid = [arena_c[:, 1024 * i:1024 * (i + 1)].rearrange("p (a n) -> p a n", a=2) for i in range(2)]
        fy = arena_c[:, 2048:2304].rearrange("p (s d) -> p s d", d=D)
        wtok = sb("wtok", [P, TILES])
        rank = sb("rank", [P, TILES])
        wkeep = sb("wkeep", [P, TILES])

        ld_attn, ld_slow, ld_tok, ld_image, ld_text, ld_rep, ld_moe, ld_ffn, ld_bias = (
            sem(n) for n in ("ld_attn", "ld_slow", "ld_tok", "ld_image", "ld_text", "ld_rep", "ld_moe", "ld_ffn", "ld_bias"))
        tokw_rep = [sem(f"tokw_rep{c}") for c in range(CHANNELS)]
        ident_set, masks_set, b2_set = sem("ident_set"), sem("masks_set"), sem("b2_set")
        par_set = sem("par_set")
        wt_ready, wt_evac = sem("wt_ready"), sem("wt_evac")
        tokw_ready, tokw_evac_a, tokw_evac_v = sem("tokw_ready"), sem("tokw_evac_a"), sem("tokw_evac_v")
        embed_ready, hT_a, hT_v, hback_ready = sem("embed_ready"), sem("hT_a"), sem("hT_v"), sem("hback_ready")
        vec = sem("vec")
        var_ready, std_ready = sem("var_ready"), sem("std_ready")
        norm_ready = sem("norm_ready")
        tr_ready, tr_evac_a, tr_evac_v = sem("tr_ready"), sem("tr_evac_a"), sem("tr_evac_v")
        qp_ready, qp_evac, score_ready, max_ready, exp_done, wos_ready, g_ready, g_evac, mix_ready, mix_used = (
            sem(n) for n in ("qp_ready", "qp_evac", "score_ready", "max_ready", "exp_done", "wos_ready", "g_ready",
                             "g_evac", "mix_ready", "mix_used"))
        rinv_set, xb_ready = sem("rinv_set"), sem("xb_ready")
        gate_ready, mask_ready, maskT_ready, maskT_evac, bias_ready, bias_used = (
            sem(n) for n in ("gate_ready", "mask_ready", "maskT_ready", "maskT_evac", "bias_ready", "bias_used"))
        up_ready, gelu_done, down_done, y_used, y_vec = (
            sem(n) for n in ("up_ready", "gelu_done", "down_done", "y_used", "y_vec"))
        proj_ready, raw_ready, rk_in, rk_exp, pre_used, hs_ready, soft_in, soft_exp, hsT_ready, hsT_evac, mixo_ready, mixo_used = (
            sem(n) for n in ("proj_ready", "raw_ready", "rk_in", "rk_exp", "pre_used", "hs_ready", "soft_in",
                             "soft_exp", "hsT_ready", "hsT_evac", "mixo_ready", "mixo_used"))
        wcol_ready, wrB_set, rank_vec, fup_ready, fgelu_done, fdown_ready, fy_vec, out_ready, stored = (
            sem(n) for n in ("wcol_ready", "wrB_set", "rank_vec", "fup_ready", "fgelu_done", "fdown_ready", "fy_vec",
                             "out_ready", "stored"))

        def wait(eng, s, value):
            if not (isinstance(value, int) and value <= 0):
                eng.wait_ge(s, value)

        class Steps:
            def __init__(self, eng, s):
                self.eng, self.s, self.base, self.n = eng, s, 0, 0

            def then(self, ins):
                ins.then_inc(self.s, 1)
                self.n += 1
                self.eng.wait_ge(self.s, self.base + self.n)

        def chunk(n):
            return (2 * (n // 3) - n % 3) % 3

        def columns(n, half):
            hd, r = 2 * (n // 3) + half, (n % 3 + half) % 3
            return (8 * r + hd - chunk(n)) // 3

        units = ps[:, 0:6, 0:324].rearrange("p b (s f) -> p b s f", s=2)

        def bs(a):
            return a.rearrange("p (b s) f -> p b s f", s=2)

        TOKW_BANKS = [6, 7, 0, 1, 2, 3]
        N_EVAC1 = 10

        block = ctx.enter_context(nc.Block())

        @block.sync
        def _(sp):
            sp.dma_start(Wq_raw, Wq.rearrange("(h k) c -> k h c", k=D)).then_inc(ld_attn, 16)
            sp.dma_start(Wk_raw, Wk).then_inc(ld_attn, 16)
            sp.dma_start(Wv_raw, Wv).then_inc(ld_attn, 16)
            sp.dma_start(Wo_raw, Wo).then_inc(ld_attn, 16)
            sp.dma_start(tokW_raw, tok_W).then_inc(ld_tok, 16)
            for c in range(4):
                sp.dma_start(rows[:, 4 * c:4 * c + 4, :, :], x[4 * c:4 * c + 4, :, :, :].rearrange("n c r w -> r n c w"))\
                  .then_inc(ld_image, 16)
            sp.dma_start(W1_sb[:, :, :], W1.rearrange("e d k -> d e k")).then_inc(ld_moe, 16)
            sp.dma_start(W2_sb[:, :, :], W2.rearrange("e k d -> k e d")).then_inc(ld_moe, 16)
            sp.dma_start(Wg_sb[:, :], Wg).then_inc(ld_moe, 16)
            sp.dma_start(wr_sb[:, :], wr).then_inc(ld_ffn, 16)
            sp.dma_start(w1_sb[:, :], w1).then_inc(ld_ffn, 16)
            sp.dma_start(w2_sb[:, :, :], w2.rearrange("(a k) d -> k a d", a=2)).then_inc(ld_ffn, 16)
            out_t = out.rearrange("b s d -> (b s) d").rearrange("(t p) d -> p t d", p=P)
            with sp.Fori(0, 6) as ch:
                sp.wait_ge(out_ready, ch + 1)
                sp.dma_start(out_t[:, bass.ds(ch * 4, 4), :], h[:, bass.ds(ch * 4, 4), :]).then_inc(stored, 16)
            sp.wait_ge(stored, 6 * 16)

        @block.gpsimd
        def _(pool):
            pool.memset(ident[:, :], 0.0).then_inc(ident_set, 1)
            pool.wait_ge(ident_set, 1)
            pool.affine_select(out=ident[:, :], in_=ident[:, :], compare_op=ALU.not_equal, fill=1.0, base=0,
                               pattern=[[-1, P]], channel_multiplier=1).then_inc(ident_set, 1)
            pool.wait_ge(ld_tok, 16)
            o, i = repeat_tokW(2)
            pool.tensor_copy(o, i).then_inc(tokw_rep[2], 1)
            masks = Steps(pool, masks_set)
            masks.then(pool.memset(earlier[:, :, :], 1.0))
            for rows_, k, base in ((slice(0, P), 0, 0), (slice(0, D), 1, P), (slice(D, P), 1, 0), (slice(0, P), 2, D)):
                m = earlier[rows_, k, :]
                masks.then(pool.affine_select(out=m, in_=m, compare_op=ALU.is_gt, fill=0.0, base=base,
                                              pattern=[[-1, SEQ]], channel_multiplier=1))
            for c in range(8):
                pool.dma_start(b2rep[8 * c:8 * c + 8, :], b2).then_inc(ld_rep, 16)
            for dst, src in ((bg_sb, bg), (tokb_sb, tok_b), (g_sb, ln_g), (b_sb, ln_b), (br_sb, br), (fb2_sb, fb2)):
                pool.dma_start(dst[:, :], src.partition_broadcast(P)).then_inc(ld_bias, 16)
            pool.wait_ge(ld_rep, 8 * 16)
            pool.tensor_copy(b2blk[:, :, :], b2rep[:, :].unsqueeze(1).to_broadcast([D, 8, D])).then_inc(b2_set, 1)
            pool.wait_ge(b2_set, 1)
            pool.affine_select(out=b2blk[:, :, :], in_=b2blk[:, :, :], compare_op=ALU.is_ge, fill=0.0, base=0,
                               pattern=[[-8, 8], [0, D]], channel_multiplier=1).then_inc(b2_set, 1)
            pool.wait_ge(b2_set, 2)
            pool.affine_select(out=b2blk[:, :, :], in_=b2blk[:, :, :], compare_op=ALU.is_ge, fill=0.0, base=7,
                               pattern=[[8, 8], [0, D]], channel_multiplier=-1).then_inc(b2_set, 1)

            pool.wait_ge(tr_evac_v, 3)
            pool.wait_ge(tr_evac_a, 3)
            for e in range(2):
                pool.tensor_copy(xb[e][:, :], xT[:, SEQ * e:SEQ * e + SEQ]).then_inc(xb_ready, 1)
            with pool.Fori(1, IMAGES // 2) as q:
                for e in range(2):
                    pool.wait_ge(g_ready, q * 2 + (e - 1))
                    pool.wait_ge(tr_evac_a, 3)
                    pool.tensor_copy(xb[e][:, :], xT[:, bass.ds((q * 2 + e) * SEQ, SEQ)]).then_inc(xb_ready, 1)

        @block.scalar
        def _(act):
            act.dma_start(slowA[0:64, :, :], slow_W.rearrange("(h f) c -> f h c", h=HEADS)[0:64, :, :]).then_inc(ld_slow, 16)
            act.dma_start(slowA[64:96, :, :], slow_W.rearrange("(h f) c -> f h c", h=HEADS)[96:128, :, :]).then_inc(ld_slow, 16)
            act.dma_start(slowB[0:32, :, :], slow_W.rearrange("(h f) c -> f h c", h=HEADS)[64:96, :, :]).then_inc(ld_slow, 16)
            act.dma_start(slowB[32:66, :, :], slow_W.rearrange("(h f) c -> f h c", h=HEADS)[128:162, :, :]).then_inc(ld_slow, 16)
            act.dma_start(outW_raw, out_W).then_inc(ld_slow, 16)
            act.dma_start(b1_raw, b1).then_inc(ld_slow, 16)
            act.dma_start(fb1_raw, fb1.rearrange("(a k) -> a k", a=2)).then_inc(ld_slow, 16)
            hv = h[:, :, :].rearrange("p (q r) d -> p q r d", r=3)
            tv = txt.rearrange("(q two) s d -> two s q d", two=2)
            act.dma_start(hv[D:P, :, 0, :], tv[0, 0:D, :, :]).then_inc(ld_text, 16)
            act.dma_start(hv[0:D, :, 1, :], tv[0, D:P, :, :]).then_inc(ld_text, 16)
            act.dma_start(hv[:, :, 2, :], tv[1, :, :, :]).then_inc(ld_text, 16)

            act.wait_ge(ld_tok, 16)
            o, i = repeat_tokW(1)
            act.activation(o, i, ACT.Copy).then_inc(tokw_rep[1], 1)
            act.wait_ge(wt_ready, 1)
            act.activation(Nh[:, :, :], ps[0:D, 0, :], ACT.Copy, scale=float(D // HEADS) ** -0.5).then_inc(wt_evac, 1)
            act.wait_ge(wt_ready, 2)
            act.activation(WoT[:, 0:8, :], ps[:, 1, :], ACT.Copy).then_inc(wt_evac, 1)
            act.wait_ge(wt_ready, 3)
            act.activation(WoT[:, 8:12, :], ps[:, 2, 0:256], ACT.Copy).then_inc(wt_evac, 1)
            act.activation(WvT[:, :, :], ps[0:D, 2, 256:320].unsqueeze(1).to_broadcast([D, 2, D]), ACT.Copy).then_inc(wt_evac, 1)
            act.activation(WoutT[:, :, :], ps[:, 2, 320:448], ACT.Copy).then_inc(wt_evac, 1)
            act.activation(b1T[:, :], ps[:, 2, 448:456], ACT.Copy).then_inc(wt_evac, 1)
            act.activation(fb1T[:, :], ps[:, 2, 456:458], ACT.Copy).then_inc(wt_evac, 1)
            for c in range(3):
                n = min(3, HEADS - 3 * c)
                act.activation(slowT[:, 3 * c:3 * c + n, :], ps[0:D, 3 + c, 0:162 * n], ACT.Copy).then_inc(wt_evac, 1)
            act.wait_ge(par_set, 2)
            for g in range(0, 6, 2):
                act.wait_ge(tokw_ready, g + 1)
                for k in range(2):
                    act.activation(Wblk[:, 8 * g:8 * g + 8, k, :], ps[:, TOKW_BANKS[g], :].rearrange("p (n e) -> p n e", e=D),
                                   ACT.Copy, scale=par[:, k:k + 1]).then_inc(tokw_evac_a, 1)
            act.wait_ge(embed_ready, 1)
            hTv = hT.rearrange("e (b i s j) -> e s i b j", i=4, s=2, j=8)
            act.activation(hTv[:, 0, :, :, :], ps[0:D, 4:8, 0:P].rearrange("e i (b j) -> e i b j", j=8), ACT.Copy)\
               .then_inc(hT_a, 1)

            def std(k):
                act.wait_ge(var_ready, k + 1)
                act.activation(stat[:, 1, :], stat[:, 1, :], ACT.Sqrt).then_inc(std_ready, 1)

            def evacuate_xT(k):
                for c in range(0, 6, 2):
                    act.wait_ge(tr_ready, 6 * k + c + 1)
                    act.activation(xT[:, 512 * c:512 * c + 512], ps[0:D, c, :], ACT.Copy).then_inc(tr_evac_a, 1)

            std(0)
            evacuate_xT(0)

            def exps(b, e):
                wait(act, g_ready, b - 1)
                wait(act, wos_ready, b - 1)
                for m in range(6):
                    act.wait_ge(max_ready, b * 6 + m + 1)
                    for s in range(2):
                        n = 2 * m + s
                        act.activation(probs[e][:, n, :], ps[:, 2 + m % 3, SEQ * s:SEQ * s + SEQ], ACT.Exp,
                                       bias=negmax[e][:, n:n + 1], accum_out=rowsum[e][:, n:n + 1]).then_inc(exp_done, 1)

            def evacuate_g(b, e):
                act.wait_ge(g_ready, b + 1)
                wait(act, mix_ready, b - 1)
                act.activation(Glo[e][:, :, :], ps[:, 6, 0:SEQ], ACT.Copy).then_inc(g_evac, 1)
                act.activation(Ghi[e][:, :, :], ps[0:D, 6, SEQ:2 * SEQ], ACT.Copy).then_inc(g_evac, 1)
                for dst, p0, c in ((Vlo[e][0:D, :, :], 0, 0), (Vlo[e][D:P, :, :], D, 1), (Vhi[e][:, :, :], 0, 2)):
                    act.activation(dst, ps[p0:p0 + D, 5, D * c:D * c + D].unsqueeze(1).to_broadcast([D, 2, D]), ACT.Copy)\
                       .then_inc(g_evac, 1)

            exps(0, 0)
            exps(1, 1)
            evacuate_g(0, 0)
            with act.Fori(1, IMAGES // 2) as q:
                for e in range(2):
                    exps(q * 2 + e, e)
                    evacuate_g(q * 2 + (e - 1), 1 - e)
            evacuate_g(IMAGES - 1, 1)

            std(1)
            evacuate_xT(1)
            act.wait_ge(maskT_ready, 3)
            for c in range(3):
                act.activation(maskT[:, c, :], ps[0:D, 1, P * c:P * c + P], ACT.Copy).then_inc(maskT_evac, 1)
            with act.Fori(0, 6) as ch:
                for e in range(EXPERTS):
                    act.wait_ge(up_ready, ch * 8 + e + 1)
                    if e >= 4:
                        act.wait_ge(down_done, ch * 8 + (e - 3))
                    else:
                        act.wait_ge(down_done, ch * 8)
                    act.activation(hid[e % 4], ps[:, e % 2, :], ACT.Gelu, bias=b1T[:, e:e + 1]).then_inc(gelu_done, 1)

            std(2)
            std(3)
            evacuate_xT(2)

            def pre(t):
                act.wait_ge(proj_ready, t + 1)
                kt = KK[:, t, :].rearrange("p (u c d) -> p u c d", c=2, d=DH)
                ut = UU[:, t, :].rearrange("p (u f) -> p u f", f=2 * DH)
                act.activation(bs(kt[:, :, 1, :]), units[:, :, :, 64:96], ACT.Copy).then_inc(raw_ready, 1)
                act.activation(bs(ut), units[:, :, :, 96:160], ACT.Copy).then_inc(raw_ready, 1)
                wait(act, pre_used, t)
                act.activation(bs(relu_qk[:, :, :]), units[:, :, :, 0:64], ACT.Relu).then_inc(raw_ready, 1)
                act.activation(bs(exp_qk[:, :, :]), units[:, :, :, 0:64], ACT.Exp).then_inc(raw_ready, 1)
                act.activation(bs(beta[t % 2][:, :, :]), units[:, :, :, 160:162], ACT.Exp, scale=-1.0).then_inc(raw_ready, 1)

            def rk_softmax(t):
                act.wait_ge(rk_in, t + 1)
                kt = KK[:, t, :].rearrange("p (u c d) -> p u c d", c=2, d=DH)[:, :, 1, :]
                act.activation(kt, kt, ACT.Exp).then_inc(rk_exp, 1)

            pre(0)
            rk_softmax(0)
            for t in range(IMAGES):
                if t + 1 < IMAGES:
                    pre(t + 1)
                    act.wait_ge(soft_in, t + 1)
                    act.activation(QE[:, :, 1, :], QE[:, :, 1, :], ACT.Exp).then_inc(soft_exp, 1)
                    rk_softmax(t + 1)
                act.wait_ge(hsT_ready, t + 1)
                wait(act, mixo_ready, t)
                act.activation(hsT[:, :, 0:P], ps[:, 6, 0:2 * P].rearrange("p (c n) -> p c n", c=2), ACT.Copy)\
                   .then_inc(hsT_evac, 1)
                act.activation(hsT[:, :, P:SEQ], ps[:, 6, 2 * P:3 * P].rearrange("p (c n) -> p c n", c=2), ACT.Copy)\
                   .then_inc(hsT_evac, 1)

            std(4)
            evacuate_xT(3)
            with act.Fori(0, 3) as c2:
                for e in range(2):
                    ch = c2 * 2 + e
                    for a in range(2):
                        act.wait_ge(fup_ready, ch * 2 + a + 1)
                        act.wait_ge(fdown_ready, c2 * 2)
                        act.activation(fhid[e][:, a, :], ps[:, 2 * e + a, :], ACT.Gelu_apprx_tanh, bias=fb1T[:, a:a + 1])\
                           .then_inc(fgelu_done, 1)

        @block.tensor
        def _(pe):
            def mm(o, lhsT, rhs, start=True, stop=True):
                return pe.matmul(o, lhsT, rhs, start=start, stop=stop)

            def tr(o, in_):
                k = in_.shape[0]
                return pe.transpose(o, in_, ident[0:k, 0:k])

            pe.wait_ge(ident_set, 2)
            pe.wait_ge(ld_attn, 4 * 16)
            for hd in range(HEADS):
                last = mm(ps[0:D, 0, D * hd:D * hd + D], Wq_raw[:, hd, :], Wk_raw)
            last.then_inc(wt_ready, 1)
            for n in range(12):
                for half in range(2):
                    k = columns(n, half)
                    mm(ps[D * half:D * half + D, 1 + n // 8, D * (n % 8):D * (n % 8) + D], Wo_raw[:, k:k + 505:8], ident[0:D, 0:D])
            tr(ps[0:D, 2, 256:320], Wv_raw).then_inc(wt_ready, 1)
            pe.wait_ge(ld_slow, 7 * 16)
            for c in range(2):
                tr(ps[:, 2, 320 + D * c:384 + D * c], outW_raw[:, P * c:P * c + P])
            tr(ps[:, 2, 448:456], b1_raw)
            tr(ps[:, 2, 456:458], fb1_raw)
            for hd in range(HEADS):
                c0 = 162 * (hd % 3)
                tr(ps[0:D, 3 + hd // 3, c0:c0 + 96], slowA[:, hd, :])
                last = tr(ps[0:D, 3 + hd // 3, c0 + 96:c0 + 162], slowB[:, hd, :])
            last.then_inc(wt_ready, 1)
            for n in range(48):
                c, px = n // PATCH, n % PATCH
                g = n // 8
                if g == 2 and n % 8 == 0:
                    pe.wait_ge(wt_evac, N_EVAC1)
                if px == 0:
                    pe.wait_ge(tokw_rep[c], 1)
                last = tr(ps[:, TOKW_BANKS[g], D * (n % 8):D * (n % 8) + D], tokW_rep[:, n, :])
                if n % 8 == 7:
                    last.then_inc(tokw_ready, 1)
            pe.wait_ge(wt_evac, N_EVAC1)
            pe.wait_ge(tokw_evac_a, 6)
            pe.wait_ge(tokw_evac_v, 6)
            pe.wait_ge(ld_image, 4 * 16)
            pix = rows.rearrange("p n c (j x) -> p n c j x", x=PATCH)
            for n in range(48):
                c, px = n // PATCH, n % PATCH
                for i in range(4):
                    s = slice(32 * i, 32 * i + 32)
                    last = mm(ps[:, 4 + i, 0:P], Wblk[s, n, :, :], pix[s, :, c, :, px], start=(n == 0), stop=(n == 47))
            last.then_inc(embed_ready, 1)
            pe.wait_ge(hT_a, 1)
            pe.wait_ge(hT_v, 1)
            for q in range(8):
                last = tr(ps[:, 0, D * q:D * q + D], hT[:, P * q:P * q + P])
            last.then_inc(hback_ready, 1)

            def transpose_x(k, src):
                pe.wait_ge(norm_ready, k + 1)
                for t in range(TILES):
                    last = tr(ps[0:D, t // 4, P * (t % 4):P * (t % 4) + P], src[:, t, :])
                    if t % 4 == 3:
                        last.then_inc(tr_ready, 1)
                pe.wait_ge(tr_evac_a, 3 * k + 3)
                pe.wait_ge(tr_evac_v, 3 * k + 3)

            transpose_x(0, xn)

            def scores(b, e):
                pe.wait_ge(xb_ready, b + 1)
                groups = xb[e][:, :].rearrange("c (u r) -> c r u", r=3)
                for k in range(2):
                    wait(pe, qp_evac, b * 6 + (3 * k - 3))
                    for i in range(2):
                        last = mm(ps[:, k, SEQ * i:SEQ * i + SEQ], Nh[:, 4 * k + 2 * i:4 * k + 2 * i + 2, :], groups)
                    last.then_inc(qp_ready, 1)
                keys = xb[e][:, :].rearrange("c (o j) -> c j o", j=3)
                for m in range(6):
                    pe.wait_ge(qp_evac, b * 6 + (3 if m < 3 else 6))
                    wait(pe, exp_done, b * 12 + (2 * m - 4))
                    for s in range(2):
                        last = mm(ps[:, 2 + m % 3, SEQ * s:SEQ * s + SEQ], Qs[e][:, 2 * m + s, :], keys)
                    last.then_inc(score_ready, 1)

            def mix(b, e):
                pe.wait_ge(g_evac, b * 5 + 5)
                wait(pe, mix_used, b * 2)
                mm(ps[:, 7, 0:SEQ], Vlo[e][:, :, :], Glo[e][:, :, :], stop=False)
                mm(ps[:, 7, 0:SEQ], Vhi[e][:, :, :], Ghi[e][:, :, :], start=False).then_inc(mix_ready, 1)

            def weigh(b, e):
                wait(pe, g_evac, b * 5)
                mm(ps[:, 5, 0:SEQ], WvT[:, :, :], xb[e][:, :])
                pe.wait_ge(wos_ready, b + 1)
                for j in range(3):
                    for m_, c0, c1 in ((P, 0, P), (D, P, SEQ)):
                        for i in range(PAIRS):
                            o = ps[0:m_, 6, (SEQ if c0 else 0) + D * j:(SEQ if c0 else 0) + D * j + D]
                            n = 3 * i + (2 * i - j) % 3
                            last = mm(o, probs[e][:, n, c0:c1], WoS[e][:, n, :], start=(i == 0),
                                      stop=(i == PAIRS - 1))
                last.then_inc(g_ready, 1)

            scores(0, 0)
            scores(1, 1)
            weigh(0, 0)
            with pe.Fori(1, IMAGES // 2) as q:
                for e in range(2):
                    scores(q * 2 + e, e)
                    mix(q * 2 + (e - 2), e)
                    weigh(q * 2 + (e - 1), 1 - e)
            mix(IMAGES - 2, 0)
            weigh(IMAGES - 1, 1)
            mix(IMAGES - 1, 1)

            transpose_x(1, xn)
            pe.wait_ge(ld_moe, 3 * 16)
            for t in range(TILES):
                last = mm(ps[:, 0, 8 * t:8 * t + 8], xT[:, P * t:P * t + P], Wg_sb[:, :])
            last.then_inc(gate_ready, 1)
            pe.wait_ge(mask_ready, 1)
            for c in range(3):
                tr(ps[0:D, 1, P * c:P * c + P], mask[:, 8 * c:8 * c + 8, :]).then_inc(maskT_ready, 1)
            pe.wait_ge(b2_set, 3)
            for c in range(3):
                pe.wait_ge(maskT_evac, c + 1)
                mm(ps[:, 2 + c, :], maskT[:, c, :], b2blk[:, :, :]).then_inc(bias_ready, 1)
            pe.wait_ge(bias_used, 3)

            def up(ch, e):
                mm(ps[:, e % 2, :], W1_sb[:, e, :], xT[:, bass.ds(ch * 512, 512)]).then_inc(up_ready, 1)

            def down(ch, e):
                pe.wait_ge(gelu_done, ch * 8 + (e + 1))
                if e == 0:
                    wait(pe, y_used, ch * 4)
                for s in range(4):
                    last = mm(ps[:, 2 + s, D * e:D * e + D], hid[e % 4][:, P * s:P * s + P], W2_sb[:, e, :])
                last.then_inc(down_done, 1)

            def experts(ch, more):
                for e in range(EXPERTS):
                    down(ch, e)
                    if e + 2 < EXPERTS:
                        up(ch, e + 2)
                    elif more:
                        up(ch + 1, e + 2 - EXPERTS)

            up(0, 0)
            up(0, 1)
            with pe.Fori(0, 5) as ch:
                experts(ch, True)
            experts(5, False)

            transpose_x(2, o_tok)

            def project(t):
                wait(pe, raw_ready, 5 * t)
                for b in range(4):
                    mm(ps[:, b, 0:324], xT[:, SEQ * t:SEQ * t + P], slowT[:, 2 * b:2 * b + 2, :])
                for b in range(2):
                    for half in range(2):
                        last = mm(ps[D * half:D * half + D, 4 + b, 0:324], xT[:, SEQ * t + P:SEQ * t + SEQ],
                                  slowT[:, 4 * half + 2 * b:4 * half + 2 * b + 2, :])
                last.then_inc(proj_ready, 1)

            project(0)
            for t in range(IMAGES):
                if t + 1 < IMAGES:
                    project(t + 1)
                pe.wait_ge(hs_ready, t + 1)
                wait(pe, hsT_evac, 2 * t)
                for c in range(3):
                    last = tr(ps[:, 6, P * c:P * c + P], hs[t % 2][:, 4 * c:4 * c + 4, :])
                last.then_inc(hsT_ready, 1)
                pe.wait_ge(hsT_evac, 2 * t + 2)
                wait(pe, mixo_used, 2 * t)
                if t % 2 == 0:
                    parts = ((ps[:, 7, 0:D], 0, P), (ps[0:D, 7, D:2 * D], P, SEQ))
                else:
                    parts = ((ps[D:P, 7, 0:D], 0, D), (ps[:, 7, D:2 * D], D, SEQ))
                for o, c0, c1 in parts:
                    for c in range(2):
                        last = mm(o, hsT[:, c, c0:c1], WoutT[:, c, :], start=(c == 0), stop=(c == 1))
                last.then_inc(mixo_ready, 1)

            transpose_x(3, xn)
            pe.wait_ge(wrB_set, 1)
            pe.wait_ge(ld_ffn, 3 * 16)
            for c in range(6):
                mm(ps[:, c, :], wrB[:, :], xT[:, 512 * c:512 * c + 512]).then_inc(wcol_ready, 1)
            pe.wait_ge(rank_vec, 6)

            def fup(ch, e):
                for a in range(2):
                    mm(ps[:, 2 * e + a, :], w1_sb[:, P * a:P * a + P], xT[:, bass.ds(ch * 512, 512)]).then_inc(fup_ready, 1)

            def fdown(ch, e, c2):
                pe.wait_ge(fgelu_done, ch * 2 + 2)
                wait(pe, out_ready, c2 * 2)
                for s in range(4):
                    for a in range(2):
                        last = mm(ps[:, 4 + e, D * s:D * s + D], fhid[e][:, a, P * s:P * s + P], w2_sb[:, a, :],
                                  start=(a == 0), stop=(a == 1))
                last.then_inc(fdown_ready, 1)

            fup(0, 0)
            with pe.Fori(0, 2) as c2:
                for e in range(2):
                    fup(c2 * 2 + (e + 1), 1 - e)
                    fdown(c2 * 2 + e, e, c2)
            fup(5, 1)
            fdown(4, 0, 2)
            fdown(5, 1, 2)

        @block.vector
        def _(dve):
            st = Steps(dve, vec)

            dve.wait_ge(ident_set, 2)
            by_parity = ident[:, :].rearrange("p (i k y) -> p k i y", i=4, k=2)
            dve.tensor_reduce(par[:, :], by_parity, axis=AXL.XY, op=ALU.add).then_inc(par_set, 2)
            dve.wait_ge(par_set, 2)
            dve.wait_ge(ld_tok, 16)
            o, i = repeat_tokW(0)
            dve.tensor_copy(o, i).then_inc(tokw_rep[0], 1)
            for g in range(1, 6, 2):
                dve.wait_ge(tokw_ready, g + 1)
                for k in range(2):
                    dve.tensor_scalar(Wblk[:, 8 * g:8 * g + 8, k, :], ps[:, TOKW_BANKS[g], :].rearrange("p (n e) -> p n e", e=D),
                                      par[:, k:k + 1], None, ALU.mult).then_inc(tokw_evac_v, 1)
            dve.wait_ge(embed_ready, 1)
            hTv = hT.rearrange("e (b i s j) -> e s i b j", i=4, s=2, j=8)
            dve.tensor_copy(hTv[:, 1, :, :, :], ps[D:P, 4:8, 0:P].rearrange("e i (b j) -> e i b j", j=8)).then_inc(hT_v, 1)
            dve.wait_ge(hback_ready, 1)
            dve.wait_ge(ld_bias, 6 * 16)
            hv = h[:, :, :].rearrange("p (q r) d -> p q r d", r=3)
            for half in range(2):
                s = slice(D * half, D * half + D)
                st.then(dve.tensor_tensor(hv[s, :, half, :], ps[s, 0, :].rearrange("p (q d) -> p q d", d=D),
                                          tokb_sb[s, :].unsqueeze(1).to_broadcast([D, 8, D]), ALU.add))
            dve.wait_ge(ld_text, 3 * 16)

            def spread(a):
                return a.unsqueeze(2).to_broadcast([P, TILES, D])

            def layer_norm(k, src, dst):
                st.then(dve.tensor_reduce(stat[:, 0, :], src, axis=AXL.X, op=ALU.add))
                st.then(dve.tensor_scalar(stat[:, 0, :], stat[:, 0, :], 1.0 / D, None, ALU.mult))
                st.then(dve.tensor_tensor(cen, src, spread(stat[:, 0, :]), ALU.subtract))
                st.then(dve.tensor_tensor(sq, cen, cen, ALU.mult))
                st.then(dve.tensor_reduce(stat[:, 1, :], sq, axis=AXL.X, op=ALU.add))
                dve.tensor_scalar(stat[:, 1, :], stat[:, 1, :], 1.0 / D, EPS, ALU.mult, ALU.add).then_inc(var_ready, 1)
                dve.wait_ge(std_ready, k + 1)
                st.then(dve.reciprocal(stat[:, 0, :], stat[:, 1, :]))
                st.then(dve.tensor_tensor(dst, cen, spread(stat[:, 0, :]), ALU.mult))

            def evacuate_xT(k):
                for c in range(1, 6, 2):
                    dve.wait_ge(tr_ready, 6 * k + c + 1)
                    dve.tensor_copy(xT[:, 512 * c:512 * c + 512], ps[0:D, c, :]).then_inc(tr_evac_v, 1)

            layer_norm(0, h[:, :, :], xn[:, :, :])
            dve.sem_inc(norm_ready, 1)
            evacuate_xT(0)

            def maxima(b, e):
                wait(dve, score_ready, b * 6 - 6)
                for k in range(2):
                    dve.wait_ge(qp_ready, b * 2 + k + 1)
                    to = Qs[e][:, 6 * k:6 * k + 6, :].rearrange("p (i r) (h u) -> p i r h u", i=2, h=2)
                    of = ps[:, k, 0:2 * SEQ].rearrange("p (i r u) -> p i r u", i=2, r=3)
                    dve.tensor_copy(to[:, :, :, 0, :], of[0:D, :, :, :]).then_inc(qp_evac, 1)
                    dve.tensor_copy(to[:, :, 0:2, 1, :], of[D:P, :, 1:3, :]).then_inc(qp_evac, 1)
                    dve.tensor_copy(to[:, :, 2, 1, :], of[D:P, :, 0, :]).then_inc(qp_evac, 1)
                wait(dve, exp_done, b * 12 - 12)
                for m in range(6):
                    dve.wait_ge(score_ready, b * 6 + m + 1)
                    dve.tensor_reduce(negmax[e][:, 2 * m:2 * m + 2],
                                      ps[:, 2 + m % 3, 0:2 * SEQ].rearrange("p (h s) -> p h s", h=2), axis=AXL.X,
                                      op=ALU.max, negate=True).then_inc(max_ready, 1)

            def scale_weights(b, e):
                dve.wait_ge(exp_done, b * 12 + 12)
                wait(dve, wos_ready, b)
                dve.reciprocal(rinv[:, :], rowsum[e][:, :]).then_inc(rinv_set, 1)
                dve.wait_ge(rinv_set, b + 1)
                wait(dve, g_ready, b - 1)
                dve.tensor_tensor(WoS[e][:, :, :], WoT[:, :, :], rinv[:, :].unsqueeze(2).to_broadcast([P, 12, D]), ALU.mult)\
                   .then_inc(wos_ready, 1)

            def residual(b, q, e):
                dve.wait_ge(mix_ready, b + 1)
                own, other = slice(D * e, D * e + D), slice(D - D * e, P - D * e)
                o = ps[:, 7, 0:SEQ].rearrange("p (j d) -> p j d", j=3)
                a = h[own, bass.ds(q * 3 + e, 2), :]
                dve.tensor_tensor(a, a, o[own, 0:3:2, :], ALU.add).then_inc(mix_used, 1)
                a = h[other, bass.ds(q * 3 + 2 * e, 1), :]
                dve.tensor_tensor(a, a, o[other, 1:2, :], ALU.add).then_inc(mix_used, 1)

            maxima(0, 0)
            maxima(1, 1)
            scale_weights(0, 0)
            with dve.Fori(1, IMAGES // 2) as q:
                for e in range(2):
                    maxima(q * 2 + e, e)
                    residual(q * 2 + (e - 2), q - 1, e)
                    scale_weights(q * 2 + (e - 1), 1 - e)
            residual(IMAGES - 2, IMAGES // 2 - 1, 0)
            scale_weights(IMAGES - 1, 1)
            residual(IMAGES - 1, IMAGES // 2 - 1, 1)
            dve.wait_ge(mix_used, 2 * IMAGES)

            layer_norm(1, h[:, :, :], xn[:, :, :])
            dve.sem_inc(norm_ready, 1)
            evacuate_xT(1)
            dve.wait_ge(gate_ready, 1)
            st.then(dve.tensor_tensor(gate[:, :, :], ps[:, 0, 0:TILES * 8].rearrange("p (t e) -> p t e", e=EXPERTS),
                                      bg_sb[:, :].unsqueeze(1).to_broadcast([P, TILES, EXPERTS]), ALU.add))
            st.then(dve.memset(beats, 0.0))
            for a in range(EXPERTS):
                if a:
                    dve.tensor_tensor(beats[:, :, a, 0:a], gate[:, :, 0:a],
                                      gate[:, :, a:a + 1].to_broadcast([P, TILES, a]), ALU.is_ge).then_inc(vec, 1)
                    st.n += 1
                if a < EXPERTS - 1:
                    dve.tensor_tensor(beats[:, :, a, a + 1:], gate[:, :, a + 1:],
                                      gate[:, :, a:a + 1].to_broadcast([P, TILES, EXPERTS - 1 - a]), ALU.is_gt).then_inc(vec, 1)
                    st.n += 1
            dve.wait_ge(vec, st.n)
            st.then(dve.tensor_reduce(mask[:, :, :], beats, axis=AXL.X, op=ALU.add))
            dve.tensor_scalar(mask[:, :, :], mask[:, :, :], 2.0, None, ALU.is_lt).then_inc(mask_ready, 1)
            dve.wait_ge(mask_ready, 1)
            for c in range(3):
                dve.wait_ge(bias_ready, c + 1)
                a = h[:, 8 * c:8 * c + 8, :]
                dve.tensor_tensor(a, a, ps[:, 2 + c, :].rearrange("p (t d) -> p t d", d=D), ALU.add).then_inc(bias_used, 1)
            dve.wait_ge(bias_used, 3)
            ys = Steps(dve, y_vec)
            with dve.Fori(0, 6) as ch:
                ys.base, ys.n = ch * 8, 0
                dve.wait_ge(down_done, ch * 8 + 8)
                for s in range(4):
                    m = mask[:, bass.ds(ch * 4 + s, 1), :].rearrange("p a e -> p (a e)").unsqueeze(2).to_broadcast([P, EXPERTS, D])
                    dve.tensor_tensor(ysel[s % 2], ps[:, 2 + s, :].rearrange("p (e d) -> p e d", e=EXPERTS), m, ALU.mult)\
                       .then_inc(y_used, 1)
                    dve.wait_ge(y_used, ch * 4 + (s + 1))
                    ys.then(dve.tensor_reduce(ysum, ysel[s % 2].rearrange("p e d -> p d e"), axis=AXL.X, op=ALU.add))
                    a = h[:, bass.ds(ch * 4 + s, 1), :]
                    ys.then(dve.tensor_tensor(a, a, ysum.unsqueeze(1), ALU.add))

            layer_norm(2, h[:, :, :], xn[:, :, :])
            layer_norm(3, xn[:, :, :], o_tok)
            st.then(dve.tensor_tensor(o_tok, o_tok, g_sb[:, :].unsqueeze(1).to_broadcast([P, TILES, D]), ALU.mult))
            st.then(dve.tensor_tensor(o_tok, o_tok, b_sb[:, :].unsqueeze(1).to_broadcast([P, TILES, D]), ALU.add))
            dve.sem_inc(norm_ready, 1)
            st.then(dve.tensor_tensor(h[:, :, :], h[:, :, :], xn[:, :, :], ALU.add))
            evacuate_xT(2)
            dve.wait_ge(tr_evac_v, 9)
            dve.memset(gram[:, :, :], 1.0).then_inc(vec, 1)
            st.n += 1
            st.then(dve.memset(QE[:, :, :, :], 1.0))

            def over_time(a, n):
                return a.unsqueeze(1).to_broadcast([P, n, a.shape[1]])

            def over_width(a):
                return a.unsqueeze(3).to_broadcast([P, a.shape[1], BOTH, DH])

            def pre(t):
                dve.wait_ge(raw_ready, 5 * t + 1)
                kt = KK[:, t, :].rearrange("p (u c d) -> p u c d", c=2, d=DH)
                ut = UU[:, t, :].rearrange("p (r d) -> p r d", d=DH)
                rk, bt = kt[:, :, 1, :], beta[t % 2]
                st.then(dve.tensor_reduce(rk_top[:, :], rk, axis=AXL.X, op=ALU.max))
                dve.tensor_tensor(rk, rk, rk_top[:, :].unsqueeze(2).to_broadcast([P, UNITS, DH]), ALU.subtract).then_inc(rk_in, 1)
                dve.wait_ge(raw_ready, 5 * t + 5)
                st.then(dve.tensor_scalar(bt[:, :, :], bt[:, :, :], 1.0, None, ALU.add))
                st.then(dve.reciprocal(bt[:, :, :], bt[:, :, :]))
                st.then(dve.tensor_tensor(ut, ut, bt[:, :, :].rearrange("p u c -> p (u c)").unsqueeze(2)
                                          .to_broadcast([P, BOTH, DH]), ALU.mult))
                for dst, c in ((QE[:, :, 0, :], 0), (kt[:, :, 0, :], 1)):
                    st.then(dve.scalar_tensor_tensor(out=dst, in0=exp_qk[:, :, DH * c:DH * c + DH], scalar=1.0,
                                                     in1=relu_qk[:, :, DH * c:DH * c + DH], op0=ALU.min, op1=ALU.add))
                dve.sem_inc(pre_used, 1)

            def update(t):
                dve.wait_ge(rk_exp, t + 1)
                kt = KK[:, t, :].rearrange("p (r d) -> p r d", d=DH)
                st.then(dve.tensor_reduce(ksum[:, :], kt, axis=AXL.X, op=ALU.add))
                st.then(dve.reciprocal(ksum[:, :], ksum[:, :]))
                st.then(dve.tensor_tensor(kt, kt, ksum[:, :].unsqueeze(2).to_broadcast([P, BOTH, DH]), ALU.mult))
                if t:
                    pt = prod[:, 0:t, :]
                    st.then(dve.tensor_tensor(pt, KK[:, 0:t, :], over_time(KK[:, t, :], t), ALU.mult))
                    gt = gram[:, 0:t, :]
                    st.then(dve.tensor_reduce(gt, pt.rearrange("p t (r d) -> p t r d", d=DH), axis=AXL.X, op=ALU.add))
                    st.then(dve.scalar_tensor_tensor(out=gt, in0=gt, scalar=-1.0,
                                                     in1=over_time(beta[t % 2][:, :, :].rearrange("p u c -> p (u c)"), t),
                                                     op0=ALU.mult, op1=ALU.mult))
                    pt = prod[:, 0:t + 1, :]
                    st.then(dve.tensor_tensor(pt.rearrange("p t (r d) -> p t r d", d=DH),
                                              UU[:, 0:t + 1, :].rearrange("p t (r d) -> p t r d", d=DH),
                                              over_width(gram[:, 0:t + 1, :]), ALU.mult))
                    st.then(dve.tensor_reduce(UU[:, t, :], pt.rearrange("p t r -> p r t"), axis=AXL.X, op=ALU.add))

            def read(t):
                if t:
                    dve.wait_ge(soft_exp, t)
                qe = QE[:, :, :, :].rearrange("p u c d -> p (u c) d")
                st.then(dve.tensor_reduce(qsum[:, :], qe, axis=AXL.X, op=ALU.add))
                st.then(dve.reciprocal(qsum[:, :], qsum[:, :]))
                pt = prod[:, 0:t + 1, :]
                st.then(dve.tensor_tensor(pt, KK[:, 0:t + 1, :], over_time(QE[:, :, :, :].rearrange("p u c d -> p (u c d)"), t + 1),
                                          ALU.mult))
                ct = coef[:, 0:t + 1, :]
                st.then(dve.tensor_reduce(ct, pt.rearrange("p t (r d) -> p t r d", d=DH), axis=AXL.X, op=ALU.add))
                st.then(dve.tensor_tensor(ct, ct, over_time(qsum[:, :], t + 1), ALU.mult))
                st.then(dve.tensor_tensor(pt.rearrange("p t (r d) -> p t r d", d=DH),
                                          UU[:, 0:t + 1, :].rearrange("p t (r d) -> p t r d", d=DH), over_width(ct), ALU.mult))
                wait(dve, hsT_ready, t - 1)
                dve.tensor_reduce(hs[t % 2][:, :, :], pt.rearrange("p t (u c d) -> p u d t c", c=2, d=DH), axis=AXL.XY,
                                  op=ALU.add).then_inc(hs_ready, 1)
                dve.wait_ge(hs_ready, t + 1)

            def soft(t):
                st.then(dve.tensor_reduce(top[:, :], hs[t % 2][:, :, :], axis=AXL.X, op=ALU.max))
                dve.tensor_tensor(QE[:, :, 1, :], hs[t % 2][:, :, :], top[:, :].unsqueeze(2).to_broadcast([P, UNITS, DH]),
                                  ALU.subtract).then_inc(soft_in, 1)

            def add_out(t):
                dve.wait_ge(mixo_ready, t + 1)
                q, e = t // 2, t % 2
                if e == 0:
                    parts = ((slice(0, P), 3 * q, 0), (slice(0, D), 3 * q + 1, D))
                else:
                    parts = ((slice(D, P), 3 * q + 1, 0), (slice(0, P), 3 * q + 2, D))
                for s, tile, c in parts:
                    dve.tensor_tensor(h[s, tile, :], h[s, tile, :], ps[s, 7, c:c + D], ALU.add).then_inc(mixo_used, 1)

            pre(0)
            update(0)
            for t in range(IMAGES):
                read(t)
                if t + 1 < IMAGES:
                    soft(t)
                    pre(t + 1)
                    update(t + 1)
                add_out(t)
            dve.wait_ge(mixo_used, 2 * IMAGES)

            dve.wait_ge(ld_ffn, 3 * 16)
            dve.tensor_copy(wrB[:, :], wr_sb[:, :].to_broadcast([D, P])).then_inc(wrB_set, 1)
            layer_norm(4, h[:, :, :], xn[:, :, :])
            dve.sem_inc(norm_ready, 1)
            st.then(dve.tensor_tensor(h[:, :, :], h[:, :, :], xn[:, :, :], ALU.add))
            evacuate_xT(3)
            for c in range(6):
                dve.wait_ge(wcol_ready, c + 1)
                dve.tensor_scalar(wcols[:, 512 * c:512 * c + 512], ps[:, c, :], br_sb[:, 0:1], None, ALU.add).then_inc(rank_vec, 1)
            dve.wait_ge(rank_vec, 6)
            dve.wait_ge(masks_set, 5)
            st.then(dve.tensor_tensor(wdiag, wcols.rearrange("p (t j) -> p t j", j=P),
                                      ident[:, :].unsqueeze(1).to_broadcast([P, TILES, P]), ALU.mult))
            st.then(dve.tensor_reduce(wtok[:, :], wdiag, axis=AXL.X, op=ALU.add))
            rv = Steps(dve, rank_vec)
            with dve.Fori(0, IMAGES // 2) as q:
                rv.base, rv.n = q * 8 + 6, 0
                for s, r, e, k in ((slice(0, P), 0, 0, 0), (slice(0, D), 1, 0, 1), (slice(D, P), 1, 1, 1), (slice(0, P), 2, 1, 2)):
                    cols = wcols[s, bass.ds(q * 384 + SEQ * e, SEQ)]
                    own = wtok[s, bass.ds(q * 3 + r, 1)]
                    rv.then(dve.scalar_tensor_tensor(out=tie[s, :], in0=cols, scalar=own, in1=earlier[s, k, :],
                                                     op0=ALU.is_equal, op1=ALU.mult))
                    rv.then(dve.scalar_tensor_tensor(out=over[s, :], in0=cols, scalar=own, in1=tie[s, :],
                                                     op0=ALU.is_gt, op1=ALU.add, accum_out=rank[s, bass.ds(q * 3 + r, 1)]))
            st.then(dve.scalar_tensor_tensor(out=wkeep[:, :], in0=rank[:, :], scalar=float(KEPT), in1=wtok[:, :],
                                             op0=ALU.is_lt, op1=ALU.mult))
            fs = Steps(dve, fy_vec)
            with dve.Fori(0, 3) as c2:
                fs.base, fs.n = c2 * 4, 0
                for e in range(2):
                    ch = c2 * 2 + e
                    dve.wait_ge(fdown_ready, ch + 1)
                    fs.then(dve.tensor_tensor(fy, ps[:, 4 + e, 0:4 * D].rearrange("p (s d) -> p s d", d=D),
                                              fb2_sb[:, :].unsqueeze(1).to_broadcast([P, 4, D]), ALU.add))
                    fs.then(dve.tensor_tensor(fy, fy, wkeep[:, bass.ds(ch * 4, 4)].unsqueeze(2).to_broadcast([P, 4, D]), ALU.mult))
                    a = h[:, bass.ds(ch * 4, 4), :]
                    dve.tensor_tensor(a, a, fy, ALU.add).then_inc(out_ready, 1)
                    dve.wait_ge(out_ready, ch + 1)


_INS = ['x', 'txt', 'L0_tok_W', 'L0_tok_b', 'L0_attn_Wq', 'L0_attn_Wk', 'L0_attn_Wv', 'L0_attn_Wo', 'L0_ffn_Wg',
        'L0_ffn_bg', 'L0_ffn_W1', 'L0_ffn_b1', 'L0_ffn_W2', 'L0_ffn_b2', 'L1_attn_slow_W', 'L1_attn_out_W',
        'L1_attn_ln_g', 'L1_attn_ln_b', 'L1_ffn_wr', 'L1_ffn_br', 'L1_ffn_w1', 'L1_ffn_b1', 'L1_ffn_w2', 'L1_ffn_b2']


def kernel(**inputs):
    import numpy as _np
    import concourse.bacc as _bacc
    from concourse import mybir as _mybir
    from concourse.bass_utils import run_bass_kernel_spmd as _run

    nc = _bacc.Bacc("TRN2", target_bir_lowering=False, num_devices=1)
    arrays, args = {}, []
    for name in _INS:
        a = _np.ascontiguousarray(inputs[name])
        arrays[f"in_{name}_dram"] = a
        args.append(nc.dram_tensor(f"in_{name}_dram", a.shape, _mybir.dt.from_np(a.dtype), kind="ExternalInput").ap())
    result = nc.dram_tensor("out_0_dram", (IMAGES, SEQ, D), F32, kind="ExternalOutput").ap()
    token_mixer_kernel(nc, *args, result)
    r = _run(nc, [arrays], core_ids=[0])
    return r.results[0]["out_0_dram"]
```

```python
import concourse.bass as bass
from concourse import mybir
from contextlib import ExitStack

F32 = mybir.dt.float32
F32R = mybir.dt.float32r
ALU = mybir.AluOpType
ACT = mybir.ActivationFunctionType
AXL = mybir.AxisListType

IMAGES, CHANNELS, SIDE, PATCH = 16, 3, 128, 16
GRID = SIDE // PATCH
D = 64
SEQ = GRID * GRID + 128
P = 128
TILES = IMAGES * SEQ // P
HEADS = 8
PAIRS = HEADS // 2
EXPERTS, HIDDEN = 8, 128
DH = 32
UNITS = 12
BOTH = 2 * UNITS
ROW = BOTH * DH
FFN_HIDDEN = 256
KEPT = SEQ // 2 - 1
EPS = 1e-5


def token_mixer_kernel(nc, x, txt, tok_W, tok_b, Wq, Wk, Wv, Wo, Wg, bg, W1, b1, W2, b2, slow_W, out_W,
                       ln_g, ln_b, wr, br, w1, fb1, w2, fb2, out):
    ctx = ExitStack()
    with ctx:
        ps = ctx.enter_context(nc.psum_tensor("ps", [P, 8, 512], F32))

        class Place:
            def __init__(self):
                self.stack = ExitStack()

            def __call__(self, name, shape, dtype=F32):
                return self.stack.enter_context(nc.sbuf_tensor(name, shape, dtype))

        sb = Place()
        ctx.enter_context(sb.stack)
        h = sb("h", [P, TILES, D])
        xn = sb("xn", [P, TILES, 2, D])
        ident = sb("ident", [P, P])
        stat = sb("stat", [P, 2, TILES])
        slowT = sb("slowT", [D, HEADS, 162])
        WoutT = sb("WoutT", [P, 2, D])
        b1T = sb("b1T", [P, EXPERTS])
        fb1T = sb("fb1T", [P, 2])
        bg_sb = sb("bg_sb", [P, EXPERTS])
        tokb_sb = sb("tokb_sb", [P, D])
        g_sb = sb("g_sb", [P, D])
        b_sb = sb("b_sb", [P, D])
        br_sb = sb("br_sb", [P, 1])
        w2_sb = sb("w2_sb", [P, 2, D])
        fb2_sb = sb("fb2_sb", [P, D])
        FW1, FWR, FWG = 0, FFN_HIDDEN, FFN_HIDDEN + P
        fsplit = sb("fsplit", [P, FFN_HIDDEN + P + EXPERTS], F32R)

        early = Place()
        xTH = early("xTH", [P, TILES * P], F32R)
        xTL = early("xTL", [P, TILES * P], F32R)
        Nh = early("Nh", [P, HEADS, P], F32R)
        WvT = early("WvT", [P, P], F32R)
        W1s = early("W1s", [P, EXPERTS, HIDDEN], F32R)
        W1_raw = early("W1_raw", [P, EXPERTS, HIDDEN])
        fraw = early("fraw", [P, FFN_HIDDEN + P + EXPERTS])
        wr_raw = early("wr_raw", [P, 1])
        W2_sb = early("W2_sb", [HIDDEN, EXPERTS, D])
        WoT = early("WoT", [P, 12, D])
        b2rep = early("b2rep", [D, D])
        b2blk = early("b2blk", [D, 8, D])
        Wq_raw = early("Wq_raw", [D, HEADS, 2, D])
        Wk_raw = early("Wk_raw", [D, D])
        Wv_raw = early("Wv_raw", [D, 2, D])
        Wo_raw = early("Wo_raw", [D, HEADS * D])
        slowA = early("slowA", [96, HEADS, D])
        slowB = early("slowB", [66, HEADS, D])
        outW_raw = early("outW_raw", [D, 256])
        b1_raw = early("b1_raw", [EXPERTS, HIDDEN])
        fb1_raw = early("fb1_raw", [2, P])

        embed = Place()
        tokW_raw = embed("tokW_raw", [D, CHANNELS * PATCH * PATCH])
        tokWT = embed("tokWT", [CHANNELS * PATCH, PATCH, D])
        pixels = embed("pixels", [CHANNELS * PATCH, IMAGES * GRID * SIDE])
        embed.stack.close()

        attn = Place()
        cen = attn("cen", [P, TILES, D])[:, :, :]
        sq = attn("sq", [P, TILES, D])[:, :, :]
        Qs = [attn(f"Qs{i}", [P, 12, 2, D], F32R) for i in range(2)]
        probs = [attn(f"probs{i}", [P, 12, SEQ]) for i in range(2)]
        WoS = [attn(f"WoS{i}", [P, 12, D]) for i in range(2)]
        negmax = [attn(f"negmax{i}", [P, 12]) for i in range(2)]
        rowsum = [attn(f"rowsum{i}", [P, 12]) for i in range(2)]
        rinv = attn("rinv", [P, 12])
        Glo = [attn(f"Glo{i}", [P, 3, D]) for i in range(2)]
        Ghi = [attn(f"Ghi{i}", [D, 3, D]) for i in range(2)]
        Vlo = [attn(f"Vlo{i}", [P, 2, D]) for i in range(2)]
        Vhi = [attn(f"Vhi{i}", [D, 2, D]) for i in range(2)]
        attn.stack.close()

        moe = Place()
        moe("layer_norm_scratch", [P, 2, TILES, D])
        gate = moe("gate", [P, TILES, EXPERTS])
        mask = moe("mask", [P, TILES, EXPERTS])
        maskT = moe("maskT", [D, 3, P])
        beats = moe("beats", [P, TILES, EXPERTS, EXPERTS])[:, :, :, :]
        hid = [moe(f"hid{i}", [P, 512])[:, :] for i in range(4)]
        ysel = [moe(f"ysel{i}", [P, EXPERTS, D])[:, :, :] for i in range(2)]
        ysum = moe("ysum", [P, D])[:, :]
        moe.stack.close()
        early.stack.close()

        fast = Place()
        KK = fast("keys", [P, IMAGES, ROW])[:, :, :]
        UU = fast("values", [P, IMAGES, ROW])[:, :, :]
        prod = fast("prod", [P, IMAGES, ROW])[:, :, :]
        GRAM_ROWS = [prod[:, 3 * i:3 * i + 3, :] for i in range(2)]
        SUM_ROWS = [prod[:, 6 + 2 * i:8 + 2 * i, :] for i in range(3)]
        COEF_ROWS = prod[:, 12:16, :]
        o_tok = prod[:, 0:2, :].rearrange("p a r -> p (a r)").rearrange("p (t d) -> p t d", d=D)
        xT = fast("xT", [D, TILES * P])
        QE = fast("QE", [P, UNITS, 2, DH])
        relu_qk = fast("relu_qk", [P, UNITS, 2 * DH])
        exp_qk = fast("exp_qk", [P, UNITS, 2 * DH])
        beta = [fast(f"beta{i}", [P, UNITS, 2]) for i in range(2)]
        top = fast("top", [P, UNITS])
        rk_top = fast("rk_top", [P, UNITS])
        ksum = fast("ksum", [P, BOTH])
        qsum = fast("qsum", [P, BOTH])
        hs = [fast(f"hs{i}", [P, UNITS, DH]) for i in range(2)]
        hsT = fast("hsT", [P, 2, SEQ])
        fast.stack.close()

        late = Place()
        xTH3 = late("xTH3", [P, TILES * P], F32R)
        xTL3 = late("xTL3", [P, TILES * P], F32R)
        cen3 = late("cen3", [P, TILES, D])[:, :, :]
        sq3 = late("sq3", [P, TILES, D])[:, :, :]
        wcols = late("wcols", [P, TILES * P])[:, :]
        wdiag = late("wdiag", [P, TILES, P])[:, :, :]
        earlier = late("earlier", [P, 3, SEQ])
        tie = late("tie", [P, SEQ])[:, :]
        over = late("over", [P, SEQ])[:, :]
        fhid = [late(f"fhid{i}", [P, 2, 512]) for i in range(2)]
        fy = late("fy", [P, 4, D])[:, :, :]
        wtok = late("wtok", [P, TILES])
        rank = late("rank", [P, TILES])
        wkeep = late("wkeep", [P, TILES])
        late.stack.close()

        def sem(name):
            return ctx.enter_context(nc.semaphore(name))

        ld_attn, ld_slow, ld_tok, ld_image, ld_text, ld_rep, ld_moe, ld_ffn, ld_bias = (
            sem(n) for n in ("ld_attn", "ld_slow", "ld_tok", "ld_image", "ld_text", "ld_rep", "ld_moe", "ld_ffn", "ld_bias"))
        ld_image = [sem(f"ld_image{c}") for c in range(4)]
        ident_set, masks_set, b2_set = sem("ident_set"), sem("masks_set"), sem("b2_set")
        wr_set, split_high, split_low = sem("wr_set"), sem("split_high"), sem("split_low")
        tokw_ready, tokw_evac, embed_ready = sem("tokw_ready"), sem("tokw_evac"), sem("embed_ready")
        wt_ready, wt_evac, wt2_ready, wt2_evac = sem("wt_ready"), sem("wt_evac"), sem("wt2_ready"), sem("wt2_evac")
        vec = sem("vec")
        var_ready, std_ready = sem("var_ready"), sem("std_ready")
        norm_ready = sem("norm_ready")
        tr_ready, tr_evac_a, tr_evac_v = sem("tr_ready"), sem("tr_evac_a"), sem("tr_evac_v")
        qp_ready, qp_evac, score_ready, max_ready, exp_done, wos_ready, g_ready, g_evac, mix_ready, mix_used = (
            sem(n) for n in ("qp_ready", "qp_evac", "score_ready", "max_ready", "exp_done", "wos_ready", "g_ready",
                             "g_evac", "mix_ready", "mix_used"))
        rinv_set, q_high, v_ready, v_evac = (sem(n) for n in ("rinv_set", "q_high", "v_ready", "v_evac"))
        gate_ready, mask_ready, maskT_ready, maskT_evac, bias_ready, bias_used = (
            sem(n) for n in ("gate_ready", "mask_ready", "maskT_ready", "maskT_evac", "bias_ready", "bias_used"))
        up_ready, gelu_done, down_done, y_used, y_vec = (
            sem(n) for n in ("up_ready", "gelu_done", "down_done", "y_used", "y_vec"))
        proj_ready, raw_ready, rk_in, rk_exp, pre_used, hs_ready, soft_in, soft_exp, hsT_ready, hsT_evac, mixo_ready, mixo_used = (
            sem(n) for n in ("proj_ready", "raw_ready", "rk_in", "rk_exp", "pre_used", "hs_ready", "soft_in",
                             "soft_exp", "hsT_ready", "hsT_evac", "mixo_ready", "mixo_used"))
        keys_ready, gram_prod, gram_used, prod_ready, summed, u_sum, u_evac = (
            sem(n) for n in ("keys_ready", "gram_prod", "gram_used", "prod_ready", "summed", "u_sum", "u_evac"))
        wcol_ready, rank_vec, fup_ready, fgelu_done, fdown_ready, fy_vec, out_ready, stored = (
            sem(n) for n in ("wcol_ready", "rank_vec", "fup_ready", "fgelu_done", "fdown_ready", "fy_vec",
                             "out_ready", "stored"))
        fy_free = sem("fy_free")

        def wait(eng, s, value):
            if not (isinstance(value, int) and value <= 0):
                eng.wait_ge(s, value)

        def in_range(s):
            return not isinstance(s, int) or 0 <= s < IMAGES

        def attention_loop(eng, step):
            for s in range(4):
                step(s, s % 2, s // 2)
            with eng.Fori(2, IMAGES // 2 - 1) as q:
                for e in range(2):
                    step(q * 2 + e, e, q)
            for s in range(IMAGES - 2, IMAGES + 2):
                step(s, s % 2, s // 2)

        class Steps:
            def __init__(self, eng, s):
                self.eng, self.s, self.base, self.n = eng, s, 0, 0

            def then(self, ins):
                ins.then_inc(self.s, 1)
                self.n += 1
                self.eng.wait_ge(self.s, self.base + self.n)

        SLOW_BANKS = (0, 1, 4)
        SCALE = float(D // HEADS) ** -0.5

        def chunk(n):
            return (2 * (n // 3) - n % 3) % 3

        def columns(n, half):
            hd, r = 2 * (n // 3) + half, (n % 3 + half) % 3
            return (8 * r + hd - chunk(n)) // 3

        FEATURES = 5 * DH + 2
        units = ps[:, 0:2, 0:3 * FEATURES].rearrange("p b (s f) -> p b s f", s=3)
        gram = ps[:, 2, 0:IMAGES * BOTH].rearrange("p (t r) -> p t r", r=BOTH)
        coef = ps[:, 3, 0:IMAGES * BOTH].rearrange("p (t r) -> p t r", r=BOTH)
        HALF_ROW = ROW // 2
        U_BANK, HS_BANK, OUT_BANK = 4, 6, 7

        def bs(a, i):
            return a[:, 6 * i:6 * i + 6, :].rearrange("p (b s) f -> p b s f", s=3)

        def sum_chunks(n):
            return (n + 1) // 2

        def gram_chunks(n):
            return (n + 2) // 3

        def sums_before(t, reading):
            n = sum(sum_chunks(i) + sum_chunks(i + 1) for i in range(t))
            return n + sum_chunks(t) if reading else n

        def grams_before(t):
            return sum(gram_chunks(i) for i in range(1, t))

        def f32(a):
            return a.bitcast(F32)

        block = ctx.enter_context(nc.Block())

        @block.sync
        def _(sp):
            sp.dma_start(tokW_raw[:, :], tok_W).then_inc(ld_tok, 16)
            pix_v = pixels[:, :].rearrange("p (n i w) -> p n i w", n=IMAGES, i=GRID)
            for n in range(IMAGES):
                for k in range(CHANNELS):
                    sp.dma_start(pix_v[PATCH * k:PATCH * k + PATCH, n, :, :], x[n, k, :, :].rearrange("(i y) w -> y i w", y=PATCH))\
                      .then_inc(ld_image[n // 4], 16)
            for half in range(2):
                rows_ = slice(D * half, D * half + D)
                sp.dma_start(W1_raw[rows_, :, :], W1.rearrange("e d k -> d e k")).then_inc(ld_moe, 16)
                sp.dma_start(fraw[rows_, FWG:FWG + EXPERTS], Wg).then_inc(ld_moe, 16)
                sp.dma_start(wr_raw[rows_, :], wr).then_inc(ld_moe, 16)
                sp.dma_start(fraw[rows_, FW1:FW1 + FFN_HIDDEN], w1).then_inc(ld_moe, 16)
            sp.dma_start(W2_sb[:, :, :], W2.rearrange("e k d -> k e d")).then_inc(ld_moe, 16)
            sp.dma_start(w2_sb[:, :, :], w2.rearrange("(a k) d -> k a d", a=2)).then_inc(ld_ffn, 16)
            out_t = out.rearrange("b s d -> (b s) d").rearrange("(t p) d -> p t d", p=P)
            with sp.Fori(0, 6) as ch:
                sp.wait_ge(out_ready, ch + 1)
                sp.dma_start(out_t[:, bass.ds(ch * 4, 4), :], h[:, bass.ds(ch * 4, 4), :]).then_inc(stored, 16)
            sp.wait_ge(stored, 6 * 16)

        @block.gpsimd
        def _(pool):
            pool.memset(ident[:, :], 0.0).then_inc(ident_set, 1)
            pool.wait_ge(ident_set, 1)
            pool.affine_select(out=ident[:, :], in_=ident[:, :], compare_op=ALU.not_equal, fill=1.0, base=0,
                               pattern=[[-1, P]], channel_multiplier=1).then_inc(ident_set, 1)
            for c in range(8):
                pool.dma_start(b2rep[8 * c:8 * c + 8, :], b2).then_inc(ld_rep, 16)
            for dst, src in ((bg_sb, bg), (tokb_sb, tok_b), (g_sb, ln_g), (b_sb, ln_b), (br_sb, br), (fb2_sb, fb2)):
                pool.dma_start(dst[:, :], src.partition_broadcast(P)).then_inc(ld_bias, 16)
            pool.wait_ge(ld_rep, 8 * 16)
            pool.tensor_copy(b2blk[:, :, :], b2rep[:, :].unsqueeze(1).to_broadcast([D, 8, D])).then_inc(b2_set, 1)
            pool.wait_ge(b2_set, 1)
            pool.affine_select(out=b2blk[:, :, :], in_=b2blk[:, :, :], compare_op=ALU.is_ge, fill=0.0, base=0,
                               pattern=[[-8, 8], [0, D]], channel_multiplier=1).then_inc(b2_set, 1)
            pool.wait_ge(b2_set, 2)
            pool.affine_select(out=b2blk[:, :, :], in_=b2blk[:, :, :], compare_op=ALU.is_ge, fill=0.0, base=7,
                               pattern=[[8, 8], [0, D]], channel_multiplier=-1).then_inc(b2_set, 1)

            for t in range(1, IMAGES):
                pool.wait_ge(keys_ready, t + 1)
                for c in range(gram_chunks(t)):
                    m, n = grams_before(t) + c, min(3, t - 3 * c)
                    wait(pool, gram_used, m - 1)
                    pool.tensor_tensor(GRAM_ROWS[m % 2][:, 0:n, :], KK[:, 3 * c:3 * c + n, :],
                                       KK[:, t, :].unsqueeze(1).to_broadcast([P, n, ROW]), ALU.mult).then_inc(gram_prod, 1)

            pool.wait_ge(norm_ready, 4)
            masks = Steps(pool, masks_set)
            masks.then(pool.memset(earlier[:, :, :], 1.0))
            for rows_, k, base in ((slice(0, P), 0, 0), (slice(0, D), 1, P), (slice(D, P), 1, 0), (slice(0, P), 2, D)):
                m = earlier[rows_, k, :]
                masks.then(pool.affine_select(out=m, in_=m, compare_op=ALU.is_gt, fill=0.0, base=base,
                                              pattern=[[-1, SEQ]], channel_multiplier=1))

        @block.scalar
        def _(act):
            for half in range(2):
                act.dma_start(Wq_raw[:, :, half, :], Wq.rearrange("(h k) c -> k h c", k=D)).then_inc(ld_attn, 16)
                act.dma_start(Wv_raw[:, half, :], Wv).then_inc(ld_attn, 16)
            act.dma_start(Wk_raw[:, :], Wk).then_inc(ld_attn, 16)
            act.dma_start(Wo_raw[:, :], Wo).then_inc(ld_attn, 16)
            act.dma_start(slowA[0:64, :, :], slow_W.rearrange("(h f) c -> f h c", h=HEADS)[0:64, :, :]).then_inc(ld_slow, 16)
            act.dma_start(slowA[64:96, :, :], slow_W.rearrange("(h f) c -> f h c", h=HEADS)[96:128, :, :]).then_inc(ld_slow, 16)
            act.dma_start(slowB[0:32, :, :], slow_W.rearrange("(h f) c -> f h c", h=HEADS)[64:96, :, :]).then_inc(ld_slow, 16)
            act.dma_start(slowB[32:66, :, :], slow_W.rearrange("(h f) c -> f h c", h=HEADS)[128:162, :, :]).then_inc(ld_slow, 16)
            act.dma_start(outW_raw[:, :], out_W).then_inc(ld_slow, 16)
            act.dma_start(b1_raw[:, :], b1).then_inc(ld_slow, 16)
            act.dma_start(fb1_raw[:, :], fb1.rearrange("(a k) -> a k", a=2)).then_inc(ld_slow, 16)
            hv = h[:, :, :].rearrange("p (q r) d -> p q r d", r=3)
            tv = txt.rearrange("(q two) s d -> two s q d", two=2)
            act.dma_start(hv[D:P, :, 0, :], tv[0, 0:D, :, :]).then_inc(ld_text, 16)
            act.dma_start(hv[0:D, :, 1, :], tv[0, D:P, :, :]).then_inc(ld_text, 16)
            act.dma_start(hv[:, :, 2, :], tv[1, :, :, :]).then_inc(ld_text, 16)

            act.wait_ge(tokw_ready, 1)
            for c in range(2):
                act.activation(tokWT[:, 8 * c:8 * c + 8, :], ps[0:CHANNELS * PATCH, c, :], ACT.Copy).then_inc(tokw_evac, 1)
            act.wait_ge(wt_ready, 1)
            for c in range(2):
                act.activation(Nh[:, 4 * c:4 * c + 4, :], ps[:, 4 + c, :], ACT.Copy, scale=SCALE).then_inc(split_high, 1)
            act.wait_ge(wt_ready, 2)
            act.activation(WvT[:, :], ps[:, 7, 256:384], ACT.Copy).then_inc(split_high, 1)
            act.activation(WoT[:, 0:8, :], ps[:, 6, :], ACT.Copy).then_inc(wt_evac, 1)
            act.activation(WoT[:, 8:12, :], ps[:, 7, 0:256], ACT.Copy).then_inc(wt_evac, 1)
            act.activation(WoutT[:, :, :], ps[:, 7, 384:512], ACT.Copy).then_inc(wt_evac, 1)
            act.wait_ge(ld_moe, 9 * 16)
            act.activation(W1s[:, :, :], W1_raw[:, :, :], ACT.Copy).then_inc(split_high, 1)
            act.wait_ge(wr_set, 1)
            act.activation(fsplit[:, :], fraw[:, :], ACT.Copy).then_inc(split_high, 1)
            act.wait_ge(wt2_ready, 1)
            act.activation(b1T[:, :], ps[:, 5, 0:8], ACT.Copy).then_inc(wt2_evac, 1)
            act.activation(fb1T[:, :], ps[:, 5, 8:10], ACT.Copy).then_inc(wt2_evac, 1)
            for c in range(3):
                n = min(3, HEADS - 3 * c)
                act.activation(slowT[:, 3 * c:3 * c + n, :], ps[0:D, SLOW_BANKS[c], 0:162 * n], ACT.Copy).then_inc(wt2_evac, 1)

            def std(k):
                act.wait_ge(var_ready, k + 1)
                act.activation(stat[:, 1, :], stat[:, 1, :], ACT.Sqrt).then_inc(std_ready, 1)

            def split_xT(k, high):
                for c in range(6):
                    act.wait_ge(tr_ready, 6 * k + c + 1)
                    act.activation(high[:, 512 * c:512 * c + 512], ps[:, c, :], ACT.Copy).then_inc(tr_evac_a, 1)

            std(0)
            split_xT(0, xTH)

            def q_halves(b, e):
                wait(act, score_ready, b * 6 - 6)
                for i in range(PAIRS):
                    act.wait_ge(qp_ready, b * 4 + (i + 1))
                    act.activation(Qs[e][:, 3 * i:3 * i + 3, :, :].rearrange("p r h u -> p h r u"),
                                   ps[:, i % 2, 0:2 * SEQ].rearrange("p (h r u) -> p h r u", h=2, r=3), ACT.Copy)\
                       .then_inc(q_high, 1)

            def exps(b, e):
                wait(act, g_ready, b - 1)
                wait(act, wos_ready, b - 1)
                for m in range(6):
                    act.wait_ge(max_ready, b * 6 + m + 1)
                    for s in range(2):
                        n = 2 * m + s
                        act.activation(probs[e][:, n, :], ps[:, 2 + m % 3, SEQ * s:SEQ * s + SEQ], ACT.Exp,
                                       bias=negmax[e][:, n:n + 1], accum_out=rowsum[e][:, n:n + 1]).then_inc(exp_done, 1)

            def evacuate_g(b, e):
                act.wait_ge(g_ready, b + 1)
                wait(act, mix_ready, b - 1)
                act.activation(Glo[e][:, :, :], ps[:, 6, 0:SEQ], ACT.Copy).then_inc(g_evac, 1)
                act.activation(Ghi[e][:, :, :], ps[0:D, 6, SEQ:2 * SEQ], ACT.Copy).then_inc(g_evac, 1)

            def attention_step(s, e, q):
                if in_range(s + 1):
                    q_halves(s + 1, 1 - e)
                if in_range(s):
                    exps(s, e)
                if in_range(s - 1):
                    evacuate_g(s - 1, 1 - e)

            q_halves(0, 0)
            attention_loop(act, attention_step)

            std(1)
            split_xT(1, xTH)
            act.wait_ge(maskT_ready, 3)
            for c in range(3):
                act.activation(maskT[:, c, :], ps[0:D, 1, P * c:P * c + P], ACT.Copy).then_inc(maskT_evac, 1)
            with act.Fori(0, 6) as ch:
                for e in range(EXPERTS):
                    act.wait_ge(up_ready, ch * 8 + e + 1)
                    act.wait_ge(down_done, ch * 8 + (e - 2 if e >= 4 else 1))
                    act.activation(hid[e % 4], ps[:, e % 2, :], ACT.Gelu, bias=b1T[:, e:e + 1]).then_inc(gelu_done, 1)

            std(2)
            std(3)
            for c in range(0, 6, 2):
                act.wait_ge(tr_ready, 12 + c + 1)
                act.activation(xT[:, 512 * c:512 * c + 512], ps[0:D, c, :], ACT.Copy).then_inc(tr_evac_a, 1)

            def pre(t):
                kt = KK[:, t, :].rearrange("p (u c d) -> p u c d", c=2, d=DH)[:, :, 1, :]
                ut = UU[:, t, :].rearrange("p (u f) -> p u f", f=2 * DH)
                for i in range(2):
                    act.wait_ge(proj_ready, 2 * t + i + 1)
                    act.activation(bs(kt, i), units[:, :, :, 64:96], ACT.Copy).then_inc(raw_ready, 1)
                    act.activation(bs(ut, i), units[:, :, :, 96:160], ACT.Copy).then_inc(raw_ready, 1)
                    wait(act, pre_used, t)
                    act.activation(bs(relu_qk[:, :, :], i), units[:, :, :, 0:64], ACT.Relu).then_inc(raw_ready, 1)
                    act.activation(bs(exp_qk[:, :, :], i), units[:, :, :, 0:64], ACT.Exp).then_inc(raw_ready, 1)
                    act.activation(bs(beta[t % 2][:, :, :], i), units[:, :, :, 160:162], ACT.Exp, scale=-1.0).then_inc(raw_ready, 1)

            def rk_softmax(t):
                act.wait_ge(rk_in, t + 1)
                kt = KK[:, t, :].rearrange("p (u c d) -> p u c d", c=2, d=DH)[:, :, 1, :]
                act.activation(kt, kt, ACT.Exp).then_inc(rk_exp, 1)

            def transposed_state(t):
                act.wait_ge(hsT_ready, t + 1)
                wait(act, mixo_ready, t)
                act.activation(hsT[:, :, 0:P], ps[:, OUT_BANK, 0:2 * P].rearrange("p (c n) -> p c n", c=2), ACT.Copy)\
                   .then_inc(hsT_evac, 1)
                act.activation(hsT[:, :, P:SEQ], ps[:, OUT_BANK, 2 * P:3 * P].rearrange("p (c n) -> p c n", c=2), ACT.Copy)\
                   .then_inc(hsT_evac, 1)

            pre(0)
            rk_softmax(0)
            pre(1)
            for t in range(IMAGES):
                if t:
                    act.wait_ge(soft_in, t)
                    act.activation(QE[:, :, 1, :], QE[:, :, 1, :], ACT.Exp).then_inc(soft_exp, 1)
                if t + 1 < IMAGES:
                    rk_softmax(t + 1)
                if t:
                    act.wait_ge(u_sum, t)
                    act.activation(UU[:, t, :].rearrange("p (b r) -> p b r", b=2), ps[:, U_BANK:U_BANK + 2, 0:HALF_ROW],
                                   ACT.Copy).then_inc(u_evac, 1)
                    transposed_state(t - 1)
                if t + 2 < IMAGES:
                    pre(t + 2)
                act.wait_ge(summed, sums_before(t + 1, False))
                wait(act, hsT_ready, t - 1)
                act.activation(hs[t % 2][:, :, :], ps[:, HS_BANK, 0:HALF_ROW].rearrange("p (u d) -> p u d", d=DH), ACT.Copy)\
                   .then_inc(hs_ready, 1)
            transposed_state(IMAGES - 1)

            std(4)
            split_xT(3, xTH3)
            with act.Fori(0, 3) as c2:
                for e in range(2):
                    ch = c2 * 2 + e
                    for a in range(2):
                        act.wait_ge(fup_ready, ch * 2 + a + 1)
                        act.wait_ge(fdown_ready, c2 * 2 + 1)
                        act.activation(fhid[e][:, a, :], ps[:, 2 * e + a, :], ACT.Gelu_apprx_tanh, bias=fb1T[:, a:a + 1])\
                           .then_inc(fgelu_done, 1)

        @block.tensor
        def _(pe):
            def mm(o, lhsT, rhs, start=True, stop=True):
                return pe.matmul(o, lhsT, rhs, start=start, stop=stop)

            def tr(o, in_):
                k = in_.shape[0]
                return pe.transpose(o, in_, ident[0:k, 0:k])

            def mm_split(o, lhsT, high, low):
                mm(o, lhsT, high, stop=False)
                return mm(o, lhsT, low, start=False)

            pe.wait_ge(ident_set, 2)
            pe.wait_ge(ld_tok, 16)
            for px in range(PATCH):
                last = tr(ps[0:CHANNELS * PATCH, px // 8, D * (px % 8):D * (px % 8) + D], tokW_raw[:, px:CHANNELS * 256:PATCH])
            last.then_inc(tokw_ready, 1)
            pe.wait_ge(ld_attn, 6 * 16)
            for hd in range(HEADS):
                last = mm(ps[:, 4 + hd // 4, P * (hd % 4):P * (hd % 4) + P], Wq_raw[:, hd, :, :],
                          Wk_raw[:, :].unsqueeze(1).to_broadcast([D, 2, D]))
            last.then_inc(wt_ready, 1)
            for n in range(12):
                for half in range(2):
                    k = columns(n, half)
                    mm(ps[D * half:D * half + D, 6 + n // 8, D * (n % 8):D * (n % 8) + D], Wo_raw[:, k:k + 505:8], ident[0:D, 0:D])
            mm(ps[:, 7, 256:384], Wv_raw[:, :, :], ident[0:D, 0:D].unsqueeze(1).to_broadcast([D, 2, D]))
            pe.wait_ge(ld_slow, 7 * 16)
            for c in range(2):
                last = tr(ps[:, 7, 384 + D * c:448 + D * c], outW_raw[:, P * c:P * c + P])
            last.then_inc(wt_ready, 1)
            pe.wait_ge(tokw_evac, 2)
            for q in range(8):
                if q % 2 == 0:
                    pe.wait_ge(ld_image[q // 2], 4 * CHANNELS * 16)
                for px in range(PATCH):
                    c0 = 2 * GRID * SIDE * q + px
                    last = mm(ps[:, 2 + q // 4, D * (q % 4):D * (q % 4) + D], pixels[:, c0:c0 + 127 * PATCH + 1:PATCH],
                              tokWT[:, px, :], start=(px == 0), stop=(px == PATCH - 1))
                if q % 4 == 3:
                    last.then_inc(embed_ready, 1)
            pe.wait_ge(split_low, 2)
            tr(ps[:, 5, 0:8], b1_raw[:, :])
            tr(ps[:, 5, 8:10], fb1_raw[:, :])
            for hd in range(HEADS):
                c0 = 162 * (hd % 3)
                tr(ps[0:D, SLOW_BANKS[hd // 3], c0:c0 + 96], slowA[:, hd, :])
                last = tr(ps[0:D, SLOW_BANKS[hd // 3], c0 + 96:c0 + 162], slowB[:, hd, :])
            last.then_inc(wt2_ready, 1)
            pe.wait_ge(wt_evac, 3)
            pe.wait_ge(wt2_evac, 5)

            def transpose_x(k, src, rows_):
                pe.wait_ge(norm_ready, k + 1)
                for t in range(TILES):
                    last = tr(ps[0:rows_, t // 4, P * (t % 4):P * (t % 4) + P], src[:, t])
                    if t % 4 == 3:
                        last.then_inc(tr_ready, 1)

            transpose_x(0, xn, P)
            pe.wait_ge(tr_evac_v, 6)

            def queries(b, e):
                high, low = (x_[:, bass.ds(b * SEQ, SEQ)].rearrange("c (u r) -> c r u", r=3) for x_ in (xTH, xTL))
                for i in range(PAIRS):
                    wait(pe, qp_evac, b * 4 + (i - 1))
                    mm_split(ps[:, i % 2, 0:SEQ], Nh[:, 2 * i, :], high, low)
                    mm_split(ps[:, i % 2, SEQ:SEQ + P], Nh[:, 2 * i + 1, :], high[:, 1:3, :], low[:, 1:3, :])
                    mm_split(ps[:, i % 2, SEQ + P:2 * SEQ], Nh[:, 2 * i + 1, :], high[:, 0:1, :], low[:, 0:1, :]).then_inc(qp_ready, 1)

            def scores(b, e):
                high, low = (x_[:, bass.ds(b * SEQ, SEQ)].rearrange("c (o j) -> c j o", j=3) for x_ in (xTH, xTL))
                for m in range(6):
                    pe.wait_ge(qp_evac, b * 4 + ((2 * m + 1) // 3 + 1))
                    wait(pe, exp_done, b * 12 + (2 * m - 4))
                    for s in range(2):
                        last = mm_split(ps[:, 2 + m % 3, SEQ * s:SEQ * s + SEQ], Qs[e][:, 2 * m + s, :, :], high, low)
                    last.then_inc(score_ready, 1)

            def values(b):
                wait(pe, v_evac, b * 3)
                mm_split(ps[:, 5, 0:SEQ], WvT[:, :], xTH[:, bass.ds(b * SEQ, SEQ)], xTL[:, bass.ds(b * SEQ, SEQ)]).then_inc(v_ready, 1)

            def mix(b, e):
                pe.wait_ge(g_evac, b * 2 + 2)
                pe.wait_ge(v_evac, b * 3 + 3)
                wait(pe, mix_used, b * 2)
                mm(ps[:, 7, 0:SEQ], Vlo[e][:, :, :], Glo[e][:, :, :], stop=False)
                mm(ps[:, 7, 0:SEQ], Vhi[e][:, :, :], Ghi[e][:, :, :], start=False).then_inc(mix_ready, 1)

            def weigh(b, e):
                wait(pe, g_evac, b * 2)
                pe.wait_ge(wos_ready, b + 1)
                for j in range(3):
                    for m_, c0, c1 in ((P, 0, P), (D, P, SEQ)):
                        for i in range(PAIRS):
                            o = ps[0:m_, 6, (SEQ if c0 else 0) + D * j:(SEQ if c0 else 0) + D * j + D]
                            n = 3 * i + (2 * i - j) % 3
                            last = mm(o, probs[e][:, n, c0:c1], WoS[e][:, n, :], start=(i == 0),
                                      stop=(i == PAIRS - 1))
                last.then_inc(g_ready, 1)

            def attention_step(s, e, q):
                if in_range(s + 1):
                    queries(s + 1, 1 - e)
                if in_range(s):
                    scores(s, e)
                if in_range(s - 1):
                    values(s - 1)
                if in_range(s - 2):
                    mix(s - 2, e)
                if in_range(s - 1):
                    weigh(s - 1, 1 - e)

            queries(0, 0)
            attention_loop(pe, attention_step)

            transpose_x(1, xn, P)
            pe.wait_ge(tr_evac_v, 12)
            pe.wait_ge(split_low, 5)
            for t in range(TILES):
                o, wg = ps[:, 0, 8 * t:8 * t + 8], fsplit[:, FWG:FWG + EXPERTS]
                mm(o, xTH[:, P * t:P * t + P], wg, stop=False)
                last = mm(o, xTL[:, P * t:P * t + P], wg, start=False)
            last.then_inc(gate_ready, 1)
            pe.wait_ge(mask_ready, 1)
            for c in range(3):
                tr(ps[0:D, 1, P * c:P * c + P], mask[:, 8 * c:8 * c + 8, :]).then_inc(maskT_ready, 1)
            pe.wait_ge(b2_set, 3)
            for c in range(3):
                pe.wait_ge(maskT_evac, c + 1)
                mm(ps[:, 2 + c, :], maskT[:, c, :], b2blk[:, :, :]).then_inc(bias_ready, 1)
            pe.wait_ge(bias_used, 3)

            def up(ch, e):
                mm_split(ps[:, e % 2, :], W1s[:, e, :], xTH[:, bass.ds(ch * 512, 512)], xTL[:, bass.ds(ch * 512, 512)])\
                    .then_inc(up_ready, 1)

            def down(ch, e):
                pe.wait_ge(gelu_done, ch * 8 + (e + 1))
                if e == 0:
                    pe.wait_ge(y_used, ch * 4 + 1)
                for s in range(4):
                    last = mm(ps[:, 2 + s, D * e:D * e + D], hid[e % 4][:, P * s:P * s + P], W2_sb[:, e, :])
                last.then_inc(down_done, 1)

            def experts(ch, more):
                for e in range(EXPERTS):
                    down(ch, e)
                    if e + 2 < EXPERTS:
                        up(ch, e + 2)
                    elif more:
                        up(ch + 1, e + 2 - EXPERTS)

            pe.sem_inc(down_done, 1)
            up(0, 0)
            up(0, 1)
            with pe.Fori(0, 5) as ch:
                experts(ch, True)
            experts(5, False)

            transpose_x(2, o_tok, D)
            pe.wait_ge(tr_evac_a, 12 + 3)
            pe.wait_ge(tr_evac_v, 12 + 3)

            def project(t):
                wait(pe, raw_ready, 10 * t)
                here, there = xT[:, SEQ * t:SEQ * t + P], xT[:, SEQ * t + P:SEQ * t + SEQ]
                for b in range(2):
                    last = mm(ps[:, b, 0:3 * FEATURES], here, slowT[:, 3 * b:3 * b + 3, :])
                last.then_inc(proj_ready, 1)
                pe.wait_ge(raw_ready, 10 * t + 5)
                mm(ps[:, 0, 0:2 * FEATURES], here, slowT[:, 6:8, :])
                for half in range(2):
                    rows_, hd = slice(D * half, D * half + D), 4 * half
                    mm(ps[rows_, 0, 2 * FEATURES:3 * FEATURES], there, slowT[:, hd, :])
                    last = mm(ps[rows_, 1, 0:3 * FEATURES], there, slowT[:, hd + 1:hd + 4, :])
                last.then_inc(proj_ready, 1)

            def sum_update(t):
                wait(pe, u_evac, t - 1)
                for c in range(sum_chunks(t)):
                    m = sums_before(t, False) + c
                    pe.wait_ge(prod_ready, m + 1)
                    for i in range(min(2, t - 2 * c)):
                        for half in range(2):
                            last = mm(ps[:, U_BANK + half, 0:HALF_ROW], ident[:, :],
                                      SUM_ROWS[m % 3][:, i, HALF_ROW * half:HALF_ROW * half + HALF_ROW],
                                      start=(c == 0 and i == 0), stop=False)
                    last.then_inc(summed, 1)
                for half in range(2):
                    last = mm(ps[:, U_BANK + half, 0:HALF_ROW], ident[:, :],
                              UU[:, t, HALF_ROW * half:HALF_ROW * half + HALF_ROW], start=False)
                last.then_inc(u_sum, 1)

            def sum_reading(t):
                wait(pe, hs_ready, t)
                for c in range(sum_chunks(t + 1)):
                    m = sums_before(t, True) + c
                    pe.wait_ge(prod_ready, m + 1)
                    n = min(2, t + 1 - 2 * c)
                    for i in range(n):
                        row = SUM_ROWS[m % 3][:, i, :].rearrange("p (u c d) -> p c u d", c=2, d=DH)
                        for memory in range(2):
                            last = mm(ps[:, HS_BANK, 0:HALF_ROW], ident[:, :], row[:, memory, :, :],
                                      start=(c == 0 and i == 0 and memory == 0), stop=(2 * c + i == t and memory == 1))
                    last.then_inc(summed, 1)

            def output_rows(t):
                pe.wait_ge(hs_ready, t + 1)
                wait(pe, mixo_used, 2 * t)
                for c in range(3):
                    last = tr(ps[:, OUT_BANK, P * c:P * c + P], hs[t % 2][:, 4 * c:4 * c + 4, :])
                last.then_inc(hsT_ready, 1)
                pe.wait_ge(hsT_evac, 2 * t + 2)
                o = ps[:, OUT_BANK, 3 * P:4 * P]
                if t % 2 == 0:
                    parts = ((o[:, 0:D], 0, P), (o[0:D, D:2 * D], P, SEQ))
                else:
                    parts = ((o[D:P, 0:D], 0, D), (o[:, D:2 * D], D, SEQ))
                for o_, c0, c1 in parts:
                    for c in range(2):
                        last = mm(o_, hsT[:, c, c0:c1], WoutT[:, c, :], start=(c == 0), stop=(c == 1))
                last.then_inc(mixo_ready, 1)

            project(0)
            project(1)
            for t in range(IMAGES):
                if t:
                    sum_update(t)
                    output_rows(t - 1)
                if t + 2 < IMAGES:
                    project(t + 2)
                sum_reading(t)
            output_rows(IMAGES - 1)

            transpose_x(3, xn, P)
            pe.wait_ge(tr_evac_v, 15 + 6)
            pe.wait_ge(ld_ffn, 16)
            for c in range(6):
                mm_split(ps[:, c, :], fsplit[:, FWR:FWR + P], xTH3[:, 512 * c:512 * c + 512], xTL3[:, 512 * c:512 * c + 512])\
                    .then_inc(wcol_ready, 1)
            pe.wait_ge(rank_vec, 6)
            pe.sem_inc(fdown_ready, 1)

            def fup(ch, e):
                for a in range(2):
                    mm_split(ps[:, 2 * e + a, :], fsplit[:, FW1 + P * a:FW1 + P * a + P], xTH3[:, bass.ds(ch * 512, 512)],
                             xTL3[:, bass.ds(ch * 512, 512)]).then_inc(fup_ready, 1)

            def fdown(ch, e, c2):
                pe.wait_ge(fgelu_done, ch * 2 + 2)
                pe.wait_ge(fy_free, c2 * 2 + 1)
                for s in range(4):
                    for a in range(2):
                        last = mm(ps[:, 4 + e, D * s:D * s + D], fhid[e][:, a, P * s:P * s + P], w2_sb[:, a, :],
                                  start=(a == 0), stop=(a == 1))
                last.then_inc(fdown_ready, 1)

            fup(0, 0)
            with pe.Fori(0, 2) as c2:
                for e in range(2):
                    fup(c2 * 2 + (e + 1), 1 - e)
                    fdown(c2 * 2 + e, e, c2)
            fup(5, 1)
            fdown(4, 0, 2)
            fdown(5, 1, 2)

        @block.vector
        def _(dve):
            st = Steps(dve, vec)

            dve.wait_ge(ld_moe, 9 * 16)
            dve.tensor_copy(fraw[:, FWR:FWR + P], wr_raw[:, :].to_broadcast([P, P])).then_inc(wr_set, 1)
            lo = slice(D, P)
            dve.wait_ge(split_high, 2)
            for c in range(2):
                dve.scalar_tensor_tensor(out=Nh[lo, 4 * c:4 * c + 4, :].rearrange("p h c -> p (h c)"), in0=ps[lo, 4 + c, :],
                                         scalar=SCALE, in1=f32(Nh[lo, 4 * c:4 * c + 4, :].rearrange("p h c -> p (h c)")),
                                         op0=ALU.mult, op1=ALU.subtract).then_inc(split_low, 1)
            dve.wait_ge(split_high, 3)
            dve.wait_ge(wt_evac, 3)
            dve.tensor_tensor(WvT[lo, :], ps[lo, 7, 256:384], f32(WvT[lo, :]), ALU.subtract).then_inc(split_low, 1)
            dve.wait_ge(split_high, 5)
            dve.tensor_tensor(W1s[lo, :, :], W1_raw[lo, :, :], f32(W1s[lo, :, :]), ALU.subtract).then_inc(split_low, 1)
            dve.tensor_tensor(fsplit[lo, :], fraw[lo, :], f32(fsplit[lo, :]), ALU.subtract).then_inc(split_low, 1)
            dve.wait_ge(ld_bias, 6 * 16)
            hv = h[:, :, :].rearrange("p (q r) d -> p q r d", r=3)
            for c in range(2):
                dve.wait_ge(embed_ready, c + 1)
                for half in range(2):
                    s = slice(D * half, D * half + D)
                    st.then(dve.tensor_tensor(hv[s, 4 * c:4 * c + 4, half, :], ps[s, 2 + c, 0:256].rearrange("p (q d) -> p q d", d=D),
                                              tokb_sb[s, :].unsqueeze(1).to_broadcast([D, 4, D]), ALU.add))
            dve.wait_ge(ld_text, 3 * 16)

            def spread(a):
                return a.unsqueeze(2).to_broadcast([P, TILES, D])

            def layer_norm(k, src, dst, cen, sq):
                st.then(dve.tensor_reduce(stat[:, 0, :], src, axis=AXL.X, op=ALU.add))
                st.then(dve.tensor_scalar(stat[:, 0, :], stat[:, 0, :], 1.0 / D, None, ALU.mult))
                st.then(dve.tensor_tensor(cen, src, spread(stat[:, 0, :]), ALU.subtract))
                st.then(dve.tensor_tensor(sq, cen, cen, ALU.mult))
                st.then(dve.tensor_reduce(stat[:, 1, :], sq, axis=AXL.X, op=ALU.add))
                dve.tensor_scalar(stat[:, 1, :], stat[:, 1, :], 1.0 / D, EPS, ALU.mult, ALU.add).then_inc(var_ready, 1)
                dve.wait_ge(std_ready, k + 1)
                st.then(dve.reciprocal(stat[:, 0, :], stat[:, 1, :]))
                scale = spread(stat[:, 0, :])
                for i in range(2 if len(dst.shape) == 4 else 1):
                    st.then(dve.tensor_tensor(dst[:, :, i, :] if len(dst.shape) == 4 else dst, cen, scale, ALU.mult))

            def split_xT(k, seen, high, low):
                for c in range(6):
                    dve.wait_ge(tr_evac_a, seen + c + 1)
                    dve.tensor_tensor(low[:, 512 * c:512 * c + 512], ps[:, c, :], f32(high[:, 512 * c:512 * c + 512]),
                                      ALU.subtract).then_inc(tr_evac_v, 1)

            layer_norm(0, h[:, :, :], xn[:, :, :, :], cen, sq)
            dve.sem_inc(norm_ready, 1)
            split_xT(0, 0, xTH, xTL)

            def q_halves(b, e):
                for i in range(PAIRS):
                    dve.wait_ge(q_high, b * 4 + (i + 1))
                    to = Qs[e][lo, 3 * i:3 * i + 3, :, :].rearrange("p r h u -> p h r u")
                    dve.tensor_tensor(to, ps[lo, i % 2, 0:2 * SEQ].rearrange("p (h r u) -> p h r u", h=2, r=3), f32(to),
                                      ALU.subtract).then_inc(qp_evac, 1)

            def maxima(b, e):
                wait(dve, exp_done, b * 12 - 12)
                for m in range(6):
                    dve.wait_ge(score_ready, b * 6 + m + 1)
                    dve.tensor_reduce(negmax[e][:, 2 * m:2 * m + 2],
                                      ps[:, 2 + m % 3, 0:2 * SEQ].rearrange("p (h s) -> p h s", h=2), axis=AXL.X,
                                      op=ALU.max, negate=True).then_inc(max_ready, 1)

            def evacuate_v(b, e):
                dve.wait_ge(v_ready, b + 1)
                wait(dve, mix_ready, b - 1)
                for dst, p0, c in ((Vlo[e][0:D, :, :], 0, 0), (Vlo[e][D:P, :, :], D, 1), (Vhi[e][:, :, :], 0, 2)):
                    dve.tensor_copy(dst, ps[p0:p0 + D, 5, D * c:D * c + D].unsqueeze(1).to_broadcast([D, 2, D])).then_inc(v_evac, 1)

            def scale_weights(b, e):
                dve.wait_ge(exp_done, b * 12 + 12)
                wait(dve, wos_ready, b)
                dve.reciprocal(rinv[:, :], rowsum[e][:, :]).then_inc(rinv_set, 1)
                dve.wait_ge(rinv_set, b + 1)
                wait(dve, g_ready, b - 1)
                dve.tensor_tensor(WoS[e][:, :, :], WoT[:, :, :], rinv[:, :].unsqueeze(2).to_broadcast([P, 12, D]), ALU.mult)\
                   .then_inc(wos_ready, 1)

            def residual(b, q, e):
                dve.wait_ge(mix_ready, b + 1)
                own, other = slice(D * e, D * e + D), slice(D - D * e, P - D * e)
                o = ps[:, 7, 0:SEQ].rearrange("p (j d) -> p j d", j=3)
                a = h[own, bass.ds(q * 3 + e, 2), :]
                dve.tensor_tensor(a, a, o[own, 0:3:2, :], ALU.add).then_inc(mix_used, 1)
                a = h[other, bass.ds(q * 3 + 2 * e, 1), :]
                dve.tensor_tensor(a, a, o[other, 1:2, :], ALU.add).then_inc(mix_used, 1)

            def attention_step(s, e, q):
                if in_range(s + 1):
                    q_halves(s + 1, 1 - e)
                if in_range(s):
                    maxima(s, e)
                if in_range(s - 2):
                    residual(s - 2, q - 1, e)
                if in_range(s - 1):
                    scale_weights(s - 1, 1 - e)
                    evacuate_v(s - 1, 1 - e)

            q_halves(0, 0)
            attention_loop(dve, attention_step)
            dve.wait_ge(mix_used, 2 * IMAGES)

            layer_norm(1, h[:, :, :], xn[:, :, :, :], cen, sq)
            dve.sem_inc(norm_ready, 1)
            split_xT(1, 6, xTH, xTL)
            dve.wait_ge(gate_ready, 1)
            st.then(dve.tensor_tensor(gate[:, :, :], ps[:, 0, 0:TILES * 8].rearrange("p (t e) -> p t e", e=EXPERTS),
                                      bg_sb[:, :].unsqueeze(1).to_broadcast([P, TILES, EXPERTS]), ALU.add))
            st.then(dve.memset(beats, 0.0))
            for a in range(EXPERTS):
                if a:
                    dve.tensor_tensor(beats[:, :, a, 0:a], gate[:, :, 0:a],
                                      gate[:, :, a:a + 1].to_broadcast([P, TILES, a]), ALU.is_ge).then_inc(vec, 1)
                    st.n += 1
                if a < EXPERTS - 1:
                    dve.tensor_tensor(beats[:, :, a, a + 1:], gate[:, :, a + 1:],
                                      gate[:, :, a:a + 1].to_broadcast([P, TILES, EXPERTS - 1 - a]), ALU.is_gt).then_inc(vec, 1)
                    st.n += 1
            dve.wait_ge(vec, st.n)
            st.then(dve.tensor_reduce(mask[:, :, :], beats, axis=AXL.X, op=ALU.add))
            dve.tensor_scalar(mask[:, :, :], mask[:, :, :], 2.0, None, ALU.is_lt).then_inc(mask_ready, 1)
            dve.wait_ge(mask_ready, 1)
            for c in range(3):
                dve.wait_ge(bias_ready, c + 1)
                a = h[:, 8 * c:8 * c + 8, :]
                dve.tensor_tensor(a, a, ps[:, 2 + c, :].rearrange("p (t d) -> p t d", d=D), ALU.add).then_inc(bias_used, 1)
            dve.wait_ge(bias_used, 3)
            dve.sem_inc(y_used, 1)
            dve.sem_inc(y_vec, 1)
            ys = Steps(dve, y_vec)
            with dve.Fori(0, 6) as ch:
                ys.base, ys.n = ch * 8 + 1, 0
                dve.wait_ge(down_done, ch * 8 + 9)
                for s in range(4):
                    m = mask[:, bass.ds(ch * 4 + s, 1), :].rearrange("p a e -> p (a e)").unsqueeze(2).to_broadcast([P, EXPERTS, D])
                    dve.tensor_tensor(ysel[s % 2], ps[:, 2 + s, :].rearrange("p (e d) -> p e d", e=EXPERTS), m, ALU.mult)\
                       .then_inc(y_used, 1)
                    dve.wait_ge(y_used, ch * 4 + (s + 2))
                    ys.then(dve.tensor_reduce(ysum, ysel[s % 2].rearrange("p e d -> p d e"), axis=AXL.X, op=ALU.add))
                    a = h[:, bass.ds(ch * 4 + s, 1), :]
                    ys.then(dve.tensor_tensor(a, a, ysum.unsqueeze(1), ALU.add))

            x1 = xn[:, :, 0, :]
            scratch = UU.rearrange("p t r -> p (t r)")
            cen2, sq2 = (scratch[:, 1536 * i:1536 * i + 1536].rearrange("p (t d) -> p t d", d=D) for i in range(2))
            layer_norm(2, h[:, :, :], x1, cen2, sq2)
            layer_norm(3, x1, o_tok, cen2, sq2)
            st.then(dve.tensor_tensor(o_tok, o_tok, g_sb[:, :].unsqueeze(1).to_broadcast([P, TILES, D]), ALU.mult))
            st.then(dve.tensor_tensor(o_tok, o_tok, b_sb[:, :].unsqueeze(1).to_broadcast([P, TILES, D]), ALU.add))
            dve.sem_inc(norm_ready, 1)
            st.then(dve.tensor_tensor(h[:, :, :], h[:, :, :], x1, ALU.add))
            for c in range(1, 6, 2):
                dve.wait_ge(tr_ready, 12 + c + 1)
                dve.tensor_copy(xT[:, 512 * c:512 * c + 512], ps[0:D, c, :]).then_inc(tr_evac_v, 1)
            dve.wait_ge(tr_evac_v, 12 + 3)
            st.then(dve.memset(QE[:, :, :, :], 1.0))

            def over_time(a, n):
                return a.unsqueeze(1).to_broadcast([P, n, a.shape[1]])

            def over_width(a):
                return a.unsqueeze(3).to_broadcast([P, a.shape[1], BOTH, DH])

            def keys_in(t):
                dve.wait_ge(raw_ready, 10 * t + 6)
                kt = KK[:, t, :].rearrange("p (u c d) -> p u c d", c=2, d=DH)
                ut = UU[:, t, :].rearrange("p (r d) -> p r d", d=DH)
                rk, bt = kt[:, :, 1, :], beta[t % 2]
                st.then(dve.tensor_reduce(rk_top[:, :], rk, axis=AXL.X, op=ALU.max))
                dve.tensor_tensor(rk, rk, rk_top[:, :].unsqueeze(2).to_broadcast([P, UNITS, DH]), ALU.subtract).then_inc(rk_in, 1)
                dve.wait_ge(raw_ready, 10 * t + 10)
                st.then(dve.tensor_scalar(bt[:, :, :], bt[:, :, :], 1.0, None, ALU.add))
                st.then(dve.reciprocal(bt[:, :, :], bt[:, :, :]))
                st.then(dve.tensor_tensor(ut, ut, bt[:, :, :].rearrange("p u c -> p (u c)").unsqueeze(2)
                                          .to_broadcast([P, BOTH, DH]), ALU.mult))
                st.then(dve.scalar_tensor_tensor(out=kt[:, :, 0, :], in0=exp_qk[:, :, DH:2 * DH], scalar=1.0,
                                                 in1=relu_qk[:, :, DH:2 * DH], op0=ALU.min, op1=ALU.add))

            def query(t):
                st.then(dve.scalar_tensor_tensor(out=QE[:, :, 0, :], in0=exp_qk[:, :, 0:DH], scalar=1.0,
                                                 in1=relu_qk[:, :, 0:DH], op0=ALU.min, op1=ALU.add))
                dve.sem_inc(pre_used, 1)

            def keys(t):
                dve.wait_ge(rk_exp, t + 1)
                kt = KK[:, t, :].rearrange("p (r d) -> p r d", d=DH)
                st.then(dve.tensor_reduce(ksum[:, :], kt, axis=AXL.X, op=ALU.add))
                st.then(dve.reciprocal(ksum[:, :], ksum[:, :]))
                dve.tensor_tensor(kt, kt, ksum[:, :].unsqueeze(2).to_broadcast([P, BOTH, DH]), ALU.mult).then_inc(keys_ready, 1)
                dve.wait_ge(keys_ready, t + 1)

            def by_width(a):
                return a.rearrange("p t (r d) -> p t r d", d=DH)

            def gram_sums(t, c):
                m, n = grams_before(t) + c, min(3, t - 3 * c)
                dve.wait_ge(gram_prod, m + 1)
                dve.tensor_reduce(gram[:, 3 * c:3 * c + n, :], by_width(GRAM_ROWS[m % 2][:, 0:n, :]), axis=AXL.X, op=ALU.add)\
                   .then_inc(gram_used, 1)

            def scale_gram(t):
                dve.wait_ge(gram_used, grams_before(t + 1))
                gt = gram[:, 0:t, :]
                st.then(dve.scalar_tensor_tensor(out=gt, in0=gt, scalar=-1.0,
                                                 in1=over_time(beta[t % 2][:, :, :].rearrange("p u c -> p (u c)"), t),
                                                 op0=ALU.mult, op1=ALU.mult))

            def weigh_values(m, first, n, weights):
                wait(dve, summed, m - 2)
                dve.tensor_tensor(by_width(SUM_ROWS[m % 3][:, 0:n, :]), by_width(UU[:, first:first + n, :]),
                                  over_width(weights[:, first:first + n, :]), ALU.mult).then_inc(prod_ready, 1)

            def coef_sums(t, c):
                n = min(4, t + 1 - 4 * c)
                st.then(dve.tensor_tensor(COEF_ROWS[:, 0:n, :], KK[:, 4 * c:4 * c + n, :],
                                          over_time(QE[:, :, :, :].rearrange("p u c d -> p (u c d)"), n), ALU.mult))
                st.then(dve.tensor_reduce(coef[:, 4 * c:4 * c + n, :], by_width(COEF_ROWS[:, 0:n, :]), axis=AXL.X, op=ALU.add))

            def soft(t):
                dve.wait_ge(hs_ready, t + 1)
                st.then(dve.tensor_reduce(top[:, :], hs[t % 2][:, :, :], axis=AXL.X, op=ALU.max))
                dve.tensor_tensor(QE[:, :, 1, :], hs[t % 2][:, :, :], top[:, :].unsqueeze(2).to_broadcast([P, UNITS, DH]),
                                  ALU.subtract).then_inc(soft_in, 1)

            def add_out(t):
                dve.wait_ge(mixo_ready, t + 1)
                q, e = t // 2, t % 2
                if e == 0:
                    parts = ((slice(0, P), 3 * q, 0), (slice(0, D), 3 * q + 1, D))
                else:
                    parts = ((slice(D, P), 3 * q + 1, 0), (slice(0, P), 3 * q + 2, D))
                for s, tile, c in parts:
                    dve.tensor_tensor(h[s, tile, :], h[s, tile, :], ps[s, OUT_BANK, 3 * P + c:3 * P + c + D], ALU.add)\
                       .then_inc(mixo_used, 1)

            keys_in(0)
            query(0)
            keys(0)
            def update_chunk(t, c):
                if c < sum_chunks(t):
                    weigh_values(sums_before(t, False) + c, 2 * c, min(2, t - 2 * c), gram)

            for t in range(IMAGES):
                more = t + 1 < IMAGES
                update_chunk(t, 0)
                update_chunk(t, 1)
                if t:
                    soft(t - 1)
                if more:
                    keys_in(t + 1)
                update_chunk(t, 2)
                if t:
                    dve.wait_ge(soft_exp, t)
                st.then(dve.tensor_reduce(qsum[:, :], QE[:, :, :, :].rearrange("p u c d -> p (u c) d"), axis=AXL.X, op=ALU.add))
                st.then(dve.reciprocal(qsum[:, :], qsum[:, :]))
                if more:
                    keys(t + 1)
                for c in range((t + 4) // 4):
                    coef_sums(t, c)
                    update_chunk(t, 2 * c + 3)
                    update_chunk(t, 2 * c + 4)
                if more:
                    query(t + 1)
                ct = coef[:, 0:t + 1, :]
                st.then(dve.tensor_tensor(ct, ct, over_time(qsum[:, :], t + 1), ALU.mult))
                for c in range(sum_chunks(t + 1)):
                    if 2 * c + 2 > t:
                        wait(dve, u_evac, t)
                    weigh_values(sums_before(t, True) + c, 2 * c, min(2, t + 1 - 2 * c), coef)
                    if more and c < gram_chunks(t + 1):
                        gram_sums(t + 1, c)
                if more:
                    for c in range(sum_chunks(t + 1), gram_chunks(t + 1)):
                        gram_sums(t + 1, c)
                    scale_gram(t + 1)
                if t:
                    add_out(t - 1)
            add_out(IMAGES - 1)
            dve.wait_ge(mixo_used, 2 * IMAGES)

            layer_norm(4, h[:, :, :], xn[:, :, :, :], cen3, sq3)
            dve.sem_inc(norm_ready, 1)
            st.then(dve.tensor_tensor(h[:, :, :], h[:, :, :], x1, ALU.add))
            split_xT(3, 15, xTH3, xTL3)
            for c in range(6):
                dve.wait_ge(wcol_ready, c + 1)
                dve.tensor_scalar(wcols[:, 512 * c:512 * c + 512], ps[:, c, :], br_sb[:, 0:1], None, ALU.add).then_inc(rank_vec, 1)
            dve.wait_ge(rank_vec, 6)
            dve.wait_ge(masks_set, 5)
            st.then(dve.tensor_tensor(wdiag, wcols.rearrange("p (t j) -> p t j", j=P),
                                      ident[:, :].unsqueeze(1).to_broadcast([P, TILES, P]), ALU.mult))
            st.then(dve.tensor_reduce(wtok[:, :], wdiag, axis=AXL.X, op=ALU.add))
            rv = Steps(dve, rank_vec)
            with dve.Fori(0, IMAGES // 2) as q:
                rv.base, rv.n = q * 8 + 6, 0
                for s, r, e, k in ((slice(0, P), 0, 0, 0), (slice(0, D), 1, 0, 1), (slice(D, P), 1, 1, 1), (slice(0, P), 2, 1, 2)):
                    cols = wcols[s, bass.ds(q * 384 + SEQ * e, SEQ)]
                    own = wtok[s, bass.ds(q * 3 + r, 1)]
                    rv.then(dve.scalar_tensor_tensor(out=tie[s, :], in0=cols, scalar=own, in1=earlier[s, k, :],
                                                     op0=ALU.is_equal, op1=ALU.mult))
                    rv.then(dve.scalar_tensor_tensor(out=over[s, :], in0=cols, scalar=own, in1=tie[s, :],
                                                     op0=ALU.is_gt, op1=ALU.add, accum_out=rank[s, bass.ds(q * 3 + r, 1)]))
            st.then(dve.scalar_tensor_tensor(out=wkeep[:, :], in0=rank[:, :], scalar=float(KEPT), in1=wtok[:, :],
                                             op0=ALU.is_lt, op1=ALU.mult))
            dve.sem_inc(fy_free, 1)
            dve.sem_inc(fy_vec, 1)
            fs = Steps(dve, fy_vec)
            with dve.Fori(0, 3) as c2:
                fs.base, fs.n = c2 * 4 + 1, 0
                for e in range(2):
                    ch = c2 * 2 + e
                    dve.wait_ge(fdown_ready, ch + 2)
                    fs.then(dve.tensor_tensor(fy, ps[:, 4 + e, 0:4 * D].rearrange("p (s d) -> p s d", d=D),
                                              fb2_sb[:, :].unsqueeze(1).to_broadcast([P, 4, D]), ALU.add))
                    dve.sem_inc(fy_free, 1)
                    fs.then(dve.tensor_tensor(fy, fy, wkeep[:, bass.ds(ch * 4, 4)].unsqueeze(2).to_broadcast([P, 4, D]), ALU.mult))
                    a = h[:, bass.ds(ch * 4, 4), :]
                    dve.tensor_tensor(a, a, fy, ALU.add).then_inc(out_ready, 1)
                    dve.wait_ge(out_ready, ch + 1)


_INS = ['x', 'txt', 'L0_tok_W', 'L0_tok_b', 'L0_attn_Wq', 'L0_attn_Wk', 'L0_attn_Wv', 'L0_attn_Wo', 'L0_ffn_Wg',
        'L0_ffn_bg', 'L0_ffn_W1', 'L0_ffn_b1', 'L0_ffn_W2', 'L0_ffn_b2', 'L1_attn_slow_W', 'L1_attn_out_W',
        'L1_attn_ln_g', 'L1_attn_ln_b', 'L1_ffn_wr', 'L1_ffn_br', 'L1_ffn_w1', 'L1_ffn_b1', 'L1_ffn_w2', 'L1_ffn_b2']


def kernel(**inputs):
    import numpy as _np
    import concourse.bacc as _bacc
    from concourse import mybir as _mybir
    from concourse.bass_utils import run_bass_kernel_spmd as _run

    nc = _bacc.Bacc("TRN2", target_bir_lowering=False, num_devices=1)
    arrays, args = {}, []
    for name in _INS:
        a = _np.ascontiguousarray(inputs[name])
        arrays[f"in_{name}_dram"] = a
        args.append(nc.dram_tensor(f"in_{name}_dram", a.shape, _mybir.dt.from_np(a.dtype), kind="ExternalInput").ap())
    result = nc.dram_tensor("out_0_dram", (IMAGES, SEQ, D), F32, kind="ExternalOutput").ap()
    token_mixer_kernel(nc, *args, result)
    r = _run(nc, [arrays], core_ids=[0])
    return r.results[0]["out_0_dram"]
```

```python
import concourse.bass as bass
from concourse import mybir
from contextlib import ExitStack

F32 = mybir.dt.float32
F32R = mybir.dt.float32r
ALU = mybir.AluOpType
ACT = mybir.ActivationFunctionType
AXL = mybir.AxisListType

IMAGES, CHANNELS, SIDE, PATCH = 16, 3, 128, 16
GRID = SIDE // PATCH
D = 64
SEQ = GRID * GRID + 128
P = 128
TILES = IMAGES * SEQ // P
HEADS = 8
PAIRS = HEADS // 2
EXPERTS, HIDDEN = 8, 128
DH = 32
UNITS = 12
BOTH = 2 * UNITS
ROW = BOTH * DH
FFN_HIDDEN = 256
KEPT = SEQ // 2 - 1
EPS = 1e-5


def token_mixer_kernel(nc, x, txt, tok_W, tok_b, Wq, Wk, Wv, Wo, Wg, bg, W1, b1, W2, b2, slow_W, out_W,
                       ln_g, ln_b, wr, br, w1, fb1, w2, fb2, out):
    ctx = ExitStack()
    with ctx:
        ps = ctx.enter_context(nc.psum_tensor("ps", [P, 8, 512], F32))

        class Place:
            def __init__(self):
                self.stack = ExitStack()

            def __call__(self, name, shape, dtype=F32):
                return self.stack.enter_context(nc.sbuf_tensor(name, shape, dtype))

        sb = Place()
        ctx.enter_context(sb.stack)
        h = sb("h", [P, TILES, D])
        xn = sb("xn", [P, TILES, 2, D])
        ident = sb("ident", [P, P])
        stat = sb("stat", [P, 2, TILES])
        slowT = sb("slowT", [D, HEADS, 162])
        WoutT = sb("WoutT", [P, 2, D])
        b1T = sb("b1T", [P, EXPERTS])
        fb1T = sb("fb1T", [P, 2])
        bg_sb = sb("bg_sb", [P, EXPERTS])
        tokb_sb = sb("tokb_sb", [P, D])
        g_sb = sb("g_sb", [P, D])
        b_sb = sb("b_sb", [P, D])
        br_sb = sb("br_sb", [P, 1])
        w2_sb = sb("w2_sb", [P, 2, D])
        fb2_sb = sb("fb2_sb", [P, D])
        FW1, FWR, FWG = 0, FFN_HIDDEN, FFN_HIDDEN + P
        fsplit = sb("fsplit", [P, FFN_HIDDEN + P + EXPERTS], F32R)

        early = Place()
        xTH = early("xTH", [P, TILES * P], F32R)
        xTL = early("xTL", [P, TILES * P], F32R)
        Nh = early("Nh", [P, HEADS, P], F32R)
        WvT = early("WvT", [P, P], F32R)
        W1s = early("W1s", [P, EXPERTS, HIDDEN], F32R)
        W1_raw = early("W1_raw", [P, EXPERTS, HIDDEN])
        fraw = early("fraw", [P, FFN_HIDDEN + P + EXPERTS])
        wr_raw = early("wr_raw", [P, 1])
        W2_sb = early("W2_sb", [HIDDEN, EXPERTS, 2, D])
        pick = early("pick", [P, EXPERTS, P], F32R)
        WoT = early("WoT", [P, 12, D])
        b2_rows = early("b2_rows", [P, 2, D])
        Wq_raw = early("Wq_raw", [D, HEADS, 2, D])
        Wk_raw = early("Wk_raw", [D, D])
        Wv_raw = early("Wv_raw", [D, 2, D])
        Wo_raw = early("Wo_raw", [D, HEADS * D])
        slowA = early("slowA", [96, HEADS, D])
        slowB = early("slowB", [66, HEADS, D])
        outW_raw = early("outW_raw", [D, 256])
        b1_raw = early("b1_raw", [EXPERTS, HIDDEN])
        fb1_raw = early("fb1_raw", [2, P])

        embed = Place()
        tokW_raw = embed("tokW_raw", [D, CHANNELS * PATCH * PATCH])
        tokWT = embed("tokWT", [CHANNELS * PATCH, PATCH, D])
        pixels = embed("pixels", [CHANNELS * PATCH, IMAGES * GRID * SIDE])
        cen0 = embed("cen0", [P, TILES, D])
        sq0 = embed("sq0", [P, TILES, D])
        embed.stack.close()

        attn = Place()
        cen = attn("cen", [P, TILES, D])[:, :, :]
        sq = attn("sq", [P, TILES, D])[:, :, :]
        Qs = [attn(f"Qs{i}", [P, 12, 2, D], F32R) for i in range(2)]
        probs = [attn(f"probs{i}", [P, 12, SEQ]) for i in range(2)]
        WoS = [attn(f"WoS{i}", [P, 12, D]) for i in range(2)]
        negmax = [attn(f"negmax{i}", [P, 12]) for i in range(2)]
        rowsum = [attn(f"rowsum{i}", [P, 12]) for i in range(2)]
        rinv = attn("rinv", [P, 12])
        GT01 = attn("GT01", [P, SEQ])
        GT2 = attn("GT2", [D, SEQ])
        Glo = [attn(f"Glo{i}", [P, 3, D]) for i in range(2)]
        Ghi = [attn(f"Ghi{i}", [D, 3, D]) for i in range(2)]
        Vlo = [attn(f"Vlo{i}", [P, 2, D]) for i in range(2)]
        Vhi = [attn(f"Vhi{i}", [D, 2, D]) for i in range(2)]
        attn.stack.close()

        moe = Place()
        moe("layer_norm_scratch", [P, 2, TILES, D])
        gate = moe("gate", [P, TILES, EXPERTS])
        mask = moe("mask", [P, TILES, EXPERTS])
        beats = moe("beats", [P, TILES, EXPERTS, EXPERTS])[:, :, :, :]
        hid = [moe(f"hid{i}", [P, 512])[:, :] for i in range(4)]
        yT = moe("yT", [D, 512])
        expert_mask = moe("expert_mask", [P, TILES * P], F32R)
        moe.stack.close()
        early.stack.close()

        fast = Place()
        KK = fast("keys", [P, IMAGES, ROW])[:, :, :]
        UU = fast("values", [P, IMAGES, ROW])[:, :, :]
        prod = fast("prod", [P, 18, ROW])[:, :, :]
        GRAM_ROWS = [prod[:, 3 * i:3 * i + 3, :] for i in range(2)]
        SUM_ROWS = [prod[:, 6 + 2 * i:8 + 2 * i, :] for i in range(3)]
        COEF1_ROWS = [prod[:, 12 + 2 * i:14 + 2 * i, :].rearrange("p a (b s) -> p (a b) s", b=2) for i in range(2)]
        COEF2_ROWS = prod[:, 16:18, :].rearrange("p a (b s) -> p (a b) s", b=2)
        xn_flat = xn[:, :, :, :].rearrange("p t c d -> p (t c d)")
        x1_fast = xn_flat[:, 0:TILES * D].rearrange("p (t d) -> p t d", d=D)
        OLD_ROWS = xn_flat[:, TILES * D:2 * TILES * D].rearrange("p (t r) -> p t r", r=ROW)
        gram_old = fast("gram_old", [P, 2, BOTH])
        coef_old = fast("coef_old", [P, 2, BOTH])
        o_tok = prod[:, 0:2, :].rearrange("p a r -> p (a r)").rearrange("p (t d) -> p t d", d=D)
        xT = fast("xT", [D, TILES * P])
        QE1 = [fast(f"QE1_{i}", [P, UNITS, DH]) for i in range(2)]
        QE2 = fast("QE2", [P, UNITS, DH])
        relu_qk = fast("relu_qk", [P, UNITS, 2 * DH])
        exp_qk = fast("exp_qk", [P, UNITS, 2 * DH])
        beta = [fast(f"beta{i}", [P, UNITS, 2]) for i in range(2)]
        top = fast("top", [P, UNITS])
        rk_top = fast("rk_top", [P, UNITS])
        ksum = fast("ksum", [P, BOTH])
        qsum = fast("qsum", [P, BOTH])
        hs = [fast(f"hs{i}", [P, UNITS, DH]) for i in range(2)]
        hsT = fast("hsT", [P, 2, SEQ])
        fast.stack.close()

        late = Place()
        xTH3 = late("xTH3", [P, TILES * P], F32R)
        xTL3 = late("xTL3", [P, TILES * P], F32R)
        cen3 = late("cen3", [P, TILES, D])[:, :, :]
        sq3 = late("sq3", [P, TILES, D])[:, :, :]
        wcols = late("wcols", [P, TILES * P])[:, :]
        wdiag = late("wdiag", [P, TILES, P])[:, :, :]
        earlier = late("earlier", [P, 3, SEQ])
        tie = late("tie", [P, 4, SEQ])
        over = late("over", [P, 4, SEQ])
        fhid = [late(f"fhid{i}", [P, 2, 512]) for i in range(2)]
        fy = late("fy", [P, TILES, D])
        wtok = late("wtok", [P, TILES])
        rank = late("rank", [P, TILES])
        wkeep = late("wkeep", [P, TILES])
        late.stack.close()

        def sem(name):
            return ctx.enter_context(nc.semaphore(name))

        ld_attn, ld_slow, ld_tok, ld_text, ld_b2, ld_moe, ld_ffn, ld_bias = (
            sem(n) for n in ("ld_attn", "ld_slow", "ld_tok", "ld_text", "ld_b2", "ld_moe", "ld_ffn", "ld_bias"))
        ld_image = [sem(f"ld_image{c}") for c in range(8)]
        ident_set, masks_set, b2_set = sem("ident_set"), sem("masks_set"), sem("b2_set")
        wr_set, split_high, split_low = sem("wr_set"), sem("split_high"), sem("split_low")
        tokw_ready, tokw_evac, embed_ready = sem("tokw_ready"), sem("tokw_evac"), sem("embed_ready")
        wt_ready, wt_evac, wt2_ready, wt2_evac = sem("wt_ready"), sem("wt_evac"), sem("wt2_ready"), sem("wt2_evac")
        vec = sem("vec")
        var_ready, std_ready = sem("var_ready"), sem("std_ready")
        norm_ready = sem("norm_ready")
        tr_ready, tr_evac_a, tr_evac_v = sem("tr_ready"), sem("tr_evac_a"), sem("tr_evac_v")
        qp_ready, qp_evac, score_ready, max_ready, exp_done, wos_ready, g_ready, g_evac, mix_ready, mix_used = (
            sem(n) for n in ("qp_ready", "qp_evac", "score_ready", "max_ready", "exp_done", "wos_ready", "g_ready",
                             "g_evac", "mix_ready", "mix_used"))
        gt_ready, gt_evac = sem("gt_ready"), sem("gt_evac")
        rinv_set, q_high, v_ready, v_evac = (sem(n) for n in ("rinv_set", "q_high", "v_ready", "v_evac"))
        gate_ready, mask_ready = sem("gate_ready"), sem("mask_ready")
        zero_set, pick_set, emask_ready, emask_evac = (sem(n) for n in ("zero_set", "pick_set", "emask_ready", "emask_evac"))
        up_ready, gelu_done, spread_ready, masked, down_done, yT_evac, y_ready, y_used = (
            sem(n) for n in ("up_ready", "gelu_done", "spread_ready", "masked", "down_done", "yT_evac", "y_ready", "y_used"))
        proj_ready, raw_ready, rk_in, rk_exp, pre_used, hs_ready, soft_in, soft_exp, hsT_ready, hsT_evac, mixo_ready, mixo_used = (
            sem(n) for n in ("proj_ready", "raw_ready", "rk_in", "rk_exp", "pre_used", "hs_ready", "soft_in",
                             "soft_exp", "hsT_ready", "hsT_evac", "mixo_ready", "mixo_used"))
        old_scaled, old_prod, old_coef, old_read, old_summed = (
            sem(n) for n in ("old_scaled", "old_prod", "old_coef", "old_read", "old_summed"))
        coef_prod, coef_used, query_ready, beta_ready, values_ready, ksum_ready = (
            sem(n) for n in ("coef_prod", "coef_used", "query_ready", "beta_ready", "values_ready", "ksum_ready"))
        keys_ready, gram_prod, gram_used, prod_ready, summed, u_sum, u_evac = (
            sem(n) for n in ("keys_ready", "gram_prod", "gram_used", "prod_ready", "summed", "u_sum", "u_evac"))
        wcol_ready, rank_vec, fup_ready, fgelu_done, fdown_ready, out_ready, stored = (
            sem(n) for n in ("wcol_ready", "rank_vec", "fup_ready", "fgelu_done", "fdown_ready",
                             "out_ready", "stored"))
        fy_free, fy_biased = sem("fy_free"), sem("fy_biased")

        def wait(eng, s, value):
            if not (isinstance(value, int) and value <= 0):
                eng.wait_ge(s, value)

        def in_range(s):
            return not isinstance(s, int) or 0 <= s < IMAGES

        def attention_loop(eng, step):
            for s in range(4):
                step(s, s % 2, s // 2)
            with eng.Fori(2, IMAGES // 2 - 1) as q:
                for e in range(2):
                    step(q * 2 + e, e, q)
            for s in range(IMAGES - 2, IMAGES + 2):
                step(s, s % 2, s // 2)

        class Steps:
            def __init__(self, eng, s):
                self.eng, self.s, self.base, self.n = eng, s, 0, 0

            def then(self, ins):
                ins.then_inc(self.s, 1)
                self.n += 1
                self.eng.wait_ge(self.s, self.base + self.n)

            def count(self, ins):
                ins.then_inc(self.s, 1)
                self.n += 1

        SLOW_BANKS = (0, 1, 4)
        EMASK_BANKS = (5, 6, 7, 0, 5, 6)
        SCALE = float(D // HEADS) ** -0.5

        def chunk(n):
            return (2 * (n // 3) - n % 3) % 3

        def columns(n, half):
            hd, r = 2 * (n // 3) + half, (n % 3 + half) % 3
            return (8 * r + hd - chunk(n)) // 3

        FEATURES = 5 * DH + 2
        units = ps[:, 0:2, 0:3 * FEATURES].rearrange("p b (s f) -> p b s f", s=3)
        gram = ps[:, 2, 0:IMAGES * BOTH].rearrange("p (t r) -> p t r", r=BOTH)
        coef = ps[:, 3, 0:IMAGES * BOTH].rearrange("p (t r) -> p t r", r=BOTH)
        HALF_ROW = ROW // 2
        U_BANK, HS_BANK, OUT_BANK = 4, 6, 7

        def bs(a, i):
            return a[:, 6 * i:6 * i + 6, :].rearrange("p (b s) f -> p b s f", s=3)

        def old_chunks(t):
            return 1 if t >= 3 else 0

        def olds_before(t):
            return sum(1 for i in range(t) if old_chunks(i))

        def update_chunks(t):
            return sum_chunks(t) - old_chunks(t)

        def reading_chunks(t):
            return sum_chunks(t + 1) - old_chunks(t)

        def sum_chunks(n):
            return (n + 1) // 2

        def gram_chunks(n):
            return (n + 2) // 3

        def sums_before(t, reading):
            n = sum(update_chunks(i) + reading_chunks(i) for i in range(t))
            return n + update_chunks(t) if reading else n

        def coef_chunks(n):
            return (n + 3) // 4

        def coefs_before(t):
            return sum(coef_chunks(i + 1) for i in range(t))

        def grams_before(t):
            return sum(gram_chunks(i) for i in range(1, t))

        def query_parts(to, i):
            source = ps[:, i % 2, 0:2 * SEQ].rearrange("p (h r u) -> p h r u", h=2, r=3)
            return ((to[:, 3 * i:3 * i + 3, 0, :], source[:, 0, :, :]),
                    (to[:, 3 * i:3 * i + 2, 1, :], source[:, 1, 1:3, :]),
                    (to[:, 3 * i + 2, 1, :], source[:, 1, 0, :]))

        def f32(a):
            return a.bitcast(F32)

        block = ctx.enter_context(nc.Block())

        @block.sync
        def _(sp):
            sp.dma_start(tokW_raw[:, :], tok_W).then_inc(ld_tok, 16)
            pix_v = pixels[:, :].rearrange("p (n i w) -> p n i w", n=IMAGES, i=GRID)
            for n in range(IMAGES):
                for k in range(CHANNELS):
                    sp.dma_start(pix_v[PATCH * k:PATCH * k + PATCH, n, :, :], x[n, k, :, :].rearrange("(i y) w -> y i w", y=PATCH))\
                      .then_inc(ld_image[n // 2], 16)
            for half in range(2):
                rows_ = slice(D * half, D * half + D)
                sp.dma_start(W1_raw[rows_, :, :], W1.rearrange("e d k -> d e k")).then_inc(ld_moe, 16)
                sp.dma_start(fraw[rows_, FWG:FWG + EXPERTS], Wg).then_inc(ld_moe, 16)
                sp.dma_start(wr_raw[rows_, :], wr).then_inc(ld_moe, 16)
                sp.dma_start(fraw[rows_, FW1:FW1 + FFN_HIDDEN], w1).then_inc(ld_moe, 16)
                sp.dma_start(W2_sb[:, :, half, :], W2.rearrange("e k d -> k e d")).then_inc(ld_moe, 16)
            sp.dma_start(w2_sb[:, :, :], w2.rearrange("(a k) d -> k a d", a=2)).then_inc(ld_ffn, 16)
            out_t = out.rearrange("b s d -> (b s) d").rearrange("(t p) d -> p t d", p=P)
            for c in range(3):
                sp.wait_ge(out_ready, c + 1)
                sp.dma_start(out_t[:, 8 * c:8 * c + 8, :], h[:, 8 * c:8 * c + 8, :]).then_inc(stored, 16)
            sp.wait_ge(stored, 3 * 16)

        @block.gpsimd
        def _(pool):
            pool.memset(ident[:, :], 0.0).then_inc(ident_set, 1)
            pool.wait_ge(ident_set, 1)
            pool.affine_select(out=ident[:, :], in_=ident[:, :], compare_op=ALU.not_equal, fill=1.0, base=0,
                               pattern=[[-1, P]], channel_multiplier=1).then_inc(ident_set, 1)
            pool.memset(b2_rows[:, :, :], 0.0).then_inc(b2_set, 1)
            pool.wait_ge(b2_set, 1)
            for half in range(2):
                pool.dma_start(b2_rows[0:EXPERTS, half, :], b2).then_inc(ld_b2, 16)
            for dst, src in ((bg_sb, bg), (tokb_sb, tok_b), (g_sb, ln_g), (b_sb, ln_b), (br_sb, br), (fb2_sb, fb2)):
                pool.dma_start(dst[:, :], src.partition_broadcast(P)).then_inc(ld_bias, 16)
            pool.wait_ge(mix_used, 2 * IMAGES)
            pool.memset(f32(expert_mask[:, :]), 0.0).then_inc(zero_set, 1)

            def by_unit(a, n):
                return a.unsqueeze(1).to_broadcast([P, n, a.shape[1]])

            def values_and_keys(t):
                pool.wait_ge(beta_ready, t + 1)
                ut = UU[:, t, :].rearrange("p (r d) -> p r d", d=DH)
                pool.tensor_tensor(ut, ut, beta[t % 2][:, :, :].rearrange("p u c -> p (u c)").unsqueeze(2)
                                   .to_broadcast([P, BOTH, DH]), ALU.mult).then_inc(values_ready, 1)
                pool.wait_ge(ksum_ready, t + 1)
                kt = KK[:, t, :].rearrange("p (r d) -> p r d", d=DH)
                pool.tensor_tensor(kt, kt, ksum[:, :].unsqueeze(2).to_broadcast([P, BOTH, DH]), ALU.mult).then_inc(keys_ready, 1)
                pool.wait_ge(keys_ready, t + 1)

            def gram_products(t, c):
                m, n = grams_before(t) + c, min(3, t - 3 * c)
                wait(pool, gram_used, m - 1)
                pool.tensor_tensor(GRAM_ROWS[m % 2][:, 0:n, :], KK[:, 3 * c:3 * c + n, :],
                                   by_unit(KK[:, t, :], n), ALU.mult).then_inc(gram_prod, 1)

            def coef_products(t, c):
                m, n = coefs_before(t) + c, min(4, t + 1 - 4 * c)
                pool.wait_ge(query_ready, t + 1)
                wait(pool, coef_used, m - 1)
                for i in range(n):
                    to = COEF1_ROWS[m % 2][:, i, :].rearrange("p (u d) -> p u d", d=DH)
                    ins = pool.tensor_tensor(to, KK[:, 4 * c + i, :].rearrange("p (u c d) -> p c u d", c=2, d=DH)[:, 0, :, :],
                                             QE1[t % 2][:, :, :], ALU.mult)
                ins.then_inc(coef_prod, 1)

            def old_products(t):
                n = 2 * old_chunks(t)
                pool.wait_ge(old_scaled, olds_before(t + 1))
                pool.wait_ge(u_evac, n - 1)
                wait(pool, old_summed, olds_before(t))
                pool.tensor_tensor(OLD_ROWS[:, 0:n, :].rearrange("p t (r d) -> p t r d", d=DH),
                                   UU[:, 0:n, :].rearrange("p t (r d) -> p t r d", d=DH),
                                   gram_old[:, 0:n, :].unsqueeze(3).to_broadcast([P, n, BOTH, DH]), ALU.mult)\
                    .then_inc(old_prod, 1)

            def old_reading(t):
                n = 2 * old_chunks(t)
                pool.wait_ge(old_coef, olds_before(t + 1))
                pool.wait_ge(u_sum, t)
                pool.tensor_tensor(OLD_ROWS[:, 0:n, :].rearrange("p t (r d) -> p t r d", d=DH),
                                   UU[:, 0:n, :].rearrange("p t (r d) -> p t r d", d=DH),
                                   coef_old[:, 0:n, :].unsqueeze(3).to_broadcast([P, n, BOTH, DH]), ALU.mult)\
                    .then_inc(old_read, 1)

            values_and_keys(0)
            coef_products(0, 0)
            for t in range(IMAGES):
                grams = gram_chunks(t + 1) if t + 1 < IMAGES else 0
                if old_chunks(t):
                    old_products(t)
                if t + 1 < IMAGES:
                    values_and_keys(t + 1)
                for c in range(2, max(coef_chunks(t + 1), grams + 2)):
                    if c - 2 < grams:
                        gram_products(t + 1, c - 2)
                    if c < coef_chunks(t + 1):
                        coef_products(t, c)
                if t + 1 < IMAGES:
                    coef_products(t + 1, 0)
                if old_chunks(t):
                    old_reading(t)
                if t + 1 < IMAGES and coef_chunks(t + 2) > 1:
                    coef_products(t + 1, 1)

            pool.wait_ge(norm_ready, 4)
            masks = Steps(pool, masks_set)
            masks.then(pool.memset(earlier[:, :, :], 1.0))
            for rows_, k, base in ((slice(0, P), 0, 0), (slice(0, D), 1, P), (slice(D, P), 1, 0), (slice(0, P), 2, D)):
                m = earlier[rows_, k, :]
                masks.then(pool.affine_select(out=m, in_=m, compare_op=ALU.is_gt, fill=0.0, base=base,
                                              pattern=[[-1, SEQ]], channel_multiplier=1))
            pool.wait_ge(fy_free, 7)
            pool.tensor_tensor(fy[:, :, :], fy[:, :, :], fb2_sb[:, :].unsqueeze(1).to_broadcast([P, TILES, D]), ALU.add)\
                .then_inc(fy_biased, 1)

        @block.scalar
        def _(act):
            for half in range(2):
                act.dma_start(Wq_raw[:, :, half, :], Wq.rearrange("(h k) c -> k h c", k=D)).then_inc(ld_attn, 16)
                act.dma_start(Wv_raw[:, half, :], Wv).then_inc(ld_attn, 16)
            act.dma_start(Wk_raw[:, :], Wk).then_inc(ld_attn, 16)
            act.dma_start(Wo_raw[:, :], Wo).then_inc(ld_attn, 16)
            act.dma_start(slowA[0:64, :, :], slow_W.rearrange("(h f) c -> f h c", h=HEADS)[0:64, :, :]).then_inc(ld_slow, 16)
            act.dma_start(slowA[64:96, :, :], slow_W.rearrange("(h f) c -> f h c", h=HEADS)[96:128, :, :]).then_inc(ld_slow, 16)
            act.dma_start(slowB[0:32, :, :], slow_W.rearrange("(h f) c -> f h c", h=HEADS)[64:96, :, :]).then_inc(ld_slow, 16)
            act.dma_start(slowB[32:66, :, :], slow_W.rearrange("(h f) c -> f h c", h=HEADS)[128:162, :, :]).then_inc(ld_slow, 16)
            act.dma_start(outW_raw[:, :], out_W).then_inc(ld_slow, 16)
            act.dma_start(b1_raw[:, :], b1).then_inc(ld_slow, 16)
            act.dma_start(fb1_raw[:, :], fb1.rearrange("(a k) -> a k", a=2)).then_inc(ld_slow, 16)
            hv = h[:, :, :].rearrange("p (q r) d -> p q r d", r=3)
            tv = txt.rearrange("(q two) s d -> two s q d", two=2)
            act.dma_start(hv[D:P, :, 0, :], tv[0, 0:D, :, :]).then_inc(ld_text, 16)
            act.dma_start(hv[0:D, :, 1, :], tv[0, D:P, :, :]).then_inc(ld_text, 16)
            act.dma_start(hv[:, :, 2, :], tv[1, :, :, :]).then_inc(ld_text, 16)

            act.wait_ge(ld_moe, 10 * 16)
            act.activation(W1s[:, :, :], W1_raw[:, :, :], ACT.Copy).then_inc(split_high, 1)
            act.wait_ge(wr_set, 1)
            act.activation(fsplit[:, :], fraw[:, :], ACT.Copy).then_inc(split_high, 1)
            act.wait_ge(wt_ready, 1)
            for c in range(2):
                act.activation(Nh[:, 4 * c:4 * c + 4, :], ps[:, 4 + c, :], ACT.Copy, scale=SCALE).then_inc(split_high, 1)
            act.wait_ge(var_ready, 1)
            act.activation(stat[:, 1, :], stat[:, 1, :], ACT.Sqrt).then_inc(std_ready, 1)
            act.wait_ge(wt_ready, 2)
            act.activation(WvT[:, :], ps[:, 7, 256:384], ACT.Copy).then_inc(split_high, 1)
            act.activation(WoT[:, 0:8, :], ps[:, 6, :], ACT.Copy).then_inc(wt_evac, 1)
            act.activation(WoT[:, 8:12, :], ps[:, 7, 0:256], ACT.Copy).then_inc(wt_evac, 1)
            act.activation(WoutT[:, :, :], ps[:, 7, 384:512], ACT.Copy).then_inc(wt_evac, 1)

            def std(k):
                act.wait_ge(var_ready, k + 1)
                act.activation(stat[:, 1, :], stat[:, 1, :], ACT.Sqrt).then_inc(std_ready, 1)

            def split_xT(k, high):
                for c in range(6):
                    act.wait_ge(tr_ready, 6 * k + c + 1)
                    act.activation(high[:, 512 * c:512 * c + 512], ps[:, c, :], ACT.Copy).then_inc(tr_evac_a, 1)

            split_xT(0, xTH)

            def q_halves(b, e):
                wait(act, score_ready, b * 6 - 6)
                for i in range(PAIRS):
                    act.wait_ge(qp_ready, b * 4 + (i + 1))
                    for to, source in query_parts(Qs[e], i):
                        act.activation(to, source, ACT.Copy).then_inc(q_high, 1)

            def exps(b, e):
                wait(act, gt_ready, b - 1)
                wait(act, wos_ready, b - 1)
                for m in range(6):
                    act.wait_ge(max_ready, b * 6 + m + 1)
                    for s in range(2):
                        n = 2 * m + s
                        act.activation(probs[e][:, n, :], ps[:, 2 + m % 3, SEQ * s:SEQ * s + SEQ], ACT.Exp,
                                       bias=negmax[e][:, n:n + 1], accum_out=rowsum[e][:, n:n + 1]).then_inc(exp_done, 1)

            def evacuate_gt(b):
                act.wait_ge(gt_ready, b + 1)
                wait(act, g_ready, b)
                act.activation(GT01[:, :], ps[:, 6, 0:SEQ], ACT.Copy).then_inc(gt_evac, 1)
                act.activation(GT2[:, :], ps[0:D, 6, SEQ:2 * SEQ], ACT.Copy).then_inc(gt_evac, 1)

            def evacuate_g(b, e):
                act.wait_ge(g_ready, b + 1)
                wait(act, mix_ready, b - 1)
                act.activation(Glo[e][:, :, :], ps[:, 5, SEQ:2 * SEQ], ACT.Copy).then_inc(g_evac, 1)
                act.activation(Ghi[e][:, :, :], ps[0:D, 7, SEQ:2 * SEQ], ACT.Copy).then_inc(g_evac, 1)

            def attention_step(s, e, q):
                if in_range(s - 2):
                    evacuate_g(s - 2, e)
                if in_range(s + 1):
                    q_halves(s + 1, 1 - e)
                if in_range(s):
                    exps(s, e)
                if in_range(s - 1):
                    evacuate_gt(s - 1)

            q_halves(0, 0)
            attention_loop(act, attention_step)

            act.wait_ge(wt2_ready, 1)
            act.activation(b1T[:, :], ps[:, 5, 0:8], ACT.Copy).then_inc(wt2_evac, 1)
            act.activation(fb1T[:, :], ps[:, 5, 8:10], ACT.Copy).then_inc(wt2_evac, 1)
            for c in range(3):
                n = min(3, HEADS - 3 * c)
                act.activation(slowT[:, 3 * c:3 * c + n, :], ps[0:D, SLOW_BANKS[c], 0:162 * n], ACT.Copy).then_inc(wt2_evac, 1)
            std(1)
            split_xT(1, xTH)
            act.activation(pick[:, :, :], ident[:, 0:EXPERTS].unsqueeze(2).to_broadcast([P, EXPERTS, P]), ACT.Copy)\
               .then_inc(pick_set, 1)
            act.wait_ge(zero_set, 1)
            for c in range(6):
                act.wait_ge(emask_ready, c + 1)
                act.activation(expert_mask[0:EXPERTS, 512 * c:512 * c + 512], ps[0:EXPERTS, EMASK_BANKS[c], :], ACT.Copy)\
                   .then_inc(emask_evac, 1)

            def gelus(ch, before):
                for e in range(EXPERTS):
                    act.wait_ge(up_ready, ch * 8 + (e + 1))
                    act.wait_ge(down_done, ch * 8 + (e + 1))
                    act.activation(hid[e % 4], ps[:, e % 2, :], ACT.Gelu, bias=b1T[:, e:e + 1]).then_inc(gelu_done, 1)
                    if e == 1 and before:
                        summed_rows(ch - 1)

            def summed_rows(ch):
                act.wait_ge(down_done, ch * 8 + 12)
                act.wait_ge(y_ready, ch + 1)
                act.activation(yT[:, :], ps[0:D, 4, :], ACT.Copy).then_inc(yT_evac, 1)

            gelus(0, False)
            with act.Fori(1, 6) as ch:
                gelus(ch, True)
            summed_rows(5)

            std(2)
            std(3)
            for c in range(0, 6, 2):
                act.wait_ge(tr_ready, 12 + c + 1)
                act.activation(xT[:, 512 * c:512 * c + 512], ps[0:D, c, :], ACT.Copy).then_inc(tr_evac_a, 1)

            def pre(t):
                kt = KK[:, t, :].rearrange("p (u c d) -> p u c d", c=2, d=DH)[:, :, 1, :]
                ut = UU[:, t, :].rearrange("p (u f) -> p u f", f=2 * DH)
                for i in range(2):
                    act.wait_ge(proj_ready, 2 * t + i + 1)
                    act.activation(bs(kt, i), units[:, :, :, 64:96], ACT.Copy).then_inc(raw_ready, 1)
                    act.activation(bs(ut, i), units[:, :, :, 96:160], ACT.Copy).then_inc(raw_ready, 1)
                    wait(act, pre_used, t)
                    act.activation(bs(relu_qk[:, :, :], i), units[:, :, :, 0:64], ACT.Relu).then_inc(raw_ready, 1)
                    act.activation(bs(exp_qk[:, :, :], i), units[:, :, :, 0:64], ACT.Exp).then_inc(raw_ready, 1)
                    wait(act, values_ready, t - 1)
                    act.activation(bs(beta[t % 2][:, :, :], i), units[:, :, :, 160:162], ACT.Exp, scale=-1.0).then_inc(raw_ready, 1)

            def rk_softmax(t):
                act.wait_ge(rk_in, t + 1)
                kt = KK[:, t, :].rearrange("p (u c d) -> p u c d", c=2, d=DH)[:, :, 1, :]
                act.activation(kt, kt, ACT.Exp).then_inc(rk_exp, 1)

            def transposed_state(t):
                act.wait_ge(hsT_ready, t + 1)
                wait(act, mixo_ready, t)
                act.activation(hsT[:, :, 0:P], ps[:, OUT_BANK, 0:2 * P].rearrange("p (c n) -> p c n", c=2), ACT.Copy)\
                   .then_inc(hsT_evac, 1)
                act.activation(hsT[:, :, P:SEQ], ps[:, OUT_BANK, 2 * P:3 * P].rearrange("p (c n) -> p c n", c=2), ACT.Copy)\
                   .then_inc(hsT_evac, 1)

            pre(0)
            rk_softmax(0)
            pre(1)
            for t in range(IMAGES):
                if t:
                    act.wait_ge(soft_in, t)
                    act.activation(QE2[:, :, :], QE2[:, :, :], ACT.Exp).then_inc(soft_exp, 1)
                if t + 1 < IMAGES:
                    rk_softmax(t + 1)
                if t:
                    act.wait_ge(u_sum, t)
                    act.activation(UU[:, t, :].rearrange("p (b r) -> p b r", b=2), ps[:, U_BANK:U_BANK + 2, 0:HALF_ROW],
                                   ACT.Copy).then_inc(u_evac, 1)
                    transposed_state(t - 1)
                if t + 2 < IMAGES:
                    pre(t + 2)
                act.wait_ge(summed, sums_before(t + 1, False))
                wait(act, old_summed, olds_before(t + 1))
                wait(act, hsT_ready, t - 1)
                act.activation(hs[t % 2][:, :, :], ps[:, HS_BANK, 0:HALF_ROW].rearrange("p (u d) -> p u d", d=DH), ACT.Copy)\
                   .then_inc(hs_ready, 1)
            transposed_state(IMAGES - 1)

            std(4)
            split_xT(3, xTH3)
            with act.Fori(0, 3) as c2:
                for e in range(2):
                    ch = c2 * 2 + e
                    for a in range(2):
                        act.wait_ge(fup_ready, ch * 2 + a + 1)
                        act.wait_ge(fdown_ready, c2 * 2 + 1)
                        act.activation(fhid[e][:, a, :], ps[:, 2 * e + a, :], ACT.Gelu_apprx_tanh, bias=fb1T[:, a:a + 1])\
                           .then_inc(fgelu_done, 1)
                    act.wait_ge(fdown_ready, ch + 2)
                    act.activation(fy[:, bass.ds(ch * 4, 4), :], ps[:, 4 + e, 0:4 * D], ACT.Copy).then_inc(fy_free, 1)

        @block.tensor
        def _(pe):
            def mm(o, lhsT, rhs, start=True, stop=True):
                return pe.matmul(o, lhsT, rhs, start=start, stop=stop)

            def tr(o, in_):
                k = in_.shape[0]
                return pe.transpose(o, in_, ident[0:k, 0:k])

            def mm_split(o, lhsT, high, low):
                mm(o, lhsT, high, stop=False)
                return mm(o, lhsT, low, start=False)

            pe.wait_ge(ident_set, 2)
            pe.wait_ge(ld_tok, 16)
            for px in range(PATCH):
                last = tr(ps[0:CHANNELS * PATCH, px // 8, D * (px % 8):D * (px % 8) + D], tokW_raw[:, px:CHANNELS * 256:PATCH])
            last.then_inc(tokw_ready, 1)
            pe.wait_ge(tokw_evac, 2)
            for q in range(8):
                pe.wait_ge(ld_image[q], 2 * CHANNELS * 16)
                for px in range(PATCH):
                    c0 = 2 * GRID * SIDE * q + px
                    last = mm(ps[:, 2 + q // 4, D * (q % 4):D * (q % 4) + D], pixels[:, c0:c0 + 127 * PATCH + 1:PATCH],
                              tokWT[:, px, :], start=(px == 0), stop=(px == PATCH - 1))
                if q % 4 == 3:
                    last.then_inc(embed_ready, 1)
            pe.wait_ge(ld_attn, 6 * 16)
            for hd in range(HEADS):
                last = mm(ps[:, 4 + hd // 4, P * (hd % 4):P * (hd % 4) + P], Wq_raw[:, hd, :, :],
                          Wk_raw[:, :].unsqueeze(1).to_broadcast([D, 2, D]))
            last.then_inc(wt_ready, 1)
            for n in range(12):
                for half in range(2):
                    k = columns(n, half)
                    mm(ps[D * half:D * half + D, 6 + n // 8, D * (n % 8):D * (n % 8) + D], Wo_raw[:, k:k + 505:8], ident[0:D, 0:D])
            mm(ps[:, 7, 256:384], Wv_raw[:, :, :], ident[0:D, 0:D].unsqueeze(1).to_broadcast([D, 2, D]))
            pe.wait_ge(ld_slow, 7 * 16)
            for c in range(2):
                last = tr(ps[:, 7, 384 + D * c:448 + D * c], outW_raw[:, P * c:P * c + P])
            last.then_inc(wt_ready, 1)
            pe.wait_ge(split_low, 4)

            def transpose_x(k, src, rows_):
                pe.wait_ge(norm_ready, k + 1)
                for t in range(TILES):
                    last = tr(ps[0:rows_, t // 4, P * (t % 4):P * (t % 4) + P], src[:, t])
                    if t % 4 == 3:
                        last.then_inc(tr_ready, 1)

            transpose_x(0, xn, P)
            pe.wait_ge(wt_evac, 3)
            pe.wait_ge(split_low, 5)
            pe.wait_ge(tr_evac_v, 6)

            def queries(b, i):
                high, low = (x_[:, bass.ds(b * SEQ, SEQ)].rearrange("c (u r) -> c r u", r=3) for x_ in (xTH, xTL))
                wait(pe, qp_evac, b * 12 + (3 * i - 3))
                for k in range(2):
                    last = mm_split(ps[:, i % 2, SEQ * k:SEQ * k + SEQ], Nh[:, 2 * i + k, :], high, low)
                last.then_inc(qp_ready, 1)

            def scores(b, e, m):
                high, low = (x_[:, bass.ds(b * SEQ, SEQ)].rearrange("c (o j) -> c j o", j=3) for x_ in (xTH, xTL))
                pe.wait_ge(qp_evac, b * 12 + (3 * ((2 * m + 1) // 3) + 3))
                wait(pe, exp_done, b * 12 + (2 * m - 4))
                for s in range(2):
                    last = mm_split(ps[:, 2 + m % 3, SEQ * s:SEQ * s + SEQ], Qs[e][:, 2 * m + s, :, :], high, low)
                last.then_inc(score_ready, 1)

            def values(b):
                wait(pe, g_evac, b * 2)
                mm_split(ps[:, 5, 0:SEQ], WvT[:, :], xTH[:, bass.ds(b * SEQ, SEQ)], xTL[:, bass.ds(b * SEQ, SEQ)]).then_inc(v_ready, 1)

            def weigh(b, e, m):
                if m == 0:
                    wait(pe, gt_evac, b * 2)
                    pe.wait_ge(wos_ready, b + 1)
                for j, i in (divmod(2 * m, PAIRS), divmod(2 * m + 1, PAIRS)):
                    o = ps[D:P, 6, 0:SEQ] if j == 1 else ps[0:D, 6, SEQ * (j // 2):SEQ * (j // 2) + SEQ]
                    n = 3 * i + (2 * i - j) % 3
                    last = mm(o, WoS[e][:, n, :], probs[e][:, n, :], start=(i == 0), stop=(i == PAIRS - 1))
                if m == 5:
                    last.then_inc(gt_ready, 1)

            def turn(b):
                pe.wait_ge(v_evac, b * 3 + 3)
                wait(pe, mix_used, b * 2)
                pe.wait_ge(gt_evac, b * 2 + 2)
                mm(ps[:, 5, SEQ:SEQ + P], GT01[:, 0:P], ident[:, :])
                mm(ps[:, 5, SEQ + P:2 * SEQ], GT2[:, 0:P], ident[0:D, 0:D])
                mm(ps[0:D, 7, SEQ:SEQ + P], GT01[:, P:SEQ], ident[:, :])
                mm(ps[0:D, 7, SEQ + P:2 * SEQ], GT2[:, P:SEQ], ident[0:D, 0:D]).then_inc(g_ready, 1)

            def mix(b, e):
                pe.wait_ge(g_evac, b * 2 + 2)
                mm(ps[:, 7, 0:SEQ], Vlo[e][:, :, :], Glo[e][:, :, :], stop=False)
                mm(ps[:, 7, 0:SEQ], Vhi[e][:, :, :], Ghi[e][:, :, :], start=False).then_inc(mix_ready, 1)

            def attention_step(s, e, q):
                if in_range(s - 2):
                    turn(s - 2)
                for i in range(PAIRS):
                    if in_range(s + 1):
                        queries(s + 1, i)
                    if i == 1 and in_range(s - 2):
                        mix(s - 2, e)
                    if i == 2 and in_range(s - 1):
                        values(s - 1)
                for m in range(6):
                    if in_range(s):
                        scores(s, e, m)
                    if in_range(s - 1):
                        weigh(s - 1, 1 - e, m)

            for i in range(PAIRS):
                queries(0, i)
            attention_loop(pe, attention_step)

            tr(ps[:, 5, 0:8], b1_raw[:, :])
            tr(ps[:, 5, 8:10], fb1_raw[:, :])
            for hd in range(HEADS):
                c0 = 162 * (hd % 3)
                tr(ps[0:D, SLOW_BANKS[hd // 3], c0:c0 + 96], slowA[:, hd, :])
                last = tr(ps[0:D, SLOW_BANKS[hd // 3], c0 + 96:c0 + 162], slowB[:, hd, :])
            last.then_inc(wt2_ready, 1)
            pe.wait_ge(wt2_evac, 5)
            transpose_x(1, xn, P)
            pe.wait_ge(split_low, 5)
            for t in range(TILES):
                if t % 4 == 0:
                    pe.wait_ge(tr_evac_v, 6 + t // 4 + 1)
                o, wg = ps[:, 0, 8 * t:8 * t + 8], fsplit[:, FWG:FWG + EXPERTS]
                mm(o, xTH[:, P * t:P * t + P], wg, stop=False)
                last = mm(o, xTL[:, P * t:P * t + P], wg, start=False)
            last.then_inc(gate_ready, 1)
            pe.wait_ge(mask_ready, 1)
            for c in range(6):
                if c >= 4:
                    pe.wait_ge(emask_evac, c - 3)
                for i in range(4):
                    last = tr(ps[0:EXPERTS, EMASK_BANKS[c], P * i:P * i + P], mask[:, 4 * c + i, :])
                last.then_inc(emask_ready, 1)
            pe.wait_ge(emask_evac, 6)
            pe.wait_ge(pick_set, 1)
            pe.wait_ge(ld_b2, 2 * 16)

            def up(ch, e):
                mm_split(ps[:, e % 2, :], W1s[:, e, :], xTH[:, bass.ds(ch * 512, 512)], xTL[:, bass.ds(ch * 512, 512)])\
                    .then_inc(up_ready, 1)

            def spread_mask(ch, e):
                mm(ps[:, 2 + e % 2, :], pick[:, e, :], expert_mask[:, bass.ds(ch * 512, 512)]).then_inc(spread_ready, 1)

            def down(ch, e):
                if e == 0:
                    pe.wait_ge(yT_evac, ch + 1)
                    mm(ps[:, 4, :], b2_rows[:, :, :], f32(expert_mask[:, bass.ds(ch * 512, 512)]), stop=False)
                mm(ps[:, 4, :], W2_sb[:, e, :, :], hid[e % 4], start=False, stop=(e == EXPERTS - 1)).then_inc(down_done, 1)

            def rows(ch):
                pe.wait_ge(yT_evac, ch + 2)
                pe.wait_ge(y_used, ch + 1)
                for i in range(4):
                    last = mm(ps[:, 5, D * i:D * i + D], yT[:, P * i:P * i + P], ident[0:D, 0:D])
                last.then_inc(y_ready, 1)

            def experts(ch, before, more):
                for e in range(EXPERTS):
                    to, ahead = (ch, e + 2) if e + 2 < EXPERTS else (ch + 1, e + 2 - EXPERTS)
                    pe.wait_ge(gelu_done, ch * 8 + (e + 1))
                    if e + 2 < EXPERTS or more:
                        up(to, ahead)
                    pe.wait_ge(masked, ch * 8 + (e + 1))
                    if e + 2 < EXPERTS or more:
                        spread_mask(to, ahead)
                    down(ch, e)
                    if e == 2 and before:
                        rows(ch - 1)

            pe.sem_inc(down_done, 4)
            pe.sem_inc(y_ready, 1)
            pe.sem_inc(yT_evac, 1)
            for e in range(2):
                up(0, e)
                spread_mask(0, e)
            experts(0, False, True)
            with pe.Fori(1, 5) as ch:
                experts(ch, True, True)
            experts(5, True, False)
            rows(5)

            transpose_x(2, o_tok, D)
            pe.wait_ge(tr_evac_a, 12 + 3)
            pe.wait_ge(tr_evac_v, 12 + 3)

            def project(t):
                wait(pe, raw_ready, 10 * t)
                here, there = xT[:, SEQ * t:SEQ * t + P], xT[:, SEQ * t + P:SEQ * t + SEQ]
                for b in range(2):
                    last = mm(ps[:, b, 0:3 * FEATURES], here, slowT[:, 3 * b:3 * b + 3, :])
                last.then_inc(proj_ready, 1)
                pe.wait_ge(raw_ready, 10 * t + 5)
                mm(ps[:, 0, 0:2 * FEATURES], here, slowT[:, 6:8, :])
                for half in range(2):
                    rows_, hd = slice(D * half, D * half + D), 4 * half
                    mm(ps[rows_, 0, 2 * FEATURES:3 * FEATURES], there, slowT[:, hd, :])
                    last = mm(ps[rows_, 1, 0:3 * FEATURES], there, slowT[:, hd + 1:hd + 4, :])
                last.then_inc(proj_ready, 1)

            def sum_update(t):
                wait(pe, u_evac, t - 1)
                for c in range(update_chunks(t)):
                    m = sums_before(t, False) + c
                    pe.wait_ge(prod_ready, m + 1)
                    for i in range(min(2, t - 2 * (c + old_chunks(t)))):
                        for half in range(2):
                            last = mm(ps[:, U_BANK + half, 0:HALF_ROW], ident[:, :],
                                      SUM_ROWS[m % 3][:, i, HALF_ROW * half:HALF_ROW * half + HALF_ROW],
                                      start=(c == 0 and i == 0), stop=False)
                    last.then_inc(summed, 1)
                if old_chunks(t):
                    pe.wait_ge(old_prod, olds_before(t + 1))
                for i in range(2 * old_chunks(t)):
                    for half in range(2):
                        mm(ps[:, U_BANK + half, 0:HALF_ROW], ident[:, :],
                           OLD_ROWS[:, i, HALF_ROW * half:HALF_ROW * half + HALF_ROW], start=False, stop=False)
                pe.wait_ge(values_ready, t + 1)
                for half in range(2):
                    last = mm(ps[:, U_BANK + half, 0:HALF_ROW], ident[:, :],
                              UU[:, t, HALF_ROW * half:HALF_ROW * half + HALF_ROW], start=False)
                last.then_inc(u_sum, 1)

            def sum_reading(t):
                wait(pe, hs_ready, t)
                old = old_chunks(t)
                for c in range(reading_chunks(t)):
                    m = sums_before(t, True) + c
                    pe.wait_ge(prod_ready, m + 1)
                    n = min(2, t + 1 - 2 * (c + old))
                    for i in range(n):
                        row = SUM_ROWS[m % 3][:, i, :].rearrange("p (u c d) -> p c u d", c=2, d=DH)
                        for memory in range(2):
                            last = mm(ps[:, HS_BANK, 0:HALF_ROW], ident[:, :], row[:, memory, :, :],
                                      start=(c == 0 and i == 0 and memory == 0),
                                      stop=(not old and 2 * c + i == t and memory == 1))
                    last.then_inc(summed, 1)
                if old:
                    pe.wait_ge(old_read, olds_before(t + 1))
                    for i in range(2 * old):
                        row = OLD_ROWS[:, i, :].rearrange("p (u c d) -> p c u d", c=2, d=DH)
                        for memory in range(2):
                            last = mm(ps[:, HS_BANK, 0:HALF_ROW], ident[:, :], row[:, memory, :, :], start=False,
                                      stop=(i == 2 * old - 1 and memory == 1))
                    last.then_inc(old_summed, 1)

            def output_rows(t):
                pe.wait_ge(hs_ready, t + 1)
                wait(pe, mixo_used, 2 * t)
                for c in range(3):
                    last = tr(ps[:, OUT_BANK, P * c:P * c + P], hs[t % 2][:, 4 * c:4 * c + 4, :])
                last.then_inc(hsT_ready, 1)
                pe.wait_ge(hsT_evac, 2 * t + 2)
                o = ps[:, OUT_BANK, 3 * P:4 * P]
                if t % 2 == 0:
                    parts = ((o[:, 0:D], 0, P), (o[0:D, D:2 * D], P, SEQ))
                else:
                    parts = ((o[D:P, 0:D], 0, D), (o[:, D:2 * D], D, SEQ))
                for o_, c0, c1 in parts:
                    for c in range(2):
                        last = mm(o_, hsT[:, c, c0:c1], WoutT[:, c, :], start=(c == 0), stop=(c == 1))
                last.then_inc(mixo_ready, 1)

            project(0)
            project(1)
            for t in range(IMAGES):
                if t:
                    sum_update(t)
                    output_rows(t - 1)
                if t + 2 < IMAGES:
                    project(t + 2)
                sum_reading(t)
            output_rows(IMAGES - 1)

            transpose_x(3, xn, P)
            pe.wait_ge(tr_evac_v, 15 + 6)
            pe.wait_ge(ld_ffn, 16)
            for c in range(6):
                mm_split(ps[:, c, :], fsplit[:, FWR:FWR + P], xTH3[:, 512 * c:512 * c + 512], xTL3[:, 512 * c:512 * c + 512])\
                    .then_inc(wcol_ready, 1)
            pe.wait_ge(rank_vec, 6)
            pe.sem_inc(fdown_ready, 1)
            pe.sem_inc(fy_free, 1)

            def fup(ch, e):
                for a in range(2):
                    mm_split(ps[:, 2 * e + a, :], fsplit[:, FW1 + P * a:FW1 + P * a + P], xTH3[:, bass.ds(ch * 512, 512)],
                             xTL3[:, bass.ds(ch * 512, 512)]).then_inc(fup_ready, 1)

            def fdown(ch, e, c2):
                pe.wait_ge(fgelu_done, ch * 2 + 2)
                pe.wait_ge(fy_free, c2 * 2 + 1)
                for s in range(4):
                    for a in range(2):
                        last = mm(ps[:, 4 + e, D * s:D * s + D], fhid[e][:, a, P * s:P * s + P], w2_sb[:, a, :],
                                  start=(a == 0), stop=(a == 1))
                last.then_inc(fdown_ready, 1)

            fup(0, 0)
            with pe.Fori(0, 2) as c2:
                for e in range(2):
                    fup(c2 * 2 + (e + 1), 1 - e)
                    fdown(c2 * 2 + e, e, c2)
            fup(5, 1)
            fdown(4, 0, 2)
            fdown(5, 1, 2)

        @block.vector
        def _(dve):
            st = Steps(dve, vec)

            dve.wait_ge(tokw_ready, 1)
            for c in range(2):
                dve.tensor_copy(tokWT[:, 8 * c:8 * c + 8, :], ps[0:CHANNELS * PATCH, c, :]).then_inc(tokw_evac, 1)
            dve.wait_ge(ld_moe, 10 * 16)
            dve.tensor_copy(fraw[:, FWR:FWR + P], wr_raw[:, :].to_broadcast([P, P])).then_inc(wr_set, 1)
            def spread(a):
                return a.unsqueeze(2).to_broadcast([P, TILES, D])

            def squares(src, cen, sq, t):
                n = t.stop - t.start
                st.then(dve.tensor_reduce(stat[:, 0, t], src[:, t, :], axis=AXL.X, op=ALU.add))
                st.then(dve.tensor_scalar(stat[:, 0, t], stat[:, 0, t], 1.0 / D, None, ALU.mult))
                st.then(dve.tensor_tensor(cen[:, t, :], src[:, t, :], stat[:, 0, t].unsqueeze(2).to_broadcast([P, n, D]), ALU.subtract))
                st.then(dve.tensor_tensor(sq[:, t, :], cen[:, t, :], cen[:, t, :], ALU.mult))
                st.then(dve.tensor_reduce(stat[:, 1, t], sq[:, t, :], axis=AXL.X, op=ALU.add))

            def variances():
                dve.tensor_scalar(stat[:, 1, :], stat[:, 1, :], 1.0 / D, EPS, ALU.mult, ALU.add).then_inc(var_ready, 1)

            def normalise(k, dst, cen):
                dve.wait_ge(std_ready, k + 1)
                st.then(dve.reciprocal(stat[:, 0, :], stat[:, 1, :]))
                scale = spread(stat[:, 0, :])
                for i in range(2 if len(dst.shape) == 4 else 1):
                    st.then(dve.tensor_tensor(dst[:, :, i, :] if len(dst.shape) == 4 else dst, cen, scale, ALU.mult))

            def layer_norm(k, src, dst, cen, sq):
                squares(src, cen, sq, slice(0, TILES))
                variances()
                normalise(k, dst, cen)

            def split_xT(k, seen, high, low):
                for c in range(6):
                    dve.wait_ge(tr_evac_a, seen + c + 1)
                    dve.tensor_tensor(low[:, 512 * c:512 * c + 512], ps[:, c, :], f32(high[:, 512 * c:512 * c + 512]),
                                      ALU.subtract).then_inc(tr_evac_v, 1)

            lo = slice(D, P)
            dve.wait_ge(split_high, 2)
            dve.tensor_tensor(W1s[lo, :, :], W1_raw[lo, :, :], f32(W1s[lo, :, :]), ALU.subtract).then_inc(split_low, 1)
            dve.tensor_tensor(fsplit[lo, :], fraw[lo, :], f32(fsplit[lo, :]), ALU.subtract).then_inc(split_low, 1)
            dve.wait_ge(ld_bias, 6 * 16)
            dve.wait_ge(ld_text, 3 * 16)
            hv = h[:, :, :].rearrange("p (q r) d -> p q r d", r=3)
            for c in range(2):
                dve.wait_ge(embed_ready, c + 1)
                for half in range(2):
                    s = slice(D * half, D * half + D)
                    st.then(dve.tensor_tensor(hv[s, 4 * c:4 * c + 4, half, :], ps[s, 2 + c, 0:256].rearrange("p (q d) -> p q d", d=D),
                                              tokb_sb[s, :].unsqueeze(1).to_broadcast([D, 4, D]), ALU.add))
                squares(h, cen0, sq0, slice(12 * c, 12 * c + 12))
            variances()
            dve.wait_ge(split_high, 4)
            for c in range(2):
                dve.scalar_tensor_tensor(out=Nh[lo, 4 * c:4 * c + 4, :].rearrange("p h c -> p (h c)"), in0=ps[lo, 4 + c, :],
                                         scalar=SCALE, in1=f32(Nh[lo, 4 * c:4 * c + 4, :].rearrange("p h c -> p (h c)")),
                                         op0=ALU.mult, op1=ALU.subtract).then_inc(split_low, 1)
            normalise(0, xn[:, :, :, :], cen0[:, :, :])
            dve.sem_inc(norm_ready, 1)
            dve.wait_ge(split_high, 5)
            dve.wait_ge(wt_evac, 3)
            dve.tensor_tensor(WvT[lo, :], ps[lo, 7, 256:384], f32(WvT[lo, :]), ALU.subtract).then_inc(split_low, 1)
            split_xT(0, 0, xTH, xTL)

            def q_halves(b, e):
                for i in range(PAIRS):
                    dve.wait_ge(q_high, b * 12 + (3 * i + 3))
                    for to, source in query_parts(Qs[e], i):
                        dve.tensor_tensor(to[lo], source[lo], f32(to[lo]), ALU.subtract).then_inc(qp_evac, 1)

            def maxima(b, e):
                wait(dve, exp_done, b * 12 - 12)
                for m in range(6):
                    dve.wait_ge(score_ready, b * 6 + m + 1)
                    dve.tensor_reduce(negmax[e][:, 2 * m:2 * m + 2],
                                      ps[:, 2 + m % 3, 0:2 * SEQ].rearrange("p (h s) -> p h s", h=2), axis=AXL.X,
                                      op=ALU.max, negate=True).then_inc(max_ready, 1)

            def evacuate_v(b, e):
                dve.wait_ge(v_ready, b + 1)
                wait(dve, mix_ready, b - 1)
                for dst, p0, c in ((Vlo[e][0:D, :, :], 0, 0), (Vlo[e][D:P, :, :], D, 1), (Vhi[e][:, :, :], 0, 2)):
                    dve.tensor_copy(dst, ps[p0:p0 + D, 5, D * c:D * c + D].unsqueeze(1).to_broadcast([D, 2, D])).then_inc(v_evac, 1)

            def scale_weights(b, e):
                dve.wait_ge(exp_done, b * 12 + 12)
                wait(dve, wos_ready, b)
                dve.reciprocal(rinv[:, :], rowsum[e][:, :]).then_inc(rinv_set, 1)
                dve.wait_ge(rinv_set, b + 1)
                wait(dve, gt_ready, b - 1)
                dve.tensor_tensor(WoS[e][:, :, :], WoT[:, :, :], rinv[:, :].unsqueeze(2).to_broadcast([P, 12, D]), ALU.mult)\
                   .then_inc(wos_ready, 1)

            def residual(b, q, e):
                dve.wait_ge(mix_ready, b + 1)
                own, other = slice(D * e, D * e + D), slice(D - D * e, P - D * e)
                o = ps[:, 7, 0:SEQ].rearrange("p (j d) -> p j d", j=3)
                a = h[own, bass.ds(q * 3 + e, 2), :]
                dve.tensor_tensor(a, a, o[own, 0:3:2, :], ALU.add).then_inc(mix_used, 1)
                a = h[other, bass.ds(q * 3 + 2 * e, 1), :]
                dve.tensor_tensor(a, a, o[other, 1:2, :], ALU.add).then_inc(mix_used, 1)

            def attention_step(s, e, q):
                if in_range(s - 1):
                    scale_weights(s - 1, 1 - e)
                if in_range(s + 1):
                    q_halves(s + 1, 1 - e)
                if in_range(s):
                    maxima(s, e)
                if in_range(s - 2):
                    residual(s - 2, q - 1, e)
                if in_range(s - 1):
                    evacuate_v(s - 1, 1 - e)

            q_halves(0, 0)
            attention_loop(dve, attention_step)
            dve.wait_ge(mix_used, 2 * IMAGES)

            layer_norm(1, h[:, :, :], xn[:, :, :, :], cen, sq)
            dve.sem_inc(norm_ready, 1)
            split_xT(1, 6, xTH, xTL)
            st.then(dve.memset(beats, 0.0))
            dve.wait_ge(gate_ready, 1)
            st.then(dve.tensor_tensor(gate[:, :, :], ps[:, 0, 0:TILES * 8].rearrange("p (t e) -> p t e", e=EXPERTS),
                                      bg_sb[:, :].unsqueeze(1).to_broadcast([P, TILES, EXPERTS]), ALU.add))
            for a in range(EXPERTS):
                if a:
                    dve.tensor_tensor(beats[:, :, a, 0:a], gate[:, :, 0:a],
                                      gate[:, :, a:a + 1].to_broadcast([P, TILES, a]), ALU.is_ge).then_inc(vec, 1)
                    st.n += 1
                if a < EXPERTS - 1:
                    dve.tensor_tensor(beats[:, :, a, a + 1:], gate[:, :, a + 1:],
                                      gate[:, :, a:a + 1].to_broadcast([P, TILES, EXPERTS - 1 - a]), ALU.is_gt).then_inc(vec, 1)
                    st.n += 1
            dve.wait_ge(vec, st.n)
            st.then(dve.tensor_reduce(mask[:, :, :], beats, axis=AXL.X, op=ALU.add))
            dve.tensor_scalar(mask[:, :, :], mask[:, :, :], 2.0, None, ALU.is_lt).then_inc(mask_ready, 1)
            dve.wait_ge(mask_ready, 1)
            dve.sem_inc(y_used, 1)

            def add_rows(ch):
                dve.wait_ge(y_ready, ch + 2)
                a = h[:, bass.ds(ch * 4, 4), :]
                dve.tensor_tensor(a, a, ps[:, 5, 0:4 * D].rearrange("p (i d) -> p i d", d=D), ALU.add).then_inc(y_used, 1)

            def mask_hidden(ch, before):
                for e in range(EXPERTS):
                    dve.wait_ge(spread_ready, ch * 8 + (e + 1))
                    dve.wait_ge(gelu_done, ch * 8 + (e + 1))
                    dve.tensor_tensor(hid[e % 4], hid[e % 4], ps[:, 2 + e % 2, :], ALU.mult).then_inc(masked, 1)
                    if e == 3 and before:
                        add_rows(ch - 1)

            mask_hidden(0, False)
            with dve.Fori(1, 6) as ch:
                mask_hidden(ch, True)
            add_rows(5)
            dve.wait_ge(y_used, 7)

            x1 = xn[:, :, 0, :]
            scratch = UU.rearrange("p t r -> p (t r)")
            cen2, sq2 = (scratch[:, 1536 * i:1536 * i + 1536].rearrange("p (t d) -> p t d", d=D) for i in range(2))
            layer_norm(2, h[:, :, :], x1_fast, cen2, sq2)
            layer_norm(3, x1_fast, o_tok, cen2, sq2)
            st.then(dve.tensor_tensor(o_tok, o_tok, g_sb[:, :].unsqueeze(1).to_broadcast([P, TILES, D]), ALU.mult))
            st.then(dve.tensor_tensor(o_tok, o_tok, b_sb[:, :].unsqueeze(1).to_broadcast([P, TILES, D]), ALU.add))
            dve.sem_inc(norm_ready, 1)
            st.then(dve.tensor_tensor(h[:, :, :], h[:, :, :], x1_fast, ALU.add))
            for c in range(1, 6, 2):
                dve.wait_ge(tr_ready, 12 + c + 1)
                dve.tensor_copy(xT[:, 512 * c:512 * c + 512], ps[0:D, c, :]).then_inc(tr_evac_v, 1)
            dve.wait_ge(tr_evac_v, 12 + 3)
            st.then(dve.memset(QE2[:, :, :], 1.0))

            def over_time(a, n):
                return a.unsqueeze(1).to_broadcast([P, n, a.shape[1]])

            def over_width(a):
                return a.unsqueeze(3).to_broadcast([P, a.shape[1], BOTH, DH])

            def keys_in(t):
                dve.wait_ge(raw_ready, 10 * t + 6)
                kt = KK[:, t, :].rearrange("p (u c d) -> p u c d", c=2, d=DH)
                rk, bt = kt[:, :, 1, :], beta[t % 2]
                st.count(dve.tensor_reduce(rk_top[:, :], rk, axis=AXL.X, op=ALU.max))
                dve.wait_ge(raw_ready, 10 * t + 10)
                st.then(dve.tensor_scalar(bt[:, :, :], bt[:, :, :], 1.0, None, ALU.add))
                dve.tensor_tensor(rk, rk, rk_top[:, :].unsqueeze(2).to_broadcast([P, UNITS, DH]), ALU.subtract).then_inc(rk_in, 1)
                dve.reciprocal(bt[:, :, :], bt[:, :, :]).then_inc(beta_ready, 1)
                st.count(dve.scalar_tensor_tensor(out=kt[:, :, 0, :], in0=exp_qk[:, :, DH:2 * DH], scalar=1.0,
                                                  in1=relu_qk[:, :, DH:2 * DH], op0=ALU.min, op1=ALU.add))

            def query(t):
                wait(dve, coef_prod, coefs_before(t - 1))
                dve.scalar_tensor_tensor(out=QE1[t % 2][:, :, :], in0=exp_qk[:, :, 0:DH], scalar=1.0,
                                         in1=relu_qk[:, :, 0:DH], op0=ALU.min, op1=ALU.add).then_inc(query_ready, 1)

            def keys(t):
                dve.wait_ge(rk_exp, t + 1)
                wait(dve, keys_ready, t)
                dve.wait_ge(query_ready, t + 1)
                dve.sem_inc(pre_used, 1)
                dve.wait_ge(vec, st.n)
                kt = KK[:, t, :].rearrange("p (r d) -> p r d", d=DH)
                st.then(dve.tensor_reduce(ksum[:, :], kt, axis=AXL.X, op=ALU.add))
                dve.reciprocal(ksum[:, :], ksum[:, :]).then_inc(ksum_ready, 1)

            def by_width(a):
                return a.rearrange("p t (r d) -> p t r d", d=DH)

            def gram_sums(t, c):
                m, n = grams_before(t) + c, min(3, t - 3 * c)
                dve.wait_ge(gram_prod, m + 1)
                dve.tensor_reduce(gram[:, 3 * c:3 * c + n, :], by_width(GRAM_ROWS[m % 2][:, 0:n, :]), axis=AXL.X, op=ALU.add)\
                   .then_inc(gram_used, 1)

            def scale_gram(t):
                dve.wait_ge(gram_used, grams_before(t + 1))
                n = 2 * old_chunks(t)
                if n:
                    wait(dve, old_prod, olds_before(t))
                    dve.scalar_tensor_tensor(out=gram_old[:, 0:n, :], in0=gram[:, 0:n, :], scalar=-1.0,
                                             in1=over_time(beta[t % 2][:, :, :].rearrange("p u c -> p (u c)"), n),
                                             op0=ALU.mult, op1=ALU.mult).then_inc(old_scaled, 1)
                gt = gram[:, n:t, :]
                st.then(dve.scalar_tensor_tensor(out=gt, in0=gt, scalar=-1.0,
                                                 in1=over_time(beta[t % 2][:, :, :].rearrange("p u c -> p (u c)"), t - n),
                                                 op0=ALU.mult, op1=ALU.mult))
                if old_chunks(t):
                    dve.wait_ge(old_scaled, olds_before(t + 1))

            def weigh_values(m, first, n, weights):
                wait(dve, summed, m - 2)
                dve.tensor_tensor(by_width(SUM_ROWS[m % 3][:, 0:n, :]), by_width(UU[:, first:first + n, :]),
                                  over_width(weights[:, first:first + n, :]), ALU.mult).then_inc(prod_ready, 1)

            def coef_sums(t, c):
                m, n = coefs_before(t) + c, min(4, t + 1 - 4 * c)
                dve.wait_ge(keys_ready, t + 1)
                dve.wait_ge(vec, st.n)
                k4 = KK[:, 4 * c:4 * c + n, :].rearrange("p t (u c d) -> p t c u d", c=2, d=DH)
                q4 = QE2[:, :, :].unsqueeze(1).to_broadcast([P, n, UNITS, DH])
                st.count(dve.tensor_tensor(COEF2_ROWS[:, 0:n, :].rearrange("p t (u d) -> p t u d", d=DH), k4[:, :, 1, :, :], q4, ALU.mult))
                c4 = coef[:, 4 * c:4 * c + n, :].rearrange("p t (u c) -> p t c u", c=2)
                dve.wait_ge(coef_prod, m + 1)
                dve.tensor_reduce(c4[:, :, 0, :], by_width(COEF1_ROWS[m % 2][:, 0:n, :]), axis=AXL.X, op=ALU.add)\
                   .then_inc(coef_used, 1)
                dve.wait_ge(vec, st.n)
                st.count(dve.tensor_reduce(c4[:, :, 1, :], by_width(COEF2_ROWS[:, 0:n, :]), axis=AXL.X, op=ALU.add))

            def soft(t):
                dve.wait_ge(hs_ready, t + 1)
                st.then(dve.tensor_reduce(top[:, :], hs[t % 2][:, :, :], axis=AXL.X, op=ALU.max))
                dve.tensor_tensor(QE2[:, :, :], hs[t % 2][:, :, :], top[:, :].unsqueeze(2).to_broadcast([P, UNITS, DH]),
                                  ALU.subtract).then_inc(soft_in, 1)

            def add_out(t):
                dve.wait_ge(mixo_ready, t + 1)
                q, e = t // 2, t % 2
                if e == 0:
                    parts = ((slice(0, P), 3 * q, 0), (slice(0, D), 3 * q + 1, D))
                else:
                    parts = ((slice(D, P), 3 * q + 1, 0), (slice(0, P), 3 * q + 2, D))
                for s, tile, c in parts:
                    dve.tensor_tensor(h[s, tile, :], h[s, tile, :], ps[s, OUT_BANK, 3 * P + c:3 * P + c + D], ALU.add)\
                       .then_inc(mixo_used, 1)

            keys_in(0)
            query(0)
            keys(0)
            def update_chunk(t, c):
                if c < update_chunks(t):
                    first = 2 * (c + old_chunks(t))
                    weigh_values(sums_before(t, False) + c, first, min(2, t - first), gram)

            for t in range(IMAGES):
                more = t + 1 < IMAGES
                update_chunk(t, 0)
                update_chunk(t, 1)
                if more:
                    keys_in(t + 1)
                if t:
                    soft(t - 1)
                if more:
                    query(t + 1)
                update_chunk(t, 2)
                if t:
                    dve.wait_ge(soft_exp, t)
                for memory, query_ in enumerate((QE1[t % 2], QE2)):
                    st.count(dve.tensor_reduce(qsum[:, memory:BOTH:2], query_[:, :, :], axis=AXL.X, op=ALU.add))
                queries_summed = st.n
                if more:
                    keys(t + 1)
                dve.wait_ge(vec, queries_summed)
                st.count(dve.reciprocal(qsum[:, :], qsum[:, :]))
                for c in range((t + 4) // 4):
                    update_chunk(t, c + 3)
                    coef_sums(t, c)
                dve.wait_ge(vec, st.n)
                dve.wait_ge(coef_used, coefs_before(t + 1))
                old = 2 * old_chunks(t)
                if old:
                    wait(dve, old_read, olds_before(t))
                    dve.tensor_tensor(coef_old[:, 0:old, :], coef[:, 0:old, :], over_time(qsum[:, :], old), ALU.mult)\
                       .then_inc(old_coef, 1)
                ct = coef[:, old:t + 1, :]
                st.then(dve.tensor_tensor(ct, ct, over_time(qsum[:, :], t + 1 - old), ALU.mult))
                if old:
                    dve.wait_ge(old_coef, olds_before(t + 1))
                for c in range(reading_chunks(t)):
                    if 2 * c + old + 2 > t:
                        wait(dve, u_evac, t)
                        wait(dve, values_ready, t + 1)
                    weigh_values(sums_before(t, True) + c, 2 * c + old, min(2, t + 1 - 2 * c - old), coef)
                    if more and c < gram_chunks(t + 1):
                        gram_sums(t + 1, c)
                if more:
                    for c in range(reading_chunks(t), gram_chunks(t + 1)):
                        gram_sums(t + 1, c)
                    scale_gram(t + 1)
                if t:
                    add_out(t - 1)
            add_out(IMAGES - 1)
            dve.wait_ge(mixo_used, 2 * IMAGES)

            layer_norm(4, h[:, :, :], xn[:, :, :, :], cen3, sq3)
            dve.sem_inc(norm_ready, 1)
            st.then(dve.tensor_tensor(h[:, :, :], h[:, :, :], x1, ALU.add))
            split_xT(3, 15, xTH3, xTL3)
            for c in range(6):
                dve.wait_ge(wcol_ready, c + 1)
                dve.tensor_scalar(wcols[:, 512 * c:512 * c + 512], ps[:, c, :], br_sb[:, 0:1], None, ALU.add).then_inc(rank_vec, 1)
            dve.wait_ge(rank_vec, 6)
            dve.wait_ge(masks_set, 5)
            st.then(dve.tensor_tensor(wdiag, wcols.rearrange("p (t j) -> p t j", j=P),
                                      ident[:, :].unsqueeze(1).to_broadcast([P, TILES, P]), ALU.mult))
            st.then(dve.tensor_reduce(wtok[:, :], wdiag, axis=AXL.X, op=ALU.add))
            with dve.Fori(0, IMAGES // 2) as q:
                parts = ((slice(0, P), 0, 0, 0), (slice(0, D), 1, 0, 1), (slice(D, P), 1, 1, 1), (slice(0, P), 2, 1, 2))
                for i, (s, r, e, k) in enumerate(parts):
                    cols = wcols[s, bass.ds(q * 384 + SEQ * e, SEQ)]
                    own = wtok[s, bass.ds(q * 3 + r, 1)]
                    dve.scalar_tensor_tensor(out=tie[s, i, :], in0=cols, scalar=own, in1=earlier[s, k, :],
                                             op0=ALU.is_equal, op1=ALU.mult).then_inc(rank_vec, 1)
                dve.wait_ge(rank_vec, q * 8 + 10)
                for i, (s, r, e, k) in enumerate(parts):
                    cols = wcols[s, bass.ds(q * 384 + SEQ * e, SEQ)]
                    own = wtok[s, bass.ds(q * 3 + r, 1)]
                    dve.scalar_tensor_tensor(out=over[s, i, :], in0=cols, scalar=own, in1=tie[s, i, :],
                                             op0=ALU.is_gt, op1=ALU.add, accum_out=rank[s, bass.ds(q * 3 + r, 1)])\
                       .then_inc(rank_vec, 1)
                dve.wait_ge(rank_vec, q * 8 + 14)
            st.then(dve.scalar_tensor_tensor(out=wkeep[:, :], in0=rank[:, :], scalar=float(KEPT), in1=wtok[:, :],
                                             op0=ALU.is_lt, op1=ALU.mult))
            dve.wait_ge(fy_biased, 1)
            for c in range(3):
                t8 = slice(8 * c, 8 * c + 8)
                st.then(dve.tensor_tensor(fy[:, t8, :], fy[:, t8, :], wkeep[:, t8].unsqueeze(2).to_broadcast([P, 8, D]), ALU.mult))
                dve.tensor_tensor(h[:, t8, :], h[:, t8, :], fy[:, t8, :], ALU.add).then_inc(out_ready, 1)


_INS = ['x', 'txt', 'L0_tok_W', 'L0_tok_b', 'L0_attn_Wq', 'L0_attn_Wk', 'L0_attn_Wv', 'L0_attn_Wo', 'L0_ffn_Wg',
        'L0_ffn_bg', 'L0_ffn_W1', 'L0_ffn_b1', 'L0_ffn_W2', 'L0_ffn_b2', 'L1_attn_slow_W', 'L1_attn_out_W',
        'L1_attn_ln_g', 'L1_attn_ln_b', 'L1_ffn_wr', 'L1_ffn_br', 'L1_ffn_w1', 'L1_ffn_b1', 'L1_ffn_w2', 'L1_ffn_b2']


def kernel(**inputs):
    import numpy as _np
    import concourse.bacc as _bacc
    from concourse import mybir as _mybir
    from concourse.bass_utils import run_bass_kernel_spmd as _run

    nc = _bacc.Bacc("TRN2", target_bir_lowering=False, num_devices=1)
    arrays, args = {}, []
    for name in _INS:
        a = _np.ascontiguousarray(inputs[name])
        arrays[f"in_{name}_dram"] = a
        args.append(nc.dram_tensor(f"in_{name}_dram", a.shape, _mybir.dt.from_np(a.dtype), kind="ExternalInput").ap())
    result = nc.dram_tensor("out_0_dram", (IMAGES, SEQ, D), F32, kind="ExternalOutput").ap()
    token_mixer_kernel(nc, *args, result)
    r = _run(nc, [arrays], core_ids=[0])
    return r.results[0]["out_0_dram"]
```
